# Optimizing a Trainium2 kernel written in Bass

```python
import numpy as np
import jax
import jax.numpy as jnp

def _softmax(x, axis=-1):
    return jax.nn.softmax(x, axis=axis)

def _gelu(x):
    return jax.nn.gelu(x, approximate=True)

def _silu(x):
    return jax.nn.silu(x)

def _sigmoid(x):
    return jax.nn.sigmoid(x)

def _layernorm(x, axis=-1, eps=1e-05):
    m = jnp.mean(x, axis=axis, keepdims=True)
    v = jnp.var(x, axis=axis, keepdims=True)
    return (x - m) / jnp.sqrt(v + eps)

def _scatter_add(tgt, idx, src, axis=0):
    return tgt.at[idx].add(src)

def _segment_sum(src, seg, n):
    return jax.ops.segment_sum(src, seg, n)
kernel_name = 'mk_early_fusion_d4_tok_img1024_r4_55c6be'

def setup_inputs(seed: int=0):
    np.random.seed(seed)
    _w = jnp.asarray

    def _rec_inputs():
        import jax
        import jax.numpy as jnp
        _rk = jax.random.key(seed)
        x = -0.00016672 + 0.999947 * jax.random.normal(jax.random.fold_in(_rk, 1), (32, 3, 96, 96), jnp.float32)
        txt = -0.000341708 + 0.57781 * jax.random.normal(jax.random.fold_in(_rk, 2), (32, 32, 256), jnp.float32)
        return (x, txt)
    x, txt = _rec_inputs()

    def _L0_tok_setup():
        import jax, jax.numpy as jnp
        import numpy as np
        IMG = 96
        P = 16
        C = 3
        D = 256
        B = 64
        key = jax.random.key(seed)
        kx, kw, kb = jax.random.split(key, 3)
        fan_in = C * P * P
        bound = 1.0 / np.sqrt(fan_in)
        x = jax.random.normal(kx, (B, C, IMG, IMG), dtype=jnp.float32)
        W = jax.random.uniform(kw, (D, fan_in), dtype=jnp.float32, minval=-bound, maxval=bound)
        b = jax.random.uniform(kb, (D,), dtype=jnp.float32, minval=-bound, maxval=bound)
        return {'x': x, 'W': W, 'b': b}
    _L0_tok_all = _L0_tok_setup()
    _L0_tok_in = {k: v for k, v in _L0_tok_all.items() if k in ('W', 'b')}
    del _L0_tok_all

    def _L0_attn_setup():
        import jax, jax.numpy as jnp
        import numpy as np
        import math
        E, N, K, R = (256, 16, 4, 64)
        B, L = (2, 512)
        key = jax.random.key(seed)
        ks = jax.random.split(key, 8)
        gn = lambda k, sh, sc: jax.random.normal(k, sh, dtype=jnp.float32) * sc
        W_z = gn(ks[0], (E, E), E ** (-0.5))
        W_params = gn(ks[1], (R + 2 * N, E), E ** (-0.5))
        conv_w = gn(ks[2], (E, 1, K), 0.5)
        dt_std = R ** (-0.5) * 0.1
        W_dt = jax.random.uniform(ks[3], (E, R), jnp.float32, -dt_std, dt_std)
        b_dt = jnp.full((E,), math.log(math.expm1(0.001)), dtype=jnp.float32)
        A_log = jnp.tile(jnp.log(jnp.arange(1, N + 1, dtype=jnp.float32))[None, :], (E, 1))
        D = jnp.ones((E,), dtype=jnp.float32)
        W_out = gn(ks[4], (E, E), E ** (-0.5))
        x = jax.random.normal(ks[5], (B, L, E), dtype=jnp.float32)
        return dict(x=x, W_z=W_z, W_params=W_params, conv_w=conv_w, W_dt=W_dt, b_dt=b_dt, A_log=A_log, D=D, W_out=W_out)
    _L0_attn_all = _L0_attn_setup()
    _L0_attn_in = {k: v for k, v in _L0_attn_all.items() if k in ('W_z', 'W_params', 'conv_w', 'W_dt', 'b_dt', 'A_log', 'D', 'W_out')}
    del _L0_attn_all

    def _L0_ffn_setup():
        import jax, jax.numpy as jnp
        import numpy as np
        B, T, D = (1, 256, 256)
        E, S, H = (8, 2, 1024)
        key = jax.random.key(seed)
        kx, kg, k1, k2, k3 = jax.random.split(key, 5)
        X = jax.random.normal(kx, (B, T, D), jnp.float32)
        Wg = jax.random.normal(kg, (D, E), jnp.float32) * 0.02
        bg = jnp.zeros((E,), jnp.float32)
        W1 = jax.random.normal(k1, (E, D, H), jnp.float32) * 0.02
        W3 = jax.random.normal(k3, (E, D, H), jnp.float32) * 0.02
        W2 = jax.random.normal(k2, (E, H, D), jnp.float32) * 0.02
        return {'X': X, 'Wg': Wg, 'bg': bg, 'W1': W1, 'W2': W2, 'W3': W3}
    _L0_ffn_all = _L0_ffn_setup()
    _L0_ffn_in = {k: v for k, v in _L0_ffn_all.items() if k in ('Wg', 'bg', 'W1', 'W2', 'W3')}
    del _L0_ffn_all

    def _L1_attn_setup():
        import jax, jax.numpy as jnp
        import numpy as np
        EPS = 1e-06

        def _rmsnorm(x, w):
            return x * jax.lax.rsqrt(jnp.mean(x * x, axis=-1, keepdims=True) + EPS) * w

        def _causal_dwconv(u, conv_w, conv_b):
            K = conv_w.shape[0]
            T = u.shape[1]
            up = jnp.pad(u, ((0, 0), (K - 1, 0), (0, 0)))
            y = conv_b
            for k in range(K):
                y = y + up[:, k:k + T, :] * conv_w[k]
            return y
        key = jax.random.key(seed)
        ks = jax.random.split(key, 6)
        B, T, D, K = (4, 1024, 256, 4)
        s = 0.02
        return {'x': jax.random.normal(ks[0], (B, T, D), dtype=jnp.float32), 'norm_w': jnp.ones((D,), jnp.float32), 'in_w': jax.random.normal(ks[1], (D, 2 * D), dtype=jnp.float32) * s, 'in_b': jnp.zeros((2 * D,), jnp.float32), 'conv_w': jax.random.normal(ks[2], (K, D), dtype=jnp.float32) * s, 'conv_b': jnp.zeros((D,), jnp.float32), 'param_w': jax.random.normal(ks[3], (D, 3 * D), dtype=jnp.float32) * s, 'param_b': jnp.zeros((3 * D,), jnp.float32), 'skip': jnp.ones((D,), jnp.float32), 'out_w': jax.random.normal(ks[4], (D, D), dtype=jnp.float32) * s, 'out_b': jnp.zeros((D,), jnp.float32)}
    _L1_attn_all = _L1_attn_setup()
    _L1_attn_in = {k: v for k, v in _L1_attn_all.items() if k in ('norm_w', 'in_w', 'in_b', 'conv_w', 'conv_b', 'param_w', 'param_b', 'skip', 'out_w', 'out_b')}
    del _L1_attn_all

    def _L1_ffn_setup():
        import jax, jax.numpy as jnp
        import numpy as np
        TOP_K = 32
        TEMPERATURE = 1.0
        PARAM_SCALE = 0.02

        def _compose_weight(logits, A, B):
            vals, idx = jax.lax.top_k(logits, TOP_K)
            w = jax.nn.softmax(vals / TEMPERATURE)
            A_sel = A[idx]
            B_sel = B[idx]
            return jnp.einsum('k,kir,kro->io', w, A_sel, B_sel)
        key = jax.random.key(seed)
        ks = jax.random.split(key, 7)
        B, S, D, F, P, R = (2, 256, 256, 1024, 64, 64)
        x = jax.random.normal(ks[0], (B, S, D), dtype=jnp.float32)
        fc1_A = jax.random.normal(ks[1], (P, D, R), dtype=jnp.float32) * PARAM_SCALE
        fc1_B = jax.random.normal(ks[2], (P, R, F), dtype=jnp.float32) * PARAM_SCALE
        fc2_A = jax.random.normal(ks[3], (P, F, R), dtype=jnp.float32) * PARAM_SCALE
        fc2_B = jax.random.normal(ks[4], (P, R, D), dtype=jnp.float32) * PARAM_SCALE
        fc1_logits = jax.random.normal(ks[5], (P,), dtype=jnp.float32)
        fc2_logits = jax.random.normal(ks[6], (P,), dtype=jnp.float32)
        return {'x': x, 'fc1_A': fc1_A, 'fc1_B': fc1_B, 'fc2_A': fc2_A, 'fc2_B': fc2_B, 'fc1_logits': fc1_logits, 'fc2_logits': fc2_logits}
    _L1_ffn_all = _L1_ffn_setup()
    _L1_ffn_in = {k: v for k, v in _L1_ffn_all.items() if k in ('fc1_A', 'fc1_B', 'fc2_A', 'fc2_B', 'fc1_logits', 'fc2_logits')}
    del _L1_ffn_all

    def _L2_attn_setup():
        import jax, jax.numpy as jnp
        import numpy as np
        SEQ_LEN = 512
        DIM_EMB = 256
        DIM_K = 256
        DIM_V = 256
        BATCH = 4
        key = jax.random.key(seed)
        kx, kq, kk, kv, ko = jax.random.split(key, 5)
        s = DIM_EMB ** (-0.5)
        return {'x': jax.random.normal(kx, (BATCH, SEQ_LEN, DIM_EMB), dtype=jnp.float32), 'Wq': jax.random.normal(kq, (DIM_EMB, DIM_K), dtype=jnp.float32) * s, 'Wk': jax.random.normal(kk, (DIM_EMB, DIM_K), dtype=jnp.float32) * s, 'Wv': jax.random.normal(kv, (DIM_EMB, DIM_V), dtype=jnp.float32) * s, 'Wo': jax.random.normal(ko, (DIM_V, DIM_V), dtype=jnp.float32) * DIM_V ** (-0.5)}
    _L2_attn_all = _L2_attn_setup()
    _L2_attn_in = {k: v for k, v in _L2_attn_all.items() if k in ('Wq', 'Wk', 'Wv', 'Wo')}
    del _L2_attn_all

    def _L2_ffn_setup():
        import jax, jax.numpy as jnp
        import numpy as np
        IN_DIM = 256
        OUT_DIM = 256
        NUM_EXPERTS = 8
        TOP_K = 2
        key = jax.random.key(seed)
        ks = jax.random.split(key, 5)
        s = 1.0 / np.sqrt(IN_DIM)
        x = jax.random.normal(ks[0], (4, 512, IN_DIM), dtype=jnp.float32)
        Wg = jax.random.uniform(ks[1], (IN_DIM, NUM_EXPERTS), jnp.float32, -s, s)
        bg = jnp.zeros((NUM_EXPERTS,), jnp.float32)
        We = jax.random.uniform(ks[2], (NUM_EXPERTS, OUT_DIM, IN_DIM), jnp.float32, -s, s)
        be = jax.random.uniform(ks[3], (NUM_EXPERTS, OUT_DIM), jnp.float32, -s, s)
        return {'x': x, 'Wg': Wg, 'bg': bg, 'We': We, 'be': be}
    _L2_ffn_all = _L2_ffn_setup()
    _L2_ffn_in = {k: v for k, v in _L2_ffn_all.items() if k in ('Wg', 'bg', 'We', 'be')}
    del _L2_ffn_all

    def _L3_attn_setup():
        import jax, jax.numpy as jnp
        import numpy as np
        EMBED = 256
        WIN = 128
        NUM_HEADS = 16
        HQ = 16
        HKV = 4
        HEAD_DIM = EMBED // NUM_HEADS
        G = HQ // HKV
        key = jax.random.key(seed)
        k = jax.random.split(key, 5)
        B, S = (1, 512)
        x = jax.random.normal(k[0], (B, S, EMBED), dtype=jnp.float32)
        Wq = jax.random.normal(k[1], (HQ * HEAD_DIM, EMBED), dtype=jnp.float32) * 0.02
        Wk = jax.random.normal(k[2], (HKV * HEAD_DIM, EMBED), dtype=jnp.float32) * 0.02
        Wv = jax.random.normal(k[3], (HKV * HEAD_DIM, EMBED), dtype=jnp.float32) * 0.02
        Wo = jax.random.normal(k[4], (EMBED, HQ * HEAD_DIM), dtype=jnp.float32) * 0.02
        return {'x': x, 'Wq': Wq, 'Wk': Wk, 'Wv': Wv, 'Wo': Wo}
    _L3_attn_all = _L3_attn_setup()
    _L3_attn_in = {k: v for k, v in _L3_attn_all.items() if k in ('Wq', 'Wk', 'Wv', 'Wo')}
    del _L3_attn_all

    def _L3_ffn_setup():
        import jax, jax.numpy as jnp
        import numpy as np
        B, S, D, T = (4, 1024, 256, 8)
        key = jax.random.key(seed)
        k1, k2, k3, k4 = jax.random.split(key, 4)
        x = jax.random.normal(k1, (B, S, D), dtype=jnp.float32)
        tile_sigs = jax.random.normal(k2, (T, D), dtype=jnp.float32)
        bound = 1.0 / np.sqrt(D)
        W = jax.random.uniform(k3, (T, D, D), minval=-bound, maxval=bound, dtype=jnp.float32)
        b = jax.random.uniform(k4, (T, D), minval=-bound, maxval=bound, dtype=jnp.float32)
        return {'x': x, 'tile_sigs': tile_sigs, 'W': W, 'b': b}
    _L3_ffn_all = _L3_ffn_setup()
    _L3_ffn_in = {k: v for k, v in _L3_ffn_all.items() if k in ('tile_sigs', 'W', 'b')}
    del _L3_ffn_all
    return {'x': x, 'txt': txt, 'L0_tok_W': _L0_tok_in['W'], 'L0_tok_b': _L0_tok_in['b'], 'L0_attn_W_z': _L0_attn_in['W_z'], 'L0_attn_W_params': _L0_attn_in['W_params'], 'L0_attn_conv_w': _L0_attn_in['conv_w'], 'L0_attn_W_dt': _L0_attn_in['W_dt'], 'L0_attn_b_dt': _L0_attn_in['b_dt'], 'L0_attn_A_log': _L0_attn_in['A_log'], 'L0_attn_D': _L0_attn_in['D'], 'L0_attn_W_out': _L0_attn_in['W_out'], 'L0_ffn_Wg': _L0_ffn_in['Wg'], 'L0_ffn_bg': _L0_ffn_in['bg'], 'L0_ffn_W1': _L0_ffn_in['W1'], 'L0_ffn_W2': _L0_ffn_in['W2'], 'L0_ffn_W3': _L0_ffn_in['W3'], 'L1_attn_norm_w': _L1_attn_in['norm_w'], 'L1_attn_in_w': _L1_attn_in['in_w'], 'L1_attn_in_b': _L1_attn_in['in_b'], 'L1_attn_conv_w': _L1_attn_in['conv_w'], 'L1_attn_conv_b': _L1_attn_in['conv_b'], 'L1_attn_param_w': _L1_attn_in['param_w'], 'L1_attn_param_b': _L1_attn_in['param_b'], 'L1_attn_skip': _L1_attn_in['skip'], 'L1_attn_out_w': _L1_attn_in['out_w'], 'L1_attn_out_b': _L1_attn_in['out_b'], 'L1_ffn_fc1_A': _L1_ffn_in['fc1_A'], 'L1_ffn_fc1_B': _L1_ffn_in['fc1_B'], 'L1_ffn_fc2_A': _L1_ffn_in['fc2_A'], 'L1_ffn_fc2_B': _L1_ffn_in['fc2_B'], 'L1_ffn_fc1_logits': _L1_ffn_in['fc1_logits'], 'L1_ffn_fc2_logits': _L1_ffn_in['fc2_logits'], 'L2_attn_Wq': _L2_attn_in['Wq'], 'L2_attn_Wk': _L2_attn_in['Wk'], 'L2_attn_Wv': _L2_attn_in['Wv'], 'L2_attn_Wo': _L2_attn_in['Wo'], 'L2_ffn_Wg': _L2_ffn_in['Wg'], 'L2_ffn_bg': _L2_ffn_in['bg'], 'L2_ffn_We': _L2_ffn_in['We'], 'L2_ffn_be': _L2_ffn_in['be'], 'L3_attn_Wq': _L3_attn_in['Wq'], 'L3_attn_Wk': _L3_attn_in['Wk'], 'L3_attn_Wv': _L3_attn_in['Wv'], 'L3_attn_Wo': _L3_attn_in['Wo'], 'L3_ffn_tile_sigs': _L3_ffn_in['tile_sigs'], 'L3_ffn_W': _L3_ffn_in['W'], 'L3_ffn_b': _L3_ffn_in['b']}

def reference(x, txt, L0_tok_W, L0_tok_b, L0_attn_W_z, L0_attn_W_params, L0_attn_conv_w, L0_attn_W_dt, L0_attn_b_dt, L0_attn_A_log, L0_attn_D, L0_attn_W_out, L0_ffn_Wg, L0_ffn_bg, L0_ffn_W1, L0_ffn_W2, L0_ffn_W3, L1_attn_norm_w, L1_attn_in_w, L1_attn_in_b, L1_attn_conv_w, L1_attn_conv_b, L1_attn_param_w, L1_attn_param_b, L1_attn_skip, L1_attn_out_w, L1_attn_out_b, L1_ffn_fc1_A, L1_ffn_fc1_B, L1_ffn_fc2_A, L1_ffn_fc2_B, L1_ffn_fc1_logits, L1_ffn_fc2_logits, L2_attn_Wq, L2_attn_Wk, L2_attn_Wv, L2_attn_Wo, L2_ffn_Wg, L2_ffn_bg, L2_ffn_We, L2_ffn_be, L3_attn_Wq, L3_attn_Wk, L3_attn_Wv, L3_attn_Wo, L3_ffn_tile_sigs, L3_ffn_W, L3_ffn_b):
    import jax
    import jax.numpy as jnp

    def _L0_tok_ref(x, W, b):
        import jax, jax.numpy as jnp
        import numpy as np
        IMG = 96
        P = 16
        C = 3
        D = 256
        B = 64
        Bsz, Cc, H, Wd = x.shape
        gh, gw = (H // P, Wd // P)
        patches = x.reshape(Bsz, Cc, gh, P, gw, P).transpose(0, 2, 4, 1, 3, 5)
        patches = patches.reshape(Bsz, gh * gw, Cc * P * P)
        return jnp.einsum('bnf,df->bnd', patches, W) + b

    def _L0_attn_ref(x, W_z, W_params, conv_w, W_dt, b_dt, A_log, D, W_out):
        import jax, jax.numpy as jnp
        import numpy as np
        import math
        E, N, K, R = (256, 16, 4, 64)
        B, L = (2, 512)
        b, l, e = x.shape
        n = A_log.shape[1]
        r = W_dt.shape[1]
        k = conv_w.shape[-1]
        z = x @ W_z.T
        params = x @ W_params.T
        dt_unproj = params[..., :r]
        C_proj = params[..., r + n:]
        dt = jax.nn.softplus(dt_unproj @ W_dt.T + b_dt)
        xc = jax.lax.conv_general_dilated(x.transpose(0, 2, 1), conv_w, (1,), [(k - 1, 0)], dimension_numbers=('NCH', 'OIH', 'NCH'), feature_group_count=e)
        u = jax.nn.silu(xc.transpose(0, 2, 1))
        A = -jnp.exp(A_log)
        A_tilde = jnp.exp(dt[..., None] * A[None, None])
        B_tilde = jnp.where(jnp.abs(A)[None, None] < 1e-05, dt[..., None], (A_tilde - 1.0) / (A[None, None] + 1e-10))
        h0 = B_tilde[:, 0] * u[:, 0, :, None]

        def step(h, inp):
            a, bt, uu = inp
            h_new = a * h + bt * uu[..., None]
            return (h_new, h_new)
        xs = (A_tilde[:, :-1].transpose(1, 0, 2, 3), B_tilde[:, :-1].transpose(1, 0, 2, 3), u[:, :-1].transpose(1, 0, 2))
        _, hs = jax.lax.scan(step, h0, xs)
        h = jnp.concatenate([h0[None], hs], axis=0).transpose(1, 0, 2, 3)
        y = jnp.einsum('bln,blen->ble', C_proj, h)
        y_ssm = y + u * D
        y_gated = y_ssm * jax.nn.silu(z)
        return y_gated @ W_out.T

    def _L0_ffn_ref(X, Wg, bg, W1, W2, W3):
        import jax, jax.numpy as jnp
        import numpy as np
        B, T, D = (1, 256, 256)
        E, S, H = (8, 2, 1024)
        logits = jnp.einsum('btd,de->bte', X, Wg) + bg
        topv, topi = jax.lax.top_k(logits, S)
        w = jax.nn.softmax(topv, axis=-1)
        xs = X[:, :, None, :] * w[..., None]
        out = X
        for e in range(E):
            h = jax.nn.silu(jnp.einsum('btsd,dh->btsh', xs, W1[e])) * jnp.einsum('btsd,dh->btsh', xs, W3[e])
            y = jnp.einsum('btsh,hd->btsd', h, W2[e])
            mask = (topi == e)[..., None]
            out = out + jnp.where(mask, y, 0.0).sum(axis=2)
        return out

    def _L1_attn_ref(x, norm_w, in_w, in_b, conv_w, conv_b, param_w, param_b, skip, out_w, out_b):
        import jax, jax.numpy as jnp
        import numpy as np
        EPS = 1e-06

        def _rmsnorm(x, w):
            return x * jax.lax.rsqrt(jnp.mean(x * x, axis=-1, keepdims=True) + EPS) * w

        def _causal_dwconv(u, conv_w, conv_b):
            K = conv_w.shape[0]
            T = u.shape[1]
            up = jnp.pad(u, ((0, 0), (K - 1, 0), (0, 0)))
            y = conv_b
            for k in range(K):
                y = y + up[:, k:k + T, :] * conv_w[k]
            return y
        residual = x
        xn = _rmsnorm(x, norm_w)
        proj = jnp.einsum('btd,de->bte', xn, in_w) + in_b
        D = x.shape[-1]
        u, gate = (proj[..., :D], proj[..., D:])
        u = jax.nn.silu(_causal_dwconv(u, conv_w, conv_b))
        params = jnp.einsum('btd,de->bte', u, param_w) + param_b
        a = jax.nn.sigmoid(params[..., :D])
        b = jnp.tanh(params[..., D:2 * D])
        c = jax.nn.sigmoid(params[..., 2 * D:])
        abu = (jnp.swapaxes(a, 0, 1), jnp.swapaxes(b, 0, 1), jnp.swapaxes(u, 0, 1))
        state0 = jnp.zeros_like(u[:, 0])

        def step(state, inp):
            a_t, b_t, u_t = inp
            state = a_t * state + b_t * u_t
            return (state, state)
        _, states = jax.lax.scan(step, state0, abu)
        states = jnp.swapaxes(states, 0, 1)
        y = c * states + skip * u
        y = y * jax.nn.silu(gate)
        y = jnp.einsum('btd,de->bte', y, out_w) + out_b
        return residual + y

    def _L1_ffn_ref(x, fc1_A, fc1_B, fc2_A, fc2_B, fc1_logits, fc2_logits):
        import jax, jax.numpy as jnp
        import numpy as np
        TOP_K = 32
        TEMPERATURE = 1.0
        PARAM_SCALE = 0.02

        def _compose_weight(logits, A, B):
            vals, idx = jax.lax.top_k(logits, TOP_K)
            w = jax.nn.softmax(vals / TEMPERATURE)
            A_sel = A[idx]
            B_sel = B[idx]
            return jnp.einsum('k,kir,kro->io', w, A_sel, B_sel)
        W1 = _compose_weight(fc1_logits, fc1_A, fc1_B)
        W2 = _compose_weight(fc2_logits, fc2_A, fc2_B)
        h = jax.nn.gelu(jnp.einsum('bsd,df->bsf', x, W1))
        return jnp.einsum('bsf,fd->bsd', h, W2)

    def _L2_attn_ref(x, Wq, Wk, Wv, Wo):
        import jax, jax.numpy as jnp
        import numpy as np
        SEQ_LEN = 512
        DIM_EMB = 256
        DIM_K = 256
        DIM_V = 256
        BATCH = 4
        q = jnp.einsum('bse,ek->bsk', x, Wq)
        k = jnp.einsum('bse,ek->bsk', x, Wk)
        v = jnp.einsum('bse,ev->bsv', x, Wv)
        scores = jnp.einsum('bqk,bsk->bqs', q, k)
        S = scores.shape[-1]
        causal_mask = jnp.triu(jnp.ones((S, S), dtype=bool), k=1)
        scores = jnp.where(causal_mask[None], -jnp.inf, scores)
        attn = jax.nn.softmax(scores * Wq.shape[1] ** (-0.5), axis=-1)
        out = jnp.einsum('bqs,bsv->bqv', attn, v)
        return jnp.einsum('bqv,vo->bqo', out, Wo)

    def _L2_ffn_ref(x, Wg, bg, We, be):
        import jax, jax.numpy as jnp
        import numpy as np
        IN_DIM = 256
        OUT_DIM = 256
        NUM_EXPERTS = 8
        TOP_K = 2
        gate = jax.nn.softmax(x @ Wg + bg, axis=-1)
        topk_vals, topk_idx = jax.lax.top_k(gate, TOP_K)
        onehot = jax.nn.one_hot(topk_idx, NUM_EXPERTS, dtype=gate.dtype)
        gate_sparse = jnp.einsum('bsk,bske->bse', topk_vals, onehot)
        gate_sparse = gate_sparse / jnp.sum(gate_sparse, axis=-1, keepdims=True)
        y = jnp.einsum('bsi,eoi->bseo', x, We) + be[None, None, :, :].transpose(0, 1, 2, 3)
        out = jnp.einsum('bseo,bse->bso', y, gate_sparse)
        return out

    def _L3_attn_ref(x, Wq, Wk, Wv, Wo):
        import jax, jax.numpy as jnp
        import numpy as np
        EMBED = 256
        WIN = 128
        NUM_HEADS = 16
        HQ = 16
        HKV = 4
        HEAD_DIM = EMBED // NUM_HEADS
        G = HQ // HKV
        B, S, _ = x.shape
        W = 2 * WIN + 1
        scale = 1.0 / np.sqrt(HEAD_DIM).astype(np.float32)
        Q = (x @ Wq.T).reshape(B, S, HKV, G, HEAD_DIM)
        K = (x @ Wk.T).reshape(B, S, HKV, HEAD_DIM)
        V = (x @ Wv.T).reshape(B, S, HKV, HEAD_DIM)
        offs = jnp.arange(W) - WIN
        idx = jnp.arange(S)[:, None] + offs[None, :]
        valid = (idx >= 0) & (idx < S)
        idxc = jnp.clip(idx, 0, S - 1)
        K_win = K[:, idxc]
        V_win = V[:, idxc]
        scores = jnp.einsum('bskgd,bswkd->bskgw', Q, K_win) * scale
        scores = jnp.where(valid[None, :, None, None, :], scores, jnp.float32(-jnp.inf))
        attn = jax.nn.softmax(scores, axis=-1)
        out = jnp.einsum('bskgw,bswkd->bskgd', attn, V_win)
        out = out.reshape(B, S, HQ * HEAD_DIM)
        return out @ Wo.T

    def _L3_ffn_ref(x, tile_sigs, W, b):
        import jax, jax.numpy as jnp
        import numpy as np
        B, S, D, T = (4, 1024, 256, 8)
        scores = jnp.einsum('bsd,td->bst', x, jnp.sign(tile_sigs))
        idx = jnp.argmax(scores, axis=-1)
        all_out = jnp.einsum('bsd,tde->bste', x, W) + b[None, None]
        out = jnp.take_along_axis(all_out, idx[:, :, None, None], axis=2)
        return out[:, :, 0, :]
    h = _L0_tok_ref(x, L0_tok_W, L0_tok_b)
    h = jnp.concatenate([h, txt], axis=1)
    h = h + _L0_attn_ref(_layernorm(h, axis=-1), L0_attn_W_z, L0_attn_W_params, L0_attn_conv_w, L0_attn_W_dt, L0_attn_b_dt, L0_attn_A_log, L0_attn_D, L0_attn_W_out)
    h = h + _L0_ffn_ref(_layernorm(h, axis=-1), L0_ffn_Wg, L0_ffn_bg, L0_ffn_W1, L0_ffn_W2, L0_ffn_W3)
    h = h + _L1_attn_ref(_layernorm(h, axis=-1), L1_attn_norm_w, L1_attn_in_w, L1_attn_in_b, L1_attn_conv_w, L1_attn_conv_b, L1_attn_param_w, L1_attn_param_b, L1_attn_skip, L1_attn_out_w, L1_attn_out_b)
    h = h + _L1_ffn_ref(_layernorm(h, axis=-1), L1_ffn_fc1_A, L1_ffn_fc1_B, L1_ffn_fc2_A, L1_ffn_fc2_B, L1_ffn_fc1_logits, L1_ffn_fc2_logits)
    h = h + _L2_attn_ref(_layernorm(h, axis=-1), L2_attn_Wq, L2_attn_Wk, L2_attn_Wv, L2_attn_Wo)
    h = h + _L2_ffn_ref(_layernorm(h, axis=-1), L2_ffn_Wg, L2_ffn_bg, L2_ffn_We, L2_ffn_be)
    h = h + _L3_attn_ref(_layernorm(h, axis=-1), L3_attn_Wq, L3_attn_Wk, L3_attn_Wv, L3_attn_Wo)
    h = h + _L3_ffn_ref(_layernorm(h, axis=-1), L3_ffn_tile_sigs, L3_ffn_W, L3_ffn_b)
    return h

_drawn_inputs = setup_inputs


def setup_inputs(seed=0):
    import zlib

    import numpy as np

    out = dict(_drawn_inputs(seed))
    spreads = {'L0_attn_b_dt': (-6.907255172729492, 0.2),
     'L0_attn_D': (1.0, 0.2),
     'L0_ffn_bg': (0.0, 2.0),
     'L1_attn_norm_w': (1.0, 0.6),
     'L1_attn_in_b': (0.0, 0.8),
     'L1_attn_conv_b': (0.0, 0.8),
     'L1_attn_param_b': (0.0, 0.8),
     'L1_attn_skip': (1.0, 0.6),
     'L1_attn_out_b': (0.0, 0.796),
     'L2_ffn_bg': (0.0, 0.619)}
    factors = {'L0_attn_W_dt': 31.773,
     'L0_ffn_Wg': 12.538,
     'L1_attn_in_w': 8.0,
     'L1_attn_conv_w': 8.0,
     'L1_attn_param_w': 8.0,
     'L1_attn_out_w': 8.0,
     'L1_ffn_fc1_A': 8.0,
     'L1_ffn_fc1_B': 8.0,
     'L1_ffn_fc2_A': 8.0,
     'L1_ffn_fc2_B': 8.0,
     'L1_ffn_fc1_logits': 8.0,
     'L1_ffn_fc2_logits': 8.0,
     'L2_ffn_be': 22.096,
     'L3_attn_Wq': 8.0,
     'L3_attn_Wk': 8.0,
     'L3_attn_Wv': 4.331,
     'L3_attn_Wo': 3.016,
     'L3_ffn_b': 27.107,
     'L0_ffn_W1': 4.08,
     'L0_ffn_W2': 3.982,
     'L0_ffn_W3': 4.073,
     'L2_attn_Wq': 4.114,
     'L2_attn_Wk': 4.39}
    for name, (base, spread) in spreads.items():
        noise = np.random.default_rng([zlib.crc32(name.encode()), seed]).standard_normal(out[name].shape)
        drawn = base * np.exp(spread * noise) if base else spread * noise
        out[name] = jnp.asarray(drawn.astype(out[name].dtype))
    for name, factor in factors.items():
        out[name] = (out[name] * factor).astype(out[name].dtype)
    return out
```

```python
from contextlib import ExitStack

import numpy as np

import concourse.bass as bass
from concourse import mybir

ALU = mybir.AluOpType
ACT = mybir.ActivationFunctionType
F32 = mybir.dt.float32
I32 = mybir.dt.int32
AX_X = mybir.AxisListType.X

P = 128
D = 256
HALVES = D // P
BATCH = 32
N_IMG = 36
N_TXT = 32
SEQ = N_IMG + N_TXT
TOKENS = BATCH * SEQ
TILES = TOKENS // P
CHUNK_BATCHES = [7, 7, 6, 6, 6]
CHUNKS = len(CHUNK_BATCHES)
CHUNK_B0 = [sum(CHUNK_BATCHES[:c]) for c in range(CHUNKS)]
NMAX = max(CHUNK_BATCHES) * SEQ
FAN_IN = 768
KT_TOK = FAN_IN // P
N_STATE = 16
DT_RANK = 64
CONV = 4
EXPERTS = 8
HIDDEN = 1024
HT = HIDDEN // P
PRIMS = 64
RANK = 64
TOP_PRIMS = 32
PRIM_TILES = PRIMS * RANK // P
KV_HEADS = 4
GROUP = 4
HEAD = 16
HPAD = 32
EPS_LN = 1e-5
EPS_RMS = 1e-6
NEG = -1e30

L0A, L0F, L1A, L1F, L2A, L2F, L3A, L3F = range(8)


class Banks:

    def __init__(self, tensor, banks):
        self.tensor, self.banks = tensor, banks
        self.index, self.freed = {}, []

    def plan(self, key, freed_by):
        self.index[key] = len(self.freed)
        self.freed.append(freed_by)

    def at(self, key):
        return self.tensor[:, self.banks[self.index[key] % len(self.banks)], :]

    def wait_free(self, engine, key):
        i = self.index[key] - len(self.banks)
        if i >= 0:
            engine.wait_ge(*self.freed[i])
        return self.at(key)


def build(nc, t, out):
    with ExitStack() as ctx:
        def sb(name, shape, dt=F32):
            return ctx.enter_context(nc.sbuf_tensor(name, shape, dt))

        sems = {}

        def sem(name):
            if name not in sems:
                sems[name] = ctx.enter_context(nc.semaphore(name))
            return sems[name]

        h = sb("h", [P, HALVES, TOKENS])
        xn = sb("xn", [P, HALVES, TOKENS])
        ident = sb("ident", [P, P])
        eps_ln = sb("eps_ln", [P, 1])
        eps_rms = sb("eps_rms", [P, 1])
        mean_w = sb("mean_w", [P, P])
        ones = sb("ones", [P, P])
        causal = sb("causal", [SEQ, SEQ])
        sq = sb("sq", [P, 2, HALVES, NMAX])
        std = sb("std", [P, 2, NMAX])
        rstd = sb("rstd", [P, 2, NMAX])
        wz = sb("wz", [P, HALVES, D])
        wpar = sb("wpar", [P, HALVES, DT_RANK + N_STATE])
        wdt = sb("wdt", [DT_RANK, D])
        wout0 = sb("wout0", [P, HALVES, D])
        conv0 = sb("conv0", [P, HALVES, CONV])
        dtb = sb("dtb", [P, HALVES])
        alog = sb("alog", [P, HALVES, N_STATE])
        a_neg = sb("a_neg", [P, HALVES, N_STATE])
        a_keep = sb("a_keep", [P, HALVES, N_STATE])
        a_guard = sb("a_guard", [P, HALVES, N_STATE])
        w_f = sb("w_f", [P, HALVES, N_STATE])
        guarded = sb("guarded", [P, 1])
        any_guard = sb("any_guard", [1, 1], I32)
        a_t = sb("a_t", [P, 4, D])
        skip0 = sb("skip0", [P, HALVES])
        tokb = sb("tokb", [P, HALVES])
        w_attn = sb("w_attn", [P, 6 * HALVES * D])
        part = lambda a, n, **k: w_attn[:, a:a + n].rearrange("p (k n) -> p k n", **k)
        win1 = part(0, 4 * D, k=HALVES)
        wp1 = part(4 * D, 6 * D, k=HALVES)
        wout1 = part(10 * D, 2 * D, k=HALVES)
        vec1 = sb("vec1", [P, 2 + 4 + 8 + 2 + 6 + 2 + 2])
        wq2 = sb("wq2", [P, HALVES, D])
        wk2 = sb("wk2", [P, HALVES, D])
        wv2 = sb("wv2", [P, HALVES, D])
        wo2 = sb("wo2", [P, HALVES, D])
        wg0 = sb("wg0", [P, HALVES, EXPERTS])
        wg2 = sb("wg2", [P, HALVES, EXPERTS])
        sig3 = sb("sig3", [P, HALVES, EXPERTS])
        sgn3 = sb("sgn3", [P, 2, HALVES, EXPERTS])
        bg0 = sb("bg0", [P, EXPERTS])
        bg2 = sb("bg2", [P, EXPERTS])
        first = sb("first", [P, EXPERTS])
        be2 = sb("be2", [EXPERTS, D])
        be3 = sb("be3", [EXPERTS, D])
        wq3 = part(0, 4 * D, k=HALVES * GROUP).rearrange("p (k j) n -> p k j n", k=HALVES)
        wk3 = part(4 * D, D, k=HALVES)
        wv3 = part(5 * D, D, k=HALVES)
        wo3 = part(6 * D, 4 * D, k=GROUP)
        gate = sb("gate", [P, 6, TILES, EXPERTS])
        gcol = sb("gcol", [P, 8, TILES])
        prow = sb("prow", [PRIMS, 2, PRIMS])
        pcol = sb("pcol", [PRIMS, 2, 8])
        ptmp = sb("ptmp", [PRIMS, 2, PRIMS])
        ptmp2 = sb("ptmp2", [PRIMS, 2, PRIMS])
        lower = sb("lower", [PRIMS, PRIMS])
        pair = sb("pair", [PRIMS, PRIM_TILES])
        sel2 = sb("sel2", [PRIMS, P])
        wexp = sb("wexp", [P, 2, PRIM_TILES])
        w_late = sb("w_late", [P, EXPERTS * HALVES * D])
        w1c = w_late[:, 0:HALVES * HIDDEN].rearrange("p (k n) -> p k n", k=HALVES)
        w2c = w_late[:, HALVES * HIDDEN:].rearrange("p (k n) -> p k n", k=HT)
        w_last = w_late[:].rearrange("p (e k n) -> p e k n", e=EXPERTS, k=HALVES)
        WORK = 25700
        work = sb("work", [P, WORK])
        psum = ctx.enter_context(nc.psum_tensor("psum", [P, 8, 512], F32))

        gT = work[0:EXPERTS, WORK - TOKENS:WORK]
        cursor = [0]

        def carve(n):
            cursor[0] += n
            assert cursor[0] <= WORK - TOKENS, cursor
            return work[:, cursor[0] - n:cursor[0]]

        def full(parts=HALVES):
            return carve(parts * TOKENS).rearrange("p (m t) -> p m t", m=parts)

        cursor[0] = 0
        xp = carve(KT_TOK * BATCH * N_IMG).rearrange("p (k n) -> p k n", k=KT_TOK)
        wtok = carve(KT_TOK * D).rearrange("p (k n) -> p k n", k=KT_TOK)
        txt = carve(HALVES * BATCH * N_TXT).rearrange("p (m b t) -> p m b t", m=HALVES, t=N_TXT)
        cursor[0] = 0
        zs = full()
        u0 = full()
        dtx = full()
        d1 = carve(HALVES * BATCH * (SEQ + 1)).rearrange("p (m b t) -> p m b t", m=HALVES, t=SEQ + 1)
        pc = carve(TOKENS)
        NS = max(CHUNK_BATCHES) * (SEQ + 1)
        d_sel = sq[:].rearrange("p r m n -> p (r m n)")[:, 0:2 * NS].rearrange("p (r n) -> p r n", r=2)
        a_buf = carve(2 * NS).rearrange("p (r n) -> p r n", r=2)
        f_buf = carve(2 * NS).rearrange("p (r n) -> p r n", r=2)
        ym = carve(2 * NMAX).rearrange("p (r n) -> p r n", r=2)
        sp_a = sq[:, 0]
        sp_r = sq[:, 1]
        xcv0 = carve(HALVES * NMAX).rearrange("p (m n) -> p m n", m=HALVES)
        ytmp = xcv0
        cursor[0] = 0
        w13 = carve(2 * 2 * HALVES * HIDDEN).rearrange("p (r w k n) -> p r w k n", r=2, w=2, k=HALVES)
        w2 = carve(2 * HT * D).rearrange("p (r k n) -> p r k n", r=2, k=HT)
        xs = carve(2 * HALVES * NMAX).rearrange("p (r m n) -> p r m n", r=2, m=HALVES)
        hm = carve(2 * HT * NMAX).rearrange("p (r m n) -> p r m n", r=2, m=HT)
        sa = carve(2 * NMAX).rearrange("p (r n) -> p r n", r=2)
        cursor[0] = 0
        u1 = full()
        gs = full()
        xr = full()
        up = carve(2 * HALVES * NMAX).rearrange("p (r m n) -> p r m n", r=2, m=HALVES)
        xcv1 = carve(2 * HALVES * NMAX).rearrange("p (r m n) -> p r m n", r=2, m=HALVES)
        abc = carve(2 * 6 * NMAX).rearrange("p (r m n) -> p r m n", r=2, m=6)
        cursor[0] = 0
        PSLOTS = 4
        tile_long = carve(PSLOTS * HIDDEN).rearrange("p (r n) -> p r n", r=PSLOTS)
        tile_short = carve(PSLOTS * D).rearrange("p (r n) -> p r n", r=PSLOTS)
        hm1 = carve(2 * HT * NMAX).rearrange("p (r m n) -> p r m n", r=2, m=HT)
        cursor[0] = 0
        qk = full(4)
        vb = carve(BATCH * D).rearrange("p (b n) -> p b n", n=D)
        pr = carve(CHUNKS * NMAX).rearrange("p (c n) -> p c n", c=CHUNKS)
        pT = carve(2 * NMAX).rearrange("p (r n) -> p r n", r=2)
        oT = carve(2 * HALVES * NMAX).rearrange("p (r m n) -> p r m n", r=2, m=HALVES)
        st = carve(CHUNKS * 3 * 8).rearrange("p (c a n) -> p c a n", c=CHUNKS, a=3)
        cursor[0] = 0
        xs2 = carve(2 * HALVES * NMAX).rearrange("p (r m n) -> p r m n", r=2, m=HALVES)
        cursor[0] = 2 * HALVES * NMAX
        kblk = carve(BATCH * KV_HEADS * SEQ).rearrange("p (b g s) -> p b g s", g=KV_HEADS, s=SEQ)
        vb3 = carve(BATCH * P).rearrange("p (b n) -> p b n", n=P)
        q3 = carve(GROUP * 2 * NMAX).rearrange("p (r j n) -> p r j n", r=2, j=GROUP)
        p3 = carve(2 * GROUP * KV_HEADS * SEQ).rearrange("p (r j g s) -> p r j g s", r=2, j=GROUP, g=KV_HEADS)
        pT3 = carve(4 * GROUP * SEQ).rearrange("p (r n) -> p r n", r=4)
        oT3 = xs2_oT3 = work[:, 0:GROUP * NMAX].rearrange("p (j n) -> p j n", j=GROUP)
        st3 = carve(2 * 3 * GROUP * KV_HEADS).rearrange("p (r a n) -> p r a n", r=2, a=3)

        nw1, inb1, cw1, cb1, pb1, sk1, ob1 = (vec1[:, a:b] for a, b in
                                              ((0, 2), (2, 6), (6, 14), (14, 16), (16, 22), (22, 24), (24, 26)))

        def chunk(c):
            return slice(CHUNK_B0[c] * SEQ, (CHUNK_B0[c] + CHUNK_BATCHES[c]) * SEQ)

        def ntok(c):
            return CHUNK_BATCHES[c] * SEQ

        def seqs(ap):
            return ap.rearrange("p (b t) -> p b t", t=SEQ)

        def both(ap, n):
            return ap.unsqueeze(1).to_broadcast([P, HALVES, n])

        def H(block, c, m):
            return 2 * (block * CHUNKS + c) + m + 1

        h_ready = sem("h_ready")
        wait_h = lambda e, block, c: e.wait_ge(h_ready, H(block, c, 1))

        A = Banks(psum, [0, 1, 2, 3, 4, 5])
        B = Banks(psum, [6, 7])
        pe_order = []

        def step(*what):
            pe_order.append(what)

        def plan_ln(b):
            for c in range(CHUNKS):
                A.plan(("mean", b, c), (sem("centred"), b * CHUNKS + c + 1))
                step("mean", b, c)
            for c in range(CHUNKS):
                if b == L1A:
                    A.plan(("var", b, c), (sem("rms_arg"), c + 1))
                else:
                    A.plan(("var", b, c), (sem("std_done"), b * CHUNKS + c + 1))
                step("var", b, c)

        def plan_h(key, block, c):
            for m in range(HALVES):
                A.plan((key, c, m), (h_ready, H(block + 1, c, m)))
            step(key, c)

        def plan_router(r):
            A.plan(("logits", r), (sem("logits_used"), r + 1))
            step("logits", r)
            for j in range(CHUNKS):
                A.plan(("gateT", r, j), (sem("gateT_kept"), r * CHUNKS + j + 1))
            step("gateT", r)

        def plan_gb(r, q):
            A.plan(("gb", r, q), (sem("x_gated"), 40 * r + q + 1))
            step("gb", r, q)

        for c in range(CHUNKS):
            for m in range(HALVES):
                A.plan(("tok", c, m), (h_ready, H(0, c, m)))
            step("tok", c)
        plan_ln(L0A)
        A.plan(("guards",), (sem("guards_kept"), 1))
        step("guards")
        A.plan(("prim_sum",), (sem("prim_sum_used"), 1))
        A.plan(("prim_w",), (sem("prim_w_kept"), 1))
        step("prims")
        for c in range(CHUNKS):
            for m in range(HALVES):
                A.plan(("z", c, m), (sem("z_silu"), 2 * c + m + 1))
            A.plan(("par", c), (sem("par_kept"), c + 1))
            step("z", c)
        for c in range(CHUNKS):
            for m in range(HALVES):
                A.plan(("dt", c, m), (sem("dt_relu"), 2 * c + m + 1))
            step("dt", c)
        A.plan(("cb", 0), (sem("y_part"), 2))
        step("cb", 0)
        for k in range(CHUNKS * N_STATE):
            c, n = divmod(k, N_STATE)
            if n == 0:
                for m in range(HALVES):
                    B.plan(("yacc", c, m), (sem("y_gated"), 2 * c + m + 1))
            if k + 1 < CHUNKS * N_STATE:
                A.plan(("cb", k + 1), (sem("y_part"), 2 * (k + 1) + 2))
                step("cb", k + 1)
            step("yacc", k)
            if n == N_STATE - 1:
                for m in range(HALVES):
                    A.plan(("w2c", c, m), (sem("y_gated"), 2 * c + m + 1))
                step("w2c", c)
                plan_h("out0", L0A, c)
        plan_ln(L0F)
        plan_router(0)
        NQ = EXPERTS * CHUNKS
        plan_gb(0, 0)
        for q in range(NQ + 1):
            if q + 1 < NQ:
                plan_gb(0, q + 1)
            if q < NQ:
                for j in range(HT):
                    A.plan(("e1", q, j), (sem("e1_silu"), HT * q + j + 1))
                    A.plan(("e3", q, j), (sem("hidden"), HT * q + j + 1))
                step("e13", q)
            if q:
                e, c = divmod(q - 1, CHUNKS)
                for m in range(HALVES):
                    B.plan(("ey", q - 1, m), (h_ready, H(L1A, c, m)) if e == EXPERTS - 1
                           else (sem("h_expert"), 2 * (q - 1) + m + 1))
                step("ey", q - 1)
        plan_ln(L1A)
        for c in range(CHUNKS):
            for j in range(4):
                A.plan(("in1", c, j), (sem("in1_u"), 2 * c + j + 1) if j < 2 else (sem("in1_gate"), 2 * c + j - 1))
            step("in1", c)
        for c in range(CHUNKS):
            for j in range(6):
                A.plan(("par1", c, j), (sem("abc_done"), 6 * c + j + 1))
            step("par1", c)
            if c:
                plan_h("out1", L1A, c - 1)
        plan_h("out1", L1A, CHUNKS - 1)
        for f in range(2):
            for j in range(4):
                A.plan(("comp", f, j), (sem("composed"), 4 * f + j + 1))
            step("comp", f)
        plan_ln(L1F)
        for c in range(CHUNKS + 1):
            if c < CHUNKS:
                for j in range(HT):
                    A.plan(("f1", c, j), (sem("f1_gelu"), HT * c + j + 1))
                step("f1", c)
            if c:
                for m in range(HALVES):
                    B.plan(("f2", c - 1, m), (h_ready, H(L2A, c - 1, m)))
                step("f2", c - 1)
        plan_ln(L2A)
        VP = [(CHUNK_BATCHES[c] + 1) // 2 for c in range(CHUNKS)]
        V0 = [sum(VP[:c]) for c in range(CHUNKS + 1)]
        for c in range(CHUNKS):
            for j in range(4):
                A.plan(("qk", c, j), (sem("qk_kept"), 4 * c + j + 1))
            for j in range(VP[c]):
                A.plan(("v2", c, j), (sem("v2_kept"), V0[c] + j + 1))
            step("qkv2", c)
            A.plan(("s2", c), (sem("s2_scaled"), c + 1))
            step("s2", c)
        for c in range(CHUNKS):
            A.plan(("pT2", c), (sem("pT2_kept"), c + 1))
            step("pT2", c)
            for m in range(HALVES):
                A.plan(("o2", c, m), (sem("o2_kept"), 2 * c + m + 1))
            step("o2", c)
            plan_h("out2", L2A, c)
        plan_ln(L2F)
        plan_router(1)

        def plan_dense(r, block):
            plan_gb(r, 0)
            for q in range(NQ):
                c, e = divmod(q, EXPERTS)
                if q + 1 < NQ:
                    plan_gb(r, q + 1)
                if e == 0:
                    for m in range(HALVES):
                        B.plan(("dy", r, c, m), (h_ready, H(block + 1, c, m)))
                step("dense", r, q)

        plan_dense(1, L2F)
        plan_ln(L3A)
        V3 = [(CHUNK_BATCHES[c] + 3) // 4 for c in range(CHUNKS)]
        V30 = [sum(V3[:c]) for c in range(CHUNKS + 1)]
        for c in range(CHUNKS):
            A.plan(("k3", c), (sem("k3_kept"), c + 1))
            for j in range(V3[c]):
                A.plan(("v3", c, j), (sem("v3_kept"), V30[c] + j + 1))
            step("kv3", c)

        def plan_s3(b):
            for j in range(GROUP):
                A.plan(("s3", b, j), (sem("s3_shifted"), GROUP * b + j + 1))
            step("s3", b)

        def plan_q3(c):
            for j in range(GROUP):
                A.plan(("q3", c, j), (sem("q3_kept"), GROUP * c + j + 1))
            step("q3", c)

        plan_q3(0)
        plan_s3(0)
        for b in range(BATCH):
            if b in CHUNK_B0 and CHUNK_B0.index(b) + 1 < CHUNKS:
                plan_q3(CHUNK_B0.index(b) + 1)
            if b + 1 < BATCH:
                plan_s3(b + 1)
            for g in range(KV_HEADS):
                A.plan(("pT3", b, g), (sem("pT3_kept"), KV_HEADS * b + g + 1))
            B.plan(("o3", b), (sem("o3_kept"), b + 1))
            step("pv3", b)
            if b + 1 == BATCH or b + 1 in CHUNK_B0:
                plan_h("out3", L3A, CHUNKS - 1 if b + 1 == BATCH else CHUNK_B0.index(b + 1) - 1)
        plan_ln(L3F)
        plan_router(2)
        plan_dense(2, L3F)

        chunk_of = [c for c in range(CHUNKS) for _ in range(CHUNK_BATCHES[c])]
        router_block = [L0F, L2F, L3F]

        block = ctx.enter_context(nc.Block())

        @block.sync
        def _(sp):
            def load(dst, name, signal):
                sp.dma_start(dst, t[name]).then_inc(sem(signal), 16)

            load(wtok, "wtok", "tok_loaded")
            load(xp, "xp", "tok_loaded")
            load(tokb[:], "tokb", "tok_loaded")
            load(txt, "txt", "txt_loaded")
            for dst, name in ((wz, "wz"), (wpar, "wpar"), (wdt, "wdt"), (wout0, "wout0"), (conv0, "conv0"),
                              (dtb, "dtb"), (alog, "alog"), (skip0, "skip0")):
                load(dst[:], name, "l0_loaded")
            load(a_t[DT_RANK:DT_RANK + N_STATE, 0, :], "alogT", "l0_loaded")
            for dst, name in ((lower, "lower"), (pair, "pair"), (sel2, "sel2")):
                load(dst[:], name, "prim_loaded")
            for f, name in enumerate(("fc1_logits", "fc2_logits")):
                sp.dma_start(prow[:, f, :], t[name + "_row"].to_broadcast([PRIMS, PRIMS])).then_inc(
                    sem("prim_loaded"), 16)
                sp.dma_start(pcol[:, f, 0:1], t[name + "_col"]).then_inc(sem("prim_loaded"), 16)
            for dst, name in ((wg0, "wg0"), (wg2, "wg2"), (sig3, "sig3"), (be2, "be2"), (be3, "be3")):
                load(dst[:], name, "gate_loaded")
            for dst, name in ((bg0, "bg0"), (bg2, "bg2"), (first, "first")):
                sp.dma_start(dst[:], t[name].to_broadcast([P, EXPERTS])).then_inc(sem("gate_loaded"), 16)
            for dst, name in ((win1, "win1"), (wp1, "wp1"), (wout1, "wout1"), (vec1[:], "vec1"), (wq2[:], "wq2"),
                              (wk2[:], "wk2"), (wv2[:], "wv2"), (wo2[:], "wo2")):
                load(dst, name, "rest_loaded")
            wait_h(sp, L0F, CHUNKS - 1)
            for e in range(EXPERTS):
                if e >= 2:
                    sp.wait_ge(sem("expert_out"), 2 * CHUNKS * (e - 1))
                for w, name in enumerate(("W1", "W3")):
                    sp.dma_start(w13[:, e % 2, w], t[name][e]).then_inc(sem(f"expert_loaded{e % 2}"), 16)
                sp.dma_start(w2[:, e % 2], t["W2"][e]).then_inc(sem(f"expert_loaded{e % 2}"), 16)
            wait_h(sp, L1F, CHUNKS - 1)
            for i in range(2 * PRIM_TILES):
                f, kt = divmod(i, PRIM_TILES)
                if i >= PSLOTS:
                    sp.wait_ge(sem("tile_used"), i - PSLOTS + 1)
                sp.dma_start(tile_long[:, i % PSLOTS], t[("B1", "A2")[f]][kt]).then_inc(sem(f"tile{i % PSLOTS}"), 16)
                sp.dma_start(tile_short[:, i % PSLOTS], t[("A1", "B2")[f]][kt]).then_inc(sem(f"tile{i % PSLOTS}"), 16)
            for dst, name in ((wq3, "wq3"), (wk3, "wk3"), (wv3, "wv3"), (wo3, "wo3")):
                load(dst, name, "attn3_loaded")
            wait_h(sp, L2A, CHUNKS - 1)
            load(w_last, "we2", "we2_loaded")
            wait_h(sp, L3A, CHUNKS - 1)
            load(w_last, "we3", "we3_loaded")
            for c in range(CHUNKS):
                wait_h(sp, L3F + 1, c)
                sp.dma_start(out[:, :, chunk(c)], h[:, :, chunk(c)]).then_inc(sem("stored"), 16)
            sp.wait_ge(sem("stored"), 16 * CHUNKS)

        @block.tensor
        def _(pe):
            def product(dst, lhs, rhs, parts):
                for k in range(parts):
                    mm = pe.matmul(dst, lhs(k), rhs(k), start=(k == 0), stop=(k == parts - 1))
                return mm

            def mean(b, c):
                if b == 0 and c == 0:
                    pe.wait_ge(sem("txt_placed"), 1)
                    pe.wait_ge(sem("consts"), 1)
                wait_h(pe, b, c)
                dst = A.wait_free(pe, ("mean", b, c))
                product(dst[:, 0:ntok(c)], lambda k: mean_w[:], lambda k: h[:, k, chunk(c)],
                        HALVES).then_inc(sem("mean_done"), 1)

            def var(b, c):
                i = b * CHUNKS + c
                pe.wait_ge(sem("squared"), i + 1)
                dst = A.wait_free(pe, ("var", b, c))
                product(dst[:, 0:ntok(c)], lambda k: mean_w[:], lambda k: sq[:, i % 2, k, 0:ntok(c)],
                        HALVES).then_inc(sem("var_done"), 1)

            def into_h(key, w, rhs, c, parts=HALVES, ring=A, signal="to_h"):
                for m in range(HALVES):
                    dst = ring.wait_free(pe, (key, c, m))
                    product(dst[:, 0:ntok(c)], lambda k: w[:, k, m * P:(m + 1) * P], rhs, parts).then_inc(sem(signal), 1)

            def tok(c):
                if c == 0:
                    pe.wait_ge(sem("tok_loaded"), 48)
                nb, b0 = CHUNK_BATCHES[c], CHUNK_B0[c]
                for m in range(HALVES):
                    dst = A.wait_free(pe, ("tok", c, m))
                    product(dst[:, 0:nb * N_IMG], lambda k: wtok[:, k, m * P:(m + 1) * P],
                            lambda k: xp[:, k, b0 * N_IMG:(b0 + nb) * N_IMG], KT_TOK).then_inc(sem("tok_done"), 1)

            def prims():
                pe.wait_ge(sem("prim_exp"), 1)
                dst = A.wait_free(pe, ("prim_sum",))
                pe.matmul(dst[0:PRIMS, 0:2], ones[0:PRIMS, 0:PRIMS], pcol[:, :, 3], start=True,
                          stop=True).then_inc(sem("prim_sum"), 1)
                pe.wait_ge(sem("prim_spread"), 1)
                dst = A.wait_free(pe, ("prim_w",))
                pe.matmul(dst[:, 0:2 * PRIM_TILES], sel2[:], ptmp[:, 0, :], start=True, stop=True).then_inc(sem("prim_w"), 1)

            def guards():
                pe.wait_ge(sem("guards_listed"), 1)
                dst = A.wait_free(pe, ("guards",))
                pe.matmul(dst[0:1, 0:1], ones[:, 0:1], guarded[:], start=True, stop=True).then_inc(
                    sem("guards_counted"), 1)

            def z(c):
                if c == 0:
                    pe.wait_ge(sem("l0_loaded"), 9 * 16)
                pe.wait_ge(sem("normed"), c + 1)
                for m in range(HALVES):
                    dst = A.wait_free(pe, ("z", c, m))
                    product(dst[:, 0:ntok(c)], lambda k: wz[:, k, m * P:(m + 1) * P], lambda k: xn[:, k, chunk(c)],
                            HALVES).then_inc(sem("z_done"), 1)
                dst = A.wait_free(pe, ("par", c))
                product(dst[0:DT_RANK + N_STATE, 0:ntok(c)], lambda k: wpar[:, k, :], lambda k: xn[:, k, chunk(c)],
                        HALVES).then_inc(sem("par_done"), 1)

            def dt(c):
                pe.wait_ge(sem("par_kept"), c + 1)
                for m in range(HALVES):
                    dst = A.wait_free(pe, ("dt", c, m))
                    pe.matmul(dst[:, 0:ntok(c)], wdt[:, m * P:(m + 1) * P], pc[0:DT_RANK, chunk(c)], start=True,
                              stop=True).then_inc(sem("dt_done"), 1)

            def cb(k):
                c, n = divmod(k, N_STATE)
                lo, hi = DT_RANK, DT_RANK + N_STATE
                dst = A.wait_free(pe, ("cb", k))
                pe.matmul(dst[:, 0:ntok(c)], ident[lo:hi, lo + n:lo + n + 1].to_broadcast([N_STATE, P]),
                          pc[lo:hi, chunk(c)], start=True, stop=True).then_inc(sem("c_spread"), 1)

            def yacc(k):
                c, n = divmod(k, N_STATE)
                for m in range(HALVES):
                    g = 2 * k + m
                    dst = B.wait_free(pe, ("yacc", c, m)) if n == 0 else B.at(("yacc", c, m))
                    pe.wait_ge(sem("y_part"), g + 1)
                    pe.matmul(dst[:, 0:ntok(c)], ident[:], ym[:, g % 2, 0:ntok(c)], start=(n == 0),
                              stop=(n == N_STATE - 1)).then_inc(sem("y_added"), 1)

            def w2c_(c):
                if c == 0:
                    pe.wait_ge(sem("a_ready"), 1)
                lo, hi = DT_RANK, DT_RANK + N_STATE
                for m in range(HALVES):
                    dst = A.wait_free(pe, ("w2c", c, m))
                    pe.matmul(dst[:, 0:ntok(c)], a_t[lo:hi, 3, m * P:(m + 1) * P], pc[lo:hi, chunk(c)], start=True,
                              stop=True).then_inc(sem("cw_done"), 1)

            def out0(c):
                pe.wait_ge(sem("y_gated"), 2 * c + 2)
                into_h("out0", wout0, lambda k: zs[:, k, chunk(c)], c)

            def logits(r):
                blk = router_block[r]
                if r == 0:
                    pe.wait_ge(sem("gate_loaded"), 8 * 16)
                    pe.wait_ge(sem("signs"), 1)
                pe.wait_ge(sem("normed"), (blk + 1) * CHUNKS)
                w = (wg0[:], wg2[:], sgn3[:, 0])[r]
                dst = A.wait_free(pe, ("logits", r))
                for i in range(TILES):
                    mm = product(dst[:, i * EXPERTS:(i + 1) * EXPERTS], lambda k: xn[:, k, i * P:(i + 1) * P],
                                 lambda k: w[:, k, :], HALVES)
                mm.then_inc(sem("logits_done"), 1)

            def gateT(r):
                pe.wait_ge(sem("gates"), r + 1)
                for j in range(CHUNKS):
                    dst = A.wait_free(pe, ("gateT", r, j))
                    for i in range(4 * j, min(4 * j + 4, TILES)):
                        tr = pe.transpose(dst[0:EXPERTS, (i - 4 * j) * P:(i - 4 * j + 1) * P], gate[:, 5, i, :], ident[:])
                    tr.then_inc(sem("gateT_done"), 1)

            def gb(r, q):
                e, c = divmod(q, CHUNKS) if r == 0 else divmod(q, EXPERTS)[::-1]
                if q == 0:
                    pe.wait_ge(sem("gateT_kept"), (r + 1) * CHUNKS)
                dst = A.wait_free(pe, ("gb", r, q))
                pe.matmul(dst[:, 0:ntok(c)], ident[0:EXPERTS, e:e + 1].to_broadcast([EXPERTS, P]), gT[:, chunk(c)],
                          start=True, stop=True).then_inc(sem("gate_spread"), 1)

            def e13(q):
                e, c = divmod(q, CHUNKS)
                if c == 0:
                    pe.wait_ge(sem(f"expert_loaded{e % 2}"), 48 * (e // 2 + 1))
                pe.wait_ge(sem("x_gated"), q + 1)
                for j in range(HT):
                    for w, (key, done) in enumerate((("e1", "e1_done"), ("e3", "e3_done"))):
                        dst = A.wait_free(pe, (key, q, j))
                        product(dst[:, 0:ntok(c)], lambda k: w13[:, e % 2, w, k, j * P:(j + 1) * P],
                                lambda k: xs[:, q % 2, k, 0:ntok(c)], HALVES).then_inc(sem(done), 1)

            def ey(q):
                e, c = divmod(q, CHUNKS)
                pe.wait_ge(sem("hidden"), HT * (q + 1))
                for m in range(HALVES):
                    dst = B.wait_free(pe, ("ey", q, m))
                    product(dst[:, 0:ntok(c)], lambda k: w2[:, e % 2, k, m * P:(m + 1) * P],
                            lambda k: hm[:, q % 2, k, 0:ntok(c)], HT).then_inc(sem("expert_out"), 1)

            def in1(c):
                if c == 0:
                    pe.wait_ge(sem("rest_loaded"), 8 * 16)
                pe.wait_ge(sem("rms_normed"), 2 * c + 2)
                for j in range(4):
                    dst = A.wait_free(pe, ("in1", c, j))
                    product(dst[:, 0:ntok(c)], lambda k: win1[:, k, j * P:(j + 1) * P],
                            lambda k: xr[:, k, chunk(c)], HALVES).then_inc(sem("in1_done"), 1)

            def par1(c):
                pe.wait_ge(sem("u1_done"), 2 * c + 2)
                for j in range(6):
                    dst = A.wait_free(pe, ("par1", c, j))
                    product(dst[:, 0:ntok(c)], lambda k: wp1[:, k, j * P:(j + 1) * P], lambda k: u1[:, k, chunk(c)],
                            HALVES).then_inc(sem("par1_done"), 1)

            def out1(c):
                pe.wait_ge(sem("y1_gated"), 2 * c + 2)
                into_h("out1", wout1, lambda k: gs[:, k, chunk(c)], c)

            def comp(f):
                banks = [A.wait_free(pe, ("comp", f, j)) for j in range(4)]
                for kt in range(PRIM_TILES):
                    i = f * PRIM_TILES + kt
                    s = i % PSLOTS
                    pe.wait_ge(sem("tile_scaled"), i + 1)
                    first_mm, last_mm = kt == 0, kt == PRIM_TILES - 1
                    if f == 0:
                        for m in range(HALVES):
                            for n in range(2):
                                mm = pe.matmul(banks[2 * m + n], tile_short[:, s, m * P:(m + 1) * P],
                                               tile_long[:, s, n * 512:(n + 1) * 512], start=first_mm, stop=last_mm)
                    else:
                        for j in range(HT):
                            mm = pe.matmul(banks[j // 2][:, (j % 2) * D:(j % 2 + 1) * D],
                                           tile_long[:, s, j * P:(j + 1) * P], tile_short[:, s, :],
                                           start=first_mm and j % 2 == 0, stop=last_mm, skip_group_check=True)
                    mm.then_inc(sem("tile_used"), 1)

            def f1(c):
                if c == 0:
                    pe.wait_ge(sem("composed"), 8)
                pe.wait_ge(sem("normed"), L1F * CHUNKS + c + 1)
                for j in range(HT):
                    dst = A.wait_free(pe, ("f1", c, j))
                    product(dst[:, 0:ntok(c)], lambda k: w1c[:, k, j * P:(j + 1) * P], lambda k: xn[:, k, chunk(c)],
                            HALVES).then_inc(sem("f1_done"), 1)

            def f2(c):
                pe.wait_ge(sem("f1_gelu"), HT * (c + 1))
                into_h("f2", w2c, lambda k: hm1[:, c % 2, k, 0:ntok(c)], c, HT, B)

            def qkv2(c):
                pe.wait_ge(sem("normed"), L2A * CHUNKS + c + 1)
                for j in range(4):
                    w = (wq2, wk2)[j // 2]
                    dst = A.wait_free(pe, ("qk", c, j))
                    product(dst[:, 0:ntok(c)], lambda k: w[:, k, (j % 2) * P:(j % 2 + 1) * P],
                            lambda k: xn[:, k, chunk(c)], HALVES).then_inc(sem("qk_done"), 1)
                for j in range(VP[c]):
                    dst = A.wait_free(pe, ("v2", c, j))
                    for i in range(2 * j, min(2 * j + 2, CHUNK_BATCHES[c])):
                        b = CHUNK_B0[c] + i
                        mm = product(dst[0:SEQ, (i % 2) * D:(i % 2 + 1) * D], lambda k: xn[:, k, b * SEQ:(b + 1) * SEQ],
                                     lambda k: wv2[:, k, :], HALVES)
                    mm.then_inc(sem("v2_done"), 1)

            def s2(c):
                pe.wait_ge(sem("qk_kept"), 4 * c + 4)
                dst = A.wait_free(pe, ("s2", c))
                for i in range(CHUNK_BATCHES[c]):
                    b = CHUNK_B0[c] + i
                    mm = product(dst[0:SEQ, i * SEQ:(i + 1) * SEQ], lambda k: qk[:, k, b * SEQ:(b + 1) * SEQ],
                                 lambda k: qk[:, 2 + k, b * SEQ:(b + 1) * SEQ], HALVES)
                mm.then_inc(sem("s2_done"), 1)

            def pT2(c):
                pe.wait_ge(sem("p2_ready"), c + 1)
                dst = A.wait_free(pe, ("pT2", c))
                for i in range(CHUNK_BATCHES[c]):
                    tr = pe.transpose(dst[0:SEQ, i * SEQ:(i + 1) * SEQ], pr[0:SEQ, c, i * SEQ:(i + 1) * SEQ],
                                      ident[0:SEQ, 0:SEQ])
                tr.then_inc(sem("pT2_done"), 1)

            def o2(c):
                pe.wait_ge(sem("pT2_kept"), c + 1)
                pe.wait_ge(sem("v2_kept"), V0[c + 1])
                for m in range(HALVES):
                    dst = A.wait_free(pe, ("o2", c, m))
                    for i in range(CHUNK_BATCHES[c]):
                        mm = pe.matmul(dst[:, i * SEQ:(i + 1) * SEQ], vb[0:SEQ, CHUNK_B0[c] + i, m * P:(m + 1) * P],
                                       pT[0:SEQ, c % 2, i * SEQ:(i + 1) * SEQ], start=True, stop=True)
                    mm.then_inc(sem("o2_done"), 1)

            def out2(c):
                pe.wait_ge(sem("o2_kept"), 2 * c + 2)
                into_h("out2", wo2, lambda k: oT[:, c % 2, k, 0:ntok(c)], c)

            def dense(r, q):
                c, e = divmod(q, EXPERTS)
                if q == 0:
                    pe.wait_ge(sem(("we2_loaded", "we3_loaded")[r - 1]), 16)
                pe.wait_ge(sem("x_gated"), 40 * r + q + 1)
                bias = (be2, be3)[r - 1]
                for m in range(HALVES):
                    dst = B.wait_free(pe, ("dy", r, c, m)) if e == 0 else B.at(("dy", r, c, m))
                    if e == 0:
                        pe.matmul(dst[:, 0:ntok(c)], bias[:, m * P:(m + 1) * P], gT[:, chunk(c)], start=True, stop=False)
                    for k in range(HALVES):
                        mm = pe.matmul(dst[:, 0:ntok(c)], w_last[:, e, k, m * P:(m + 1) * P],
                                       xs2[:, q % 2, k, 0:ntok(c)], start=False,
                                       stop=(e == EXPERTS - 1 and k == HALVES - 1))
                    if e == EXPERTS - 1:
                        mm.then_inc(sem("dense_out"), 1)
                    elif m == HALVES - 1:
                        mm.then_inc(sem("dense_used"), 1)

            def kv3(c):
                if c == 0:
                    pe.wait_ge(sem("attn3_loaded"), 4 * 16)
                pe.wait_ge(sem("normed"), L3A * CHUNKS + c + 1)
                dst = A.wait_free(pe, ("k3", c))
                product(dst[:, 0:ntok(c)], lambda k: wk3[:, k, :], lambda k: xn[:, k, chunk(c)],
                        HALVES).then_inc(sem("k3_done"), 1)
                for j in range(V3[c]):
                    dst = A.wait_free(pe, ("v3", c, j))
                    for i in range(4 * j, min(4 * j + 4, CHUNK_BATCHES[c])):
                        b = CHUNK_B0[c] + i
                        mm = product(dst[0:SEQ, (i % 4) * P:(i % 4 + 1) * P], lambda k: xn[:, k, b * SEQ:(b + 1) * SEQ],
                                     lambda k: wv3[:, k, :], HALVES)
                    mm.then_inc(sem("v3_done"), 1)

            def q3_(c):
                for j in range(GROUP):
                    dst = A.wait_free(pe, ("q3", c, j))
                    product(dst[:, 0:ntok(c)], lambda k: wq3[:, k, j, :], lambda k: xn[:, k, chunk(c)],
                            HALVES).then_inc(sem("q3_done"), 1)

            def s3(b):
                c = chunk_of[b]
                i = b - CHUNK_B0[c]
                pe.wait_ge(sem("q3_kept"), GROUP * (c + 1))
                pe.wait_ge(sem("k3_kept"), c + 1)
                for j in range(GROUP):
                    dst = A.wait_free(pe, ("s3", b, j))
                    pe.matmul(dst[0:SEQ, 0:KV_HEADS * SEQ], q3[:, c % 2, j, i * SEQ:(i + 1) * SEQ], kblk[:, b],
                              start=True, stop=True).then_inc(sem("s3_done"), 1)

            def pv3(b):
                c = chunk_of[b]
                pe.wait_ge(sem("p3_ready"), b + 1)
                for g in range(KV_HEADS):
                    dst = A.wait_free(pe, ("pT3", b, g))
                    for j in range(GROUP):
                        tr = pe.transpose(dst[0:SEQ, j * SEQ:(j + 1) * SEQ], p3[0:SEQ, b % 2, j, g, :],
                                          ident[0:SEQ, 0:SEQ])
                    tr.then_inc(sem("pT3_done"), 1)
                pe.wait_ge(sem("v3_kept"), V30[c + 1])
                dst = B.wait_free(pe, ("o3", b))
                for g in range(KV_HEADS):
                    pe.wait_ge(sem("pT3_kept"), KV_HEADS * b + g + 1)
                    mm = pe.matmul(dst[g * HPAD:(g + 1) * HPAD, 0:GROUP * SEQ], vb3[0:SEQ, b, g * HPAD:(g + 1) * HPAD],
                                   pT3[0:SEQ, g, :], start=True, stop=True, tile_position=(0, g * HPAD))
                mm.then_inc(sem("o3_done"), 1)

            def out3(c):
                pe.wait_ge(sem("o3_kept"), CHUNK_B0[c] + CHUNK_BATCHES[c])
                into_h("out3", wo3, lambda k: oT3[:, k, 0:ntok(c)], c, GROUP)

            steps = {"mean": mean, "var": var, "tok": tok, "prims": prims, "guards": guards, "z": z, "dt": dt, "cb": cb, "yacc": yacc,
                     "w2c": w2c_, "out0": out0, "logits": logits, "gateT": gateT, "gb": gb, "e13": e13, "ey": ey,
                     "in1": in1, "par1": par1, "out1": out1, "comp": comp, "f1": f1, "f2": f2, "qkv2": qkv2,
                     "s2": s2, "pT2": pT2, "o2": o2, "out2": out2, "dense": dense, "kv3": kv3, "q3": q3_,
                     "s3": s3, "pv3": pv3, "out3": out3}
            for name, *args in pe_order:
                steps[name](*args)

        @block.scalar
        def _(act):
            count = [0]

            def link(ins):
                count[0] += 1
                ins.then_inc(sem("act_chain"), 1)
                act.wait_ge(sem("act_chain"), count[0])

            def ln(b):
                for c in range(CHUNKS):
                    i = b * CHUNKS + c
                    act.wait_ge(sem("centred"), i + 1)
                    if i >= 2:
                        act.wait_ge(sem("var_done"), i - 1)
                    act.activation(sq[:, i % 2, :, 0:ntok(c)], xn[:, :, chunk(c)], ACT.Square).then_inc(sem("squared"), 1)
                for c in range(CHUNKS):
                    i = b * CHUNKS + c
                    act.wait_ge(sem("var_done"), i + 1)
                    if i >= 2:
                        act.wait_ge(sem("inverted"), i - 1)
                    act.activation(std[:, i % 2, 0:ntok(c)], A.at(("var", b, c))[:, 0:ntok(c)], ACT.Sqrt,
                                   bias=eps_ln[:, 0:1]).then_inc(sem("std_done"), 1)
                    if b == L1A:
                        act.wait_ge(sem("rms_arg"), c + 1)
                        act.activation(std[:, i % 2, 0:ntok(c)], rstd[:, i % 2, 0:ntok(c)], ACT.Sqrt,
                                       bias=eps_rms[:, 0:1]).then_inc(sem("rms_done"), 1)

            def copy(dst, src, signal):
                act.activation(dst, src, ACT.Copy).then_inc(sem(signal), 1)

            def router_act(r):
                if r == 0:
                    act.wait_ge(sem("top_shift"), 1)
                    act.activation(gcol[:, 3], gcol[:, 2], ACT.Exp).then_inc(sem("top_exp"), 1)
                if r == 1:
                    act.wait_ge(sem("router_shift"), 1)
                    act.activation(gate[:, 0], gate[:, 0], ACT.Exp).then_inc(sem("router_exp"), 1)
                for j in range(CHUNKS):
                    n = min(4 * P, TOKENS - 4 * P * j)
                    act.wait_ge(sem("gateT_done"), r * CHUNKS + j + 1)
                    copy(gT[:, 4 * P * j:4 * P * j + n], A.at(("gateT", r, j))[0:EXPERTS, 0:n], "gateT_kept")

            act.wait_ge(sem("l0_loaded"), 9 * 16)
            act.activation(a_neg[:], alog[:], ACT.Exp)
            act.activation(a_t[DT_RANK:DT_RANK + N_STATE, 1, :], a_t[DT_RANK:DT_RANK + N_STATE, 0, :],
                           ACT.Exp).then_inc(sem("a_exp"), 1)
            act.wait_ge(sem("prim_shift"), 1)
            act.activation(pcol[:, :, 2], pcol[:, :, 1], ACT.Exp).then_inc(sem("prim_e"), 1)
            act.wait_ge(sem("gate_loaded"), 8 * 16)
            act.wait_ge(sem("consts"), 1)
            act.activation(sgn3[:, 0], sig3[:], ACT.Sign).then_inc(sem("signs"), 1)
            ln(L0A)
            act.wait_ge(sem("prim_w"), 1)
            copy(wexp[:], A.at(("prim_w",))[:, 0:2 * PRIM_TILES].rearrange("p (f n) -> p f n", f=2), "prim_w_kept")
            for c in range(CHUNKS):
                for m in range(HALVES):
                    act.wait_ge(sem("z_done"), 2 * c + m + 1)
                    act.activation(zs[:, m, chunk(c)], A.at(("z", c, m))[:, 0:ntok(c)], ACT.Silu).then_inc(sem("z_silu"), 1)
                act.wait_ge(sem("par_done"), c + 1)
                copy(pc[0:DT_RANK + N_STATE, chunk(c)], A.at(("par", c))[0:DT_RANK + N_STATE, 0:ntok(c)], "par_kept")
                for m in range(HALVES):
                    act.wait_ge(sem("conv0"), 2 * c + m + 1)
                    act.activation(u0[:, m, chunk(c)], xcv0[:, m, 0:ntok(c)], ACT.Silu).then_inc(sem("u0_done"), 1)
            for c in range(CHUNKS):
                for m in range(HALVES):
                    g, n = 2 * c + m, ntok(c)
                    v = A.at(("dt", c, m))[:, 0:n]
                    act.wait_ge(sem("dt_done"), g + 1)
                    if g >= 2:
                        act.wait_ge(sem("dt_ready"), g - 1)
                    link(act.activation(sp_a[:, g % 2, 0:n], v, ACT.Abs, bias=dtb[:, m:m + 1]))
                    act.activation(sp_r[:, g % 2, 0:n], v, ACT.Relu, bias=dtb[:, m:m + 1]).then_inc(sem("dt_relu"), 1)
                    link(act.activation(sp_a[:, g % 2, 0:n], sp_a[:, g % 2, 0:n], ACT.Exp, scale=-1.0))
                    act.activation(sp_a[:, g % 2, 0:n], sp_a[:, g % 2, 0:n], ACT.Ln, bias=1.0).then_inc(sem("dt_ln"), 1)
            act.wait_ge(sem("a_ready"), 1)
            act.wait_ge(sem("edges"), 1)
            for k in range(CHUNKS * N_STATE):
                c, n = divmod(k, N_STATE)
                nb, b0 = CHUNK_BATCHES[c], CHUNK_B0[c]
                for m in range(HALVES):
                    g = 2 * k + m
                    if n == 0:
                        act.wait_ge(sem("dt_ready"), 2 * c + m + 1)
                    if g >= 2:
                        act.wait_ge(sem("scanned"), g - 1)
                    dst = a_buf[:, g % 2, 0:nb * (SEQ + 1)].rearrange("p (b t) -> p b t", t=SEQ + 1)[:, :, 1:SEQ + 1]
                    act.activation(dst, seqs(dtx[:, m, chunk(c)]), ACT.Exp, scale=a_neg[:, m, n:n + 1]).then_inc(
                        sem("decay"), 1)
            ln(L0F)
            router_act(0)
            for q in range(NQ):
                c = q % CHUNKS
                for j in range(HT):
                    i = HT * q + j
                    act.wait_ge(sem("e1_done"), i + 1)
                    if i >= 2:
                        act.wait_ge(sem("hidden"), i - 1)
                    act.activation(sa[:, i % 2, 0:ntok(c)], A.at(("e1", q, j))[:, 0:ntok(c)], ACT.Silu).then_inc(
                        sem("e1_silu"), 1)
            ln(L1A)
            for c in range(CHUNKS):
                for j in range(4):
                    src = A.at(("in1", c, j))[:, 0:ntok(c)]
                    act.wait_ge(sem("in1_done"), 4 * c + j + 1)
                    if j < 2:
                        if c >= 2:
                            act.wait_ge(sem("conv1"), 2 * (c - 2) + j + 1)
                        act.activation(up[:, c % 2, j, 0:ntok(c)], src, ACT.Identity, bias=inb1[:, j:j + 1]).then_inc(
                            sem("in1_u"), 1)
                    else:
                        act.activation(gs[:, j - 2, chunk(c)], src, ACT.Silu, bias=inb1[:, j:j + 1]).then_inc(
                            sem("in1_gate"), 1)
                for m in range(HALVES):
                    act.wait_ge(sem("conv1"), 2 * c + m + 1)
                    act.activation(u1[:, m, chunk(c)], xcv1[:, c % 2, m, 0:ntok(c)], ACT.Silu).then_inc(sem("u1_done"), 1)
            for c in range(CHUNKS):
                for j in range(6):
                    act.wait_ge(sem("par1_done"), 6 * c + j + 1)
                    if c >= 2 and j == 0:
                        act.wait_ge(sem("y1_gated"), 2 * (c - 1))
                    act.activation(abc[:, c % 2, j, 0:ntok(c)], A.at(("par1", c, j))[:, 0:ntok(c)],
                                   ACT.Tanh if j // 2 == 1 else ACT.Sigmoid, bias=pb1[:, j:j + 1]).then_inc(
                        sem("abc_done"), 1)
            for f in range(2):
                act.wait_ge(sem("tile_used"), (f + 1) * PRIM_TILES)
                for j in range(4):
                    src = A.at(("comp", f, j))
                    if f == 0:
                        copy(w1c[:, j // 2, (j % 2) * 512:(j % 2 + 1) * 512], src, "composed")
                    else:
                        copy(w2c[:, 2 * j:2 * j + 2, :], src.rearrange("p (k n) -> p k n", k=2), "composed")
            ln(L1F)
            for c in range(CHUNKS):
                for j in range(HT):
                    act.wait_ge(sem("f1_done"), HT * c + j + 1)
                    if c >= 2 and j == 0:
                        wait_h(act, L2A, c - 2)
                    act.activation(hm1[:, c % 2, j, 0:ntok(c)], A.at(("f1", c, j))[:, 0:ntok(c)],
                                   ACT.Gelu_apprx_tanh).then_inc(sem("f1_gelu"), 1)
            ln(L2A)
            for c in range(CHUNKS):
                for j in range(4):
                    act.wait_ge(sem("qk_done"), 4 * c + j + 1)
                    copy(qk[:, j, chunk(c)], A.at(("qk", c, j))[:, 0:ntok(c)], "qk_kept")
                for j in range(VP[c]):
                    n = min(2, CHUNK_BATCHES[c] - 2 * j)
                    b = CHUNK_B0[c] + 2 * j
                    act.wait_ge(sem("v2_done"), V0[c] + j + 1)
                    copy(vb[0:SEQ, b:b + n, :], A.at(("v2", c, j))[0:SEQ, 0:n * D].rearrange("p (b n) -> p b n", n=D),
                         "v2_kept")
            for c in range(CHUNKS):
                act.wait_ge(sem("s2_shifted"), c + 1)
                act.activation(pr[0:SEQ, c, 0:ntok(c)], pr[0:SEQ, c, 0:ntok(c)], ACT.Exp).then_inc(sem("s2_exp"), 1)
            for c in range(CHUNKS):
                act.wait_ge(sem("pT2_done"), c + 1)
                if c >= 2:
                    act.wait_ge(sem("o2_done"), 2 * (c - 1))
                copy(pT[0:SEQ, c % 2, 0:ntok(c)], A.at(("pT2", c))[0:SEQ, 0:ntok(c)], "pT2_kept")
                for m in range(HALVES):
                    act.wait_ge(sem("o2_done"), 2 * c + m + 1)
                    if c >= 2:
                        wait_h(act, L2F, c - 2)
                    copy(oT[:, c % 2, m, 0:ntok(c)], A.at(("o2", c, m))[:, 0:ntok(c)], "o2_kept")
            ln(L2F)
            router_act(1)
            ln(L3A)
            act.wait_ge(sem("kblk_clear"), 1)
            for c in range(CHUNKS):
                act.wait_ge(sem("k3_done"), c + 1)
                src = A.at(("k3", c))
                for g in range(KV_HEADS):
                    rows = slice(g * HPAD, (g + 1) * HPAD)
                    ins = act.activation(kblk[rows, CHUNK_B0[c]:CHUNK_B0[c] + CHUNK_BATCHES[c], g, :],
                                         seqs(src[rows, 0:ntok(c)]), ACT.Copy)
                ins.then_inc(sem("k3_kept"), 1)
                for j in range(V3[c]):
                    n = min(4, CHUNK_BATCHES[c] - 4 * j)
                    b = CHUNK_B0[c] + 4 * j
                    act.wait_ge(sem("v3_done"), V30[c] + j + 1)
                    copy(vb3[0:SEQ, b:b + n, :], A.at(("v3", c, j))[0:SEQ, 0:n * P].rearrange("p (b n) -> p b n", n=P),
                         "v3_kept")

            def keep_q3(c):
                for j in range(GROUP):
                    act.wait_ge(sem("q3_done"), GROUP * c + j + 1)
                    if c >= 2 and j == 0:
                        act.wait_ge(sem("s3_done"), GROUP * CHUNK_B0[c - 1])
                    copy(q3[:, c % 2, j, 0:ntok(c)], A.at(("q3", c, j))[:, 0:ntok(c)], "q3_kept")

            def exp3(b):
                act.wait_ge(sem("s3_shifted"), GROUP * (b + 1))
                v = p3[0:SEQ, b % 2]
                act.activation(v, v, ACT.Exp, scale=float(HEAD) ** -0.5).then_inc(sem("s3_exp"), 1)

            keep_q3(0)
            exp3(0)
            for b in range(BATCH):
                c = chunk_of[b]
                if b == CHUNK_B0[c] and c + 1 < CHUNKS:
                    keep_q3(c + 1)
                for g in range(KV_HEADS):
                    act.wait_ge(sem("pT3_done"), KV_HEADS * b + g + 1)
                    if b:
                        act.wait_ge(sem("o3_done"), b)
                    copy(pT3[0:SEQ, g, :], A.at(("pT3", b, g))[0:SEQ, 0:GROUP * SEQ], "pT3_kept")
                if b + 1 < BATCH:
                    exp3(b + 1)
                act.wait_ge(sem("o3_done"), b + 1)
                i = b - CHUNK_B0[c]
                if i == 0 and c >= 1:
                    wait_h(act, L3F, c - 1)
                copy(oT3[:, :, i * SEQ:(i + 1) * SEQ],
                     B.at(("o3", b))[:, 0:GROUP * SEQ].rearrange("p (j t) -> p j t", j=GROUP), "o3_kept")
            ln(L3F)
            router_act(2)

        @block.vector
        def _(dve):
            count = [0]

            def link(ins):
                count[0] += 1
                ins.then_inc(sem("dve_chain"), 1)
                dve.wait_ge(sem("dve_chain"), count[0])

            def ln(b):
                for c in range(CHUNKS):
                    i = b * CHUNKS + c
                    dve.wait_ge(sem("mean_done"), i + 1)
                    dve.tensor_tensor(xn[:, :, chunk(c)], h[:, :, chunk(c)],
                                      both(A.at(("mean", b, c))[:, 0:ntok(c)], ntok(c)), ALU.subtract).then_inc(
                        sem("centred"), 1)
                for c in range(CHUNKS):
                    i, n = b * CHUNKS + c, ntok(c)
                    r = rstd[:, i % 2, 0:n]
                    dve.wait_ge(sem("std_done"), i + 1)
                    dve.reciprocal(r, std[:, i % 2, 0:n]).then_inc(sem("inverted"), 1)
                    dve.wait_ge(sem("inverted"), i + 1)
                    dve.wait_ge(sem("squared"), i + 1)
                    dve.tensor_tensor(xn[:, :, chunk(c)], xn[:, :, chunk(c)], both(r, n), ALU.mult).then_inc(
                        sem("normed"), 1)
                    if b == L1A:
                        dve.wait_ge(sem("normed"), i + 1)
                        link(dve.tensor_tensor(r, r, r, ALU.mult))
                        dve.tensor_tensor(r, r, A.at(("var", b, c))[:, 0:n], ALU.mult).then_inc(sem("rms_arg"), 1)
                        dve.wait_ge(sem("rms_done"), c + 1)
                        link(dve.reciprocal(r, std[:, i % 2, 0:n]))
                        for m in range(HALVES):
                            dve.scalar_tensor_tensor(xr[:, m, chunk(c)], xn[:, m, chunk(c)], nw1[:, m:m + 1], r,
                                                     ALU.mult, ALU.mult).then_inc(sem("rms_normed"), 1)

            to_h = [0]

            def add_h(block, key, c, ring=A, signal="to_h", bias=None):
                for m in range(HALVES):
                    to_h[0] += 1
                    dve.wait_ge(sem(signal), to_h[0])
                    dst, src = h[:, m, chunk(c)], ring.at((key, c, m))[:, 0:ntok(c)]
                    if bias is None:
                        ins = dve.tensor_tensor(dst, dst, src, ALU.add)
                    else:
                        ins = dve.scalar_tensor_tensor(dst, src, bias[:, m:m + 1], dst, ALU.add, ALU.add)
                    ins.then_inc(h_ready, 1)

            def conv(dst, src, taps, bias, signal):
                if bias is None:
                    link(dve.tensor_scalar(dst, src, taps[:, CONV - 1:CONV], None, ALU.mult))
                else:
                    link(dve.tensor_scalar(dst, src, taps[:, CONV - 1:CONV], bias, ALU.mult, ALU.add))
                d, s = seqs(dst), seqs(src)
                for k in range(1, CONV):
                    ins = dve.scalar_tensor_tensor(d[:, :, k:SEQ], s[:, :, 0:SEQ - k], taps[:, CONV - 1 - k:CONV - k],
                                                   d[:, :, k:SEQ], ALU.mult, ALU.add)
                    if k < CONV - 1:
                        link(ins)
                ins.then_inc(sem(signal), 1)

            def top1(src, dst, tmp, col):
                bc = lambda a: a.unsqueeze(2).to_broadcast([P, TILES, EXPERTS])
                link(dve.tensor_reduce(gcol[:, col], src, AX_X, ALU.max))
                link(dve.tensor_tensor(tmp, src, bc(gcol[:, col]), ALU.is_equal))
                link(dve.tensor_tensor(tmp, tmp, first[:].unsqueeze(1).to_broadcast([P, TILES, EXPERTS]), ALU.mult))
                link(dve.tensor_reduce(gcol[:, 7], tmp, AX_X, ALU.max))
                link(dve.tensor_tensor(dst, tmp, bc(gcol[:, 7]), ALU.is_equal))

            def router(r):
                bc = lambda a: a.unsqueeze(2).to_broadcast([P, TILES, EXPERTS])
                x, tmp, oh1, oh2, rest, res = (gate[:, i] for i in range(6))
                dve.wait_ge(sem("logits_done"), r + 1)
                if r == 0:
                    dve.wait_ge(sem("gate_loaded"), 8 * 16)
                src = A.at(("logits", r))[:, 0:TILES * EXPERTS].rearrange("p (i e) -> p i e", e=EXPERTS)
                if r < 2:
                    bias = (bg0, bg2)[r][:].unsqueeze(1).to_broadcast([P, TILES, EXPERTS])
                    ins = dve.tensor_tensor(x, src, bias, ALU.add)
                else:
                    ins = dve.tensor_copy(x, src)
                ins.then_inc(sem("logits_used"), 1)
                dve.wait_ge(sem("logits_used"), r + 1)
                if r == 1:
                    link(dve.tensor_reduce(gcol[:, 2], x, AX_X, ALU.max))
                    dve.tensor_tensor(x, x, bc(gcol[:, 2]), ALU.subtract).then_inc(sem("router_shift"), 1)
                    dve.wait_ge(sem("router_exp"), 1)
                    link(dve.tensor_reduce(gcol[:, 2], x, AX_X, ALU.add))
                    link(dve.reciprocal(gcol[:, 3], gcol[:, 2]))
                    link(dve.tensor_tensor(x, x, bc(gcol[:, 3]), ALU.mult))
                if r == 2:
                    top1(x, oh1, tmp, 0)
                    dve.tensor_copy(res, oh1).then_inc(sem("gates"), 1)
                    return
                top1(x, oh1, tmp, 0)
                link(dve.tensor_scalar(rest, oh1, -3.0e38, None, ALU.mult))
                link(dve.tensor_tensor(rest, rest, x, ALU.add))
                top1(rest, oh2, tmp, 1)
                if r == 0:
                    dve.tensor_tensor(gcol[:, 2], gcol[:, 1], gcol[:, 0], ALU.subtract).then_inc(sem("top_shift"), 1)
                    dve.wait_ge(sem("top_exp"), 1)
                    link(dve.tensor_scalar(gcol[:, 4], gcol[:, 3], 1.0, None, ALU.add))
                    link(dve.reciprocal(gcol[:, 5], gcol[:, 4]))
                    link(dve.tensor_tensor(gcol[:, 6], gcol[:, 3], gcol[:, 5], ALU.mult))
                else:
                    link(dve.tensor_tensor(gcol[:, 2], gcol[:, 0], gcol[:, 1], ALU.add))
                    link(dve.reciprocal(gcol[:, 3], gcol[:, 2]))
                    link(dve.tensor_tensor(gcol[:, 5], gcol[:, 0], gcol[:, 3], ALU.mult))
                    link(dve.tensor_tensor(gcol[:, 6], gcol[:, 1], gcol[:, 3], ALU.mult))
                link(dve.tensor_tensor(oh1, oh1, bc(gcol[:, 5]), ALU.mult))
                link(dve.tensor_tensor(oh2, oh2, bc(gcol[:, 6]), ALU.mult))
                dve.tensor_tensor(res, oh1, oh2, ALU.add).then_inc(sem("gates"), 1)

            def gate_x(r, q, buf):
                c = q % CHUNKS if r == 0 else q // EXPERTS
                dve.wait_ge(sem("gate_spread"), 40 * r + q + 1)
                if r == 0 and q >= 2:
                    dve.wait_ge(sem("e3_done"), HT * (q - 1))
                if r > 0 and q >= 2:
                    c2, e2 = divmod(q - 2, EXPERTS)
                    if e2 == EXPERTS - 1:
                        dve.wait_ge(sem("dense_out"), HALVES * ((r - 1) * CHUNKS + c2 + 1))
                    else:
                        dve.wait_ge(sem("dense_used"), (EXPERTS - 1) * ((r - 1) * CHUNKS + c2) + e2 + 1)
                dve.tensor_tensor(buf[:, q % 2, :, 0:ntok(c)], xn[:, :, chunk(c)],
                                  both(A.at(("gb", r, q))[:, 0:ntok(c)], ntok(c)), ALU.mult).then_inc(sem("x_gated"), 1)

            def dense(r, blk):
                gate_x(r, 0, xs2)
                for q in range(NQ):
                    if q + 1 < NQ:
                        gate_x(r, q + 1, xs2)
                    c, e = divmod(q, EXPERTS)
                    if e == EXPERTS - 1:
                        for m in range(HALVES):
                            dve.wait_ge(sem("dense_out"), HALVES * ((r - 1) * CHUNKS + c) + m + 1)
                            dve.tensor_tensor(h[:, m, chunk(c)], h[:, m, chunk(c)], B.at(("dy", r, c, m))[:, 0:ntok(c)],
                                              ALU.add).then_inc(h_ready, 1)

            dve.memset(mean_w[:], 1.0 / D)
            dve.memset(ones[:], 1.0)
            dve.memset(eps_ln[:], EPS_LN)
            dve.memset(eps_rms[:], EPS_RMS).then_inc(sem("dve_consts"), 1)
            dve.wait_ge(sem("a_exp"), 1)
            rows = slice(DT_RANK, DT_RANK + N_STATE)
            link(dve.tensor_scalar(a_guard[:], a_neg[:], 1e-5, None, ALU.is_lt))
            dve.tensor_reduce(guarded[:], a_guard[:].rearrange("p m n -> p (m n)"), AX_X, ALU.max).then_inc(
                sem("guards_listed"), 1)
            link(dve.tensor_scalar(a_keep[:], a_guard[:], -1.0, 1.0, ALU.mult, ALU.add))
            link(dve.tensor_scalar(a_neg[:], a_neg[:], -1.0, None, ALU.mult))
            link(dve.tensor_scalar(w_f[:], a_neg[:], 1e-10, None, ALU.add))
            link(dve.tensor_tensor(w_f[:], w_f[:], a_keep[:], ALU.mult))
            link(dve.tensor_tensor(w_f[:], w_f[:], a_guard[:], ALU.add))
            link(dve.reciprocal(w_f[:], w_f[:]))
            at, gt, kt = a_t[rows, 1, :], a_t[rows, 2, :], a_t[rows, 3, :]
            link(dve.tensor_scalar(gt, at, 1e-5, None, ALU.is_lt))
            link(dve.tensor_scalar(at, at, -1.0, 1e-10, ALU.mult, ALU.add))
            link(dve.tensor_scalar(kt, gt, -1.0, 1.0, ALU.mult, ALU.add))
            link(dve.tensor_tensor(at, at, kt, ALU.mult))
            link(dve.tensor_tensor(at, at, gt, ALU.add))
            link(dve.reciprocal(at, at))
            dve.tensor_tensor(kt, at, kt, ALU.mult).then_inc(sem("a_ready"), 1)
            dve.wait_ge(sem("prim_loaded"), 7 * 16)
            for f in range(2):
                lcol = pcol[:, f, 0:1]
                link(dve.tensor_scalar(ptmp[:, f], prow[:, f], lcol, None, ALU.is_equal))
                link(dve.tensor_tensor(ptmp[:, f], ptmp[:, f], lower[:], ALU.mult))
                link(dve.tensor_scalar(ptmp2[:, f], prow[:, f], lcol, None, ALU.is_gt))
                link(dve.tensor_tensor(ptmp[:, f], ptmp[:, f], ptmp2[:, f], ALU.add))
                link(dve.tensor_reduce(pcol[:, f, 4:5], ptmp[:, f], AX_X, ALU.add))
                link(dve.tensor_scalar(pcol[:, f, 5:6], pcol[:, f, 4:5], float(TOP_PRIMS), None, ALU.is_lt))
                link(dve.tensor_reduce(pcol[:, f, 6:7], prow[:, f], AX_X, ALU.max))
                link(dve.tensor_tensor(pcol[:, f, 1:2], pcol[:, f, 0:1], pcol[:, f, 6:7], ALU.subtract))
            dve.tensor_copy(pcol[:, :, 7], pcol[:, :, 1]).then_inc(sem("prim_shift"), 1)
            dve.wait_ge(sem("prim_e"), 1)
            dve.tensor_tensor(pcol[:, :, 3], pcol[:, :, 2], pcol[:, :, 5], ALU.mult).then_inc(sem("prim_exp"), 1)
            for c in range(CHUNKS):
                nb, b0 = CHUNK_BATCHES[c], CHUNK_B0[c]
                for m in range(HALVES):
                    dve.wait_ge(sem("tok_done"), 2 * c + m + 1)
                    dve.tensor_scalar(seqs(h[:, m, chunk(c)])[:, :, 0:N_IMG],
                                      A.at(("tok", c, m))[:, 0:nb * N_IMG].rearrange("p (b t) -> p b t", t=N_IMG),
                                      tokb[:, m:m + 1], None, ALU.add).then_inc(h_ready, 1)
            ln(L0A)
            dve.wait_ge(sem("guards_counted"), 1)
            dve.tensor_copy(any_guard[:], A.at(("guards",))[0:1, 0:1]).then_inc(sem("guards_kept"), 1)
            dve.wait_ge(sem("prim_sum"), 1)
            dve.reciprocal(pcol[:, :, 4], A.at(("prim_sum",))[0:PRIMS, 0:2]).then_inc(sem("prim_sum_used"), 1)
            dve.wait_ge(sem("prim_sum_used"), 1)
            link(dve.tensor_tensor(pcol[:, :, 7], pcol[:, :, 3], pcol[:, :, 4], ALU.mult))
            ptv = ptmp[:, 0, :].rearrange("p (f n) -> p f n", f=2)
            for f in range(2):
                ins = dve.tensor_scalar(ptv[:, f], pair[:], pcol[:, f, 7:8], None, ALU.mult)
            ins.then_inc(sem("prim_spread"), 1)
            for c in range(CHUNKS):
                for m in range(HALVES):
                    if c >= 1:
                        dve.wait_ge(sem("u0_done"), 2 * (c - 1) + m + 1)
                    conv(xcv0[:, m, 0:ntok(c)], xn[:, m, chunk(c)], conv0[:, m], None, "conv0")
            for c in range(CHUNKS):
                for m in range(HALVES):
                    g, n = 2 * c + m, ntok(c)
                    dve.wait_ge(sem("dt_ln"), g + 1)
                    r, l = seqs(sp_r[:, g % 2, 0:n]), seqs(sp_a[:, g % 2, 0:n])
                    d = seqs(dtx[:, m, chunk(c)])
                    dve.tensor_tensor(d[:, :, 1:SEQ], r[:, :, 0:SEQ - 1], l[:, :, 0:SEQ - 1], ALU.add)
                    dve.tensor_tensor(d[:, :, 0:1], r[:, :, 0:1], l[:, :, 0:1], ALU.add).then_inc(sem("dt_ready"), 1)

            def scan(g, general):
                k, m = divmod(g, 2)
                c, n = divmod(k, N_STATE)
                seq = slice(CHUNK_B0[c], CHUNK_B0[c] + CHUNK_BATCHES[c])
                N = CHUNK_BATCHES[c] * (SEQ + 1)
                added = d1[:, m, seq, :].rearrange("p b t -> p (b t)")
                dve.wait_ge(sem("steps_ready"), 2 * c + m + 1)
                if general:
                    sel = d_sel[:, g % 2, 0:N]
                    s3 = sel.rearrange("p (b t) -> p b t", t=SEQ + 1)
                    d, u = seqs(dtx[:, m, chunk(c)]), seqs(u0[:, m, chunk(c)])
                    guard, keep = a_guard[:, m, n:n + 1], a_keep[:, m, n:n + 1]
                    if g == 0:
                        dve.wait_ge(sem("dt_ready"), 2 * CHUNKS)
                    if g >= 2:
                        dve.wait_ge(sem("scanned"), g - 1)
                    general_link(dve.memset(sel, 0.0))
                    general_link(dve.scalar_tensor_tensor(s3[:, :, 1:2], d[:, :, 0:1], guard, u[:, :, 0:1],
                                                          ALU.mult, ALU.mult))
                    general_link(dve.scalar_tensor_tensor(s3[:, :, 2:SEQ + 1], d[:, :, 1:SEQ], guard,
                                                          u[:, :, 0:SEQ - 1], ALU.mult, ALU.mult))
                    general_link(dve.scalar_tensor_tensor(sel, added, keep, sel, ALU.mult, ALU.add))
                    added = sel
                dve.wait_ge(sem("decay"), g + 1)
                if g >= 2:
                    dve.wait_ge(sem("y_part"), g - 1)
                dve.tensor_tensor_scan(f_buf[:, g % 2, 0:N], a_buf[:, g % 2, 0:N], added, 0.0,
                                       ALU.mult, ALU.add).then_inc(sem("scanned"), 1)

            NG = 2 * CHUNKS * N_STATE

            def scans(general):
                scan(0, general)
                for g in range(NG):
                    k, m = divmod(g, 2)
                    c, n = divmod(k, N_STATE)
                    if g + 1 < NG:
                        scan(g + 1, general)
                    dve.wait_ge(sem("scanned"), g + 1)
                    dve.wait_ge(sem("c_spread"), k + 1)
                    if g >= 2:
                        dve.wait_ge(sem("y_added"), g - 1)
                    f = f_buf[:, g % 2, 0:CHUNK_BATCHES[c] * (SEQ + 1)].rearrange("p (b t) -> p b t", t=SEQ + 1)
                    dve.scalar_tensor_tensor(seqs(ym[:, g % 2, 0:ntok(c)]), f[:, :, 1:SEQ + 1], w_f[:, m, n:n + 1],
                                             seqs(A.at(("cb", k))[:, 0:ntok(c)]), ALU.mult, ALU.mult).then_inc(
                        sem("y_part"), 1)
                    if n < N_STATE - 1 or m == 0:
                        continue
                    for mm in range(HALVES):
                        N = ntok(c)
                        dve.wait_ge(sem("cw_done"), 2 * c + mm + 1)
                        dve.wait_ge(sem("y_added"), 2 * (c * N_STATE + N_STATE - 1) + mm + 1)
                        y = ytmp[:, mm, 0:N]
                        scan_link(dve.scalar_tensor_tensor(y, A.at(("w2c", c, mm))[:, 0:N], skip0[:, mm:mm + 1],
                                                           u0[:, mm, chunk(c)], ALU.subtract, ALU.mult))
                        scan_link(dve.tensor_tensor(y, B.at(("yacc", c, mm))[:, 0:N], y, ALU.subtract))
                        dve.tensor_tensor(zs[:, mm, chunk(c)], y, zs[:, mm, chunk(c)], ALU.mult).then_inc(
                            sem("y_gated"), 1)
                    add_h(L0A, "out0", c)

            steps_seen = [0, 0]

            def general_link(ins):
                steps_seen[0] += 1
                ins.then_inc(sem("general_chain"), 1)
                dve.wait_ge(sem("general_chain"), steps_seen[0])

            def scan_link(ins):
                steps_seen[1] += 1
                ins.then_inc(sem("scan_chain"), 1)
                dve.wait_ge(sem("scan_chain"), steps_seen[1])

            dve.wait_ge(sem("guards_kept"), 1)
            flag = dve.value_load(any_guard[0:1, 0:1], min_val=0, max_val=P)
            before = to_h[0]
            with dve.If(flag > 0):
                scans(True)
            to_h[0], steps_seen[1] = before, 0
            with dve.Else():
                scans(False)
            ln(L0F)
            router(0)
            gate_x(0, 0, xs)

            def add_expert(q):
                e, c = divmod(q, CHUNKS)
                if e == 0:
                    dve.wait_ge(sem("h_plus_x"), c + 1)
                for m in range(HALVES):
                    dve.wait_ge(sem("expert_out"), 2 * q + m + 1)
                    if e:
                        dve.wait_ge(sem("h_expert"), 2 * (q - CHUNKS) + m + 1)
                    dve.tensor_tensor(h[:, m, chunk(c)], h[:, m, chunk(c)], B.at(("ey", q, m))[:, 0:ntok(c)],
                                      ALU.add).then_inc(h_ready if e == EXPERTS - 1 else sem("h_expert"), 1)

            for q in range(NQ + 1):
                if q + 1 < NQ:
                    gate_x(0, q + 1, xs)
                if q < NQ:
                    c = q % CHUNKS
                    if q >= 2:
                        dve.wait_ge(sem("expert_out"), 2 * (q - 1))
                    for j in range(HT):
                        i = HT * q + j
                        dve.wait_ge(sem("e1_silu"), i + 1)
                        dve.wait_ge(sem("e3_done"), i + 1)
                        dve.tensor_tensor(hm[:, q % 2, j, 0:ntok(c)], sa[:, i % 2, 0:ntok(c)],
                                          A.at(("e3", q, j))[:, 0:ntok(c)], ALU.mult).then_inc(sem("hidden"), 1)
                if q:
                    add_expert(q - 1)
            ln(L1A)
            for c in range(CHUNKS):
                for m in range(HALVES):
                    dve.wait_ge(sem("in1_u"), 2 * c + m + 1)
                    if c >= 2:
                        dve.wait_ge(sem("u1_done"), 2 * (c - 2) + m + 1)
                    conv(xcv1[:, c % 2, m, 0:ntok(c)], up[:, c % 2, m, 0:ntok(c)], cw1[:, m * CONV:(m + 1) * CONV],
                         cb1[:, m:m + 1], "conv1")
            for c in range(CHUNKS):
                N = ntok(c)
                for m in range(HALVES):
                    a, b, cc = (abc[:, c % 2, 2 * i + m, 0:N] for i in range(3))
                    u, g = u1[:, m, chunk(c)], gs[:, m, chunk(c)]
                    dve.wait_ge(sem("abc_done"), 6 * c + 4 + m + 1)
                    dve.wait_ge(sem("u1_done"), 2 * c + m + 1)
                    dve.wait_ge(sem("in1_gate"), 2 * c + m + 1)
                    dve.memset(seqs(a)[:, :, 0:1], 0.0)
                    link(dve.tensor_tensor(b, b, u, ALU.mult))
                    link(dve.tensor_tensor_scan(a, a, b, 0.0, ALU.mult, ALU.add))
                    link(dve.tensor_tensor(cc, cc, a, ALU.mult))
                    link(dve.scalar_tensor_tensor(cc, u, sk1[:, m:m + 1], cc, ALU.mult, ALU.add))
                    dve.tensor_tensor(g, cc, g, ALU.mult).then_inc(sem("y1_gated"), 1)
                if c >= 1:
                    dve.wait_ge(sem("h_plus_x"), CHUNKS + c)
                    add_h(L1A, "out1", c - 1, bias=ob1)
            dve.wait_ge(sem("h_plus_x"), 2 * CHUNKS)
            add_h(L1A, "out1", CHUNKS - 1, bias=ob1)
            ln(L1F)
            for c in range(CHUNKS):
                add_h(L1F, "f2", c, B)
            ln(L2A)
            for c in range(CHUNKS):
                nb, N = CHUNK_BATCHES[c], ntok(c)
                s = seqs(pr[0:SEQ, c, 0:N])
                bc = lambda a: a.unsqueeze(2).to_broadcast([SEQ, nb, SEQ])
                mx = st[0:SEQ, c, 0, 0:nb]
                dve.wait_ge(sem("s2_done"), c + 1)
                dve.scalar_tensor_tensor(s, seqs(A.at(("s2", c))[0:SEQ, 0:N]), float(D) ** -0.5,
                                         causal[:].unsqueeze(1).to_broadcast([SEQ, nb, SEQ]), ALU.mult,
                                         ALU.add).then_inc(sem("s2_scaled"), 1)
                dve.wait_ge(sem("s2_scaled"), c + 1)
                link(dve.tensor_reduce(mx, s, AX_X, ALU.max))
                dve.tensor_tensor(s, s, bc(mx), ALU.subtract).then_inc(sem("s2_shifted"), 1)
            for c in range(CHUNKS):
                nb, N = CHUNK_BATCHES[c], ntok(c)
                s = seqs(pr[0:SEQ, c, 0:N])
                bc = lambda a: a.unsqueeze(2).to_broadcast([SEQ, nb, SEQ])
                total, inv = st[0:SEQ, c, 1, 0:nb], st[0:SEQ, c, 2, 0:nb]
                dve.wait_ge(sem("s2_exp"), c + 1)
                link(dve.tensor_reduce(total, s, AX_X, ALU.add))
                link(dve.reciprocal(inv, total))
                dve.tensor_tensor(s, s, bc(inv), ALU.mult).then_inc(sem("p2_ready"), 1)
            for c in range(CHUNKS):
                add_h(L2A, "out2", c)
            ln(L2F)
            router(1)
            dense(1, L2F)
            ln(L3A)

            def shift3(b):
                if b >= 2:
                    dve.wait_ge(sem("pT3_done"), KV_HEADS * (b - 1))
                for j in range(GROUP):
                    dve.wait_ge(sem("s3_done"), GROUP * b + j + 1)
                    s = A.at(("s3", b, j))[0:SEQ, 0:KV_HEADS * SEQ].rearrange("p (g s) -> p g s", g=KV_HEADS)
                    mx = st3[0:SEQ, b % 2, 0, j * KV_HEADS:(j + 1) * KV_HEADS]
                    link(dve.tensor_reduce(mx, s, AX_X, ALU.max))
                    dve.tensor_tensor(p3[0:SEQ, b % 2, j], s, mx.unsqueeze(2).to_broadcast([SEQ, KV_HEADS, SEQ]),
                                      ALU.subtract).then_inc(sem("s3_shifted"), 1)

            shift3(0)
            for b in range(BATCH):
                if b in CHUNK_B0 and b:
                    add_h(L3A, "out3", CHUNK_B0.index(b) - 1)
                if b + 1 < BATCH:
                    shift3(b + 1)
                dve.wait_ge(sem("s3_exp"), b + 1)
                v = p3[0:SEQ, b % 2].rearrange("p j g s -> p (j g) s")
                total, inv = st3[0:SEQ, b % 2, 1, :], st3[0:SEQ, b % 2, 2, :]
                link(dve.tensor_reduce(total, v, AX_X, ALU.add))
                if b >= 2:
                    dve.wait_ge(sem("p3_ready"), b - 1)
                dve.reciprocal(inv, total).then_inc(sem("s3_sum"), 1)
            add_h(L3A, "out3", CHUNKS - 1)
            ln(L3F)
            router(2)
            dense(2, L3F)

        @block.gpsimd
        def _(pool):
            pool.memset(ident[:], 0.0).then_inc(sem("pool_zeros"), 1)
            pool.memset(causal[:], 0.0).then_inc(sem("pool_zeros"), 1)
            pool.wait_ge(sem("pool_zeros"), 2)
            pool.affine_select(out=ident[:], in_=ident[:], compare_op=ALU.not_equal, fill=1.0, base=0,
                               pattern=[[-1, P]], channel_multiplier=1)
            pool.affine_select(out=causal[:], in_=causal[:], compare_op=ALU.is_ge, fill=NEG, base=0,
                               pattern=[[-1, SEQ]], channel_multiplier=1).then_inc(sem("pool_consts"), 1)
            pool.wait_ge(sem("pool_consts"), 1)
            pool.wait_ge(sem("dve_consts"), 1)
            pool.memset(gT[:, 0:1], 0.0).then_inc(sem("consts"), 1)
            pool.wait_ge(sem("txt_loaded"), 16)
            hv = h[:].rearrange("p m (b t) -> p m b t", t=SEQ)
            for m in range(HALVES):
                ins = pool.tensor_copy(hv[:, m, :, N_IMG:SEQ], txt[:, m])
            ins.then_inc(sem("txt_placed"), 1)
            wait_h(pool, 0, CHUNKS - 1)
            pool.wait_ge(sem("txt_placed"), 1)
            for r in range(2):
                pool.memset(a_buf[:, r].rearrange("p (b t) -> p b t", t=SEQ + 1)[:, :, 0:1], 0.0)
            pool.memset(d1[:, :, :, 1:2], 0.0).then_inc(sem("edges"), 1)
            for c in range(CHUNKS):
                for m in range(HALVES):
                    d = d1[:, m, CHUNK_B0[c]:CHUNK_B0[c] + CHUNK_BATCHES[c], :]
                    u = seqs(u0[:, m, chunk(c)])
                    pool.wait_ge(sem("u0_done"), 2 * c + m + 1)
                    pool.tensor_copy(d[:, :, 0:1], u[:, :, 0:1])
                    pool.tensor_tensor(d[:, :, 2:SEQ + 1], u[:, :, 1:SEQ], u[:, :, 0:SEQ - 1], ALU.subtract).then_inc(
                        sem("steps_ready"), 1)

            def add_x(blk):
                for c in range(CHUNKS):
                    pool.wait_ge(sem("normed"), blk * CHUNKS + c + 1)
                    pool.tensor_tensor(h[:, :, chunk(c)], h[:, :, chunk(c)], xn[:, :, chunk(c)], ALU.add).then_inc(
                        sem("h_plus_x"), 1)

            add_x(L0F)
            add_x(L1A)
            for i in range(2 * PRIM_TILES):
                f, kt = divmod(i, PRIM_TILES)
                pool.wait_ge(sem(f"tile{i % PSLOTS}"), 32 * (i // PSLOTS + 1))
                pool.wait_ge(sem("prim_w_kept"), 1)
                v = tile_short[:, i % PSLOTS]
                pool.tensor_scalar(v, v, wexp[:, f, kt:kt + 1], None, ALU.mult).then_inc(sem("tile_scaled"), 1)
            wait_h(pool, L3A, CHUNKS - 1)
            pool.memset(kblk, 0.0).then_inc(sem("kblk_clear"), 1)
            for b in range(BATCH):
                pool.wait_ge(sem("s3_sum"), b + 1)
                v = p3[0:SEQ, b % 2].rearrange("p j g s -> p (j g) s")
                pool.tensor_tensor(v, v, st3[0:SEQ, b % 2, 2, :].unsqueeze(2).to_broadcast([SEQ, GROUP * KV_HEADS, SEQ]),
                                   ALU.mult).then_inc(sem("p3_ready"), 1)


def rows(w):
    k, n = w.shape
    return w.reshape(k // P, P, n).transpose(1, 0, 2)


def halves(v):
    return v.reshape(HALVES, P, *v.shape[1:]).swapaxes(0, 1)


def pad_heads(w, heads):
    out = np.zeros((w.shape[0], heads, HPAD), w.dtype)
    out[:, :, :HEAD] = w.reshape(w.shape[0], heads, HEAD)
    return out


def layouts(i):
    patch = i["x"].reshape(BATCH, 3, 6, 16, 6, 16).transpose(1, 3, 5, 0, 2, 4).reshape(FAN_IN, BATCH * N_IMG)
    wpar = i["L0_attn_W_params"]
    wpar = np.concatenate([wpar[:DT_RANK], wpar[DT_RANK + N_STATE:]], 0).T
    q = pad_heads(i["L3_attn_Wq"].T, KV_HEADS * GROUP).reshape(D, KV_HEADS, GROUP, HPAD).transpose(0, 2, 1, 3)
    o = pad_heads(i["L3_attn_Wo"], KV_HEADS * GROUP).reshape(D, KV_HEADS, GROUP, HPAD).transpose(1, 3, 2, 0)
    vec = [halves(i["L1_attn_norm_w"]), i["L1_attn_in_b"].reshape(4, P).T,
           i["L1_attn_conv_w"].T.reshape(HALVES, P, CONV).transpose(1, 0, 2).reshape(P, -1),
           halves(i["L1_attn_conv_b"]), i["L1_attn_param_b"].reshape(6, P).T, halves(i["L1_attn_skip"]),
           halves(i["L1_attn_out_b"])]
    f32 = np.float32
    idx = np.arange(PRIMS)

    def factors(a, b):
        a = a.transpose(0, 2, 1).reshape(PRIM_TILES, P, -1)
        return a, b.reshape(PRIM_TILES, P, -1)

    a1, b1 = factors(i["L1_ffn_fc1_A"], i["L1_ffn_fc1_B"])
    a2, b2 = factors(i["L1_ffn_fc2_A"], i["L1_ffn_fc2_B"])
    return {
        "xp": rows(patch), "wtok": rows(i["L0_tok_W"].T), "tokb": halves(i["L0_tok_b"]),
        "txt": halves(i["txt"].transpose(2, 0, 1)),
        "wz": rows(i["L0_attn_W_z"].T), "wpar": rows(wpar), "wdt": i["L0_attn_W_dt"].T,
        "wout0": rows(i["L0_attn_W_out"].T), "conv0": halves(i["L0_attn_conv_w"][:, 0]),
        "dtb": halves(i["L0_attn_b_dt"]), "alog": halves(i["L0_attn_A_log"]), "alogT": i["L0_attn_A_log"].T,
        "skip0": halves(i["L0_attn_D"]),
        "lower": (idx[None, :] < idx[:, None]).astype(f32),
        "pair": (idx[:, None] // 2 == np.arange(PRIM_TILES)[None, :]).astype(f32),
        "sel2": (idx[:, None] % 2 == np.arange(P)[None, :] // RANK).astype(f32),
        "fc1_logits_row": i["L1_ffn_fc1_logits"][None], "fc1_logits_col": i["L1_ffn_fc1_logits"][:, None],
        "fc2_logits_row": i["L1_ffn_fc2_logits"][None], "fc2_logits_col": i["L1_ffn_fc2_logits"][:, None],
        "wg0": rows(i["L0_ffn_Wg"]), "wg2": rows(i["L2_ffn_Wg"]), "sig3": rows(i["L3_ffn_tile_sigs"].T),
        "be2": i["L2_ffn_be"], "be3": i["L3_ffn_b"], "bg0": i["L0_ffn_bg"][None], "bg2": i["L2_ffn_bg"][None],
        "first": (EXPERTS - np.arange(EXPERTS)).astype(f32)[None],
        "win1": rows(i["L1_attn_in_w"]), "wp1": rows(i["L1_attn_param_w"]), "wout1": rows(i["L1_attn_out_w"]),
        "vec1": np.concatenate([v.reshape(P, -1) for v in vec], 1),
        "wq2": rows(i["L2_attn_Wq"]), "wk2": rows(i["L2_attn_Wk"]), "wv2": rows(i["L2_attn_Wv"]),
        "wo2": rows(i["L2_attn_Wo"]),
        "wq3": rows(q.reshape(D, -1)).reshape(P, HALVES, GROUP, P),
        "wk3": rows(pad_heads(i["L3_attn_Wk"].T, KV_HEADS).reshape(D, -1)),
        "wv3": rows(pad_heads(i["L3_attn_Wv"].T, KV_HEADS).reshape(D, -1)),
        "wo3": o.reshape(P, GROUP, D),
        "we2": i["L2_ffn_We"].transpose(2, 0, 1).reshape(HALVES, P, EXPERTS, D).transpose(1, 2, 0, 3),
        "we3": i["L3_ffn_W"].transpose(1, 0, 2).reshape(HALVES, P, EXPERTS, D).transpose(1, 2, 0, 3),
        "W1": i["L0_ffn_W1"].reshape(EXPERTS, HALVES, P, HIDDEN).transpose(0, 2, 1, 3),
        "W3": i["L0_ffn_W3"].reshape(EXPERTS, HALVES, P, HIDDEN).transpose(0, 2, 1, 3),
        "W2": i["L0_ffn_W2"].reshape(EXPERTS, HT, P, D).transpose(0, 2, 1, 3),
        "A1": a1, "B1": b1, "A2": a2, "B2": b2,
    }


def kernel(**inputs):
    import concourse.bacc as bacc
    from concourse.bass_utils import run_bass_kernel_spmd

    nc = bacc.Bacc("TRN2", target_bir_lowering=False, num_devices=1)
    arrays, t = {}, {}
    for name, a in layouts({k: np.asarray(v) for k, v in inputs.items()}).items():
        a = np.ascontiguousarray(a)
        arrays[f"in_{name}"] = a
        t[name] = nc.dram_tensor(f"in_{name}", a.shape, F32, kind="ExternalInput").ap()
    out = nc.dram_tensor("out", (P, HALVES, TOKENS), F32, kind="ExternalOutput").ap()
    build(nc, t, out)
    got = run_bass_kernel_spmd(nc, [arrays], core_ids=[0]).results[0]["out"]
    return np.ascontiguousarray(got.swapaxes(0, 1).reshape(D, BATCH, SEQ).transpose(1, 2, 0))
```

```python
from contextlib import ExitStack

import numpy as np

import concourse.bass as bass
from concourse import mybir

ALU = mybir.AluOpType
ACT = mybir.ActivationFunctionType
F32 = mybir.dt.float32
I32 = mybir.dt.int32
AX_X = mybir.AxisListType.X

P = 128
D = 256
HALVES = D // P
BATCH = 32
N_IMG = 36
N_TXT = 32
SEQ = N_IMG + N_TXT
TOKENS = BATCH * SEQ
TILES = TOKENS // P
CHUNK_BATCHES = [7, 7, 6, 6, 6]
CHUNKS = len(CHUNK_BATCHES)
CHUNK_B0 = [sum(CHUNK_BATCHES[:c]) for c in range(CHUNKS)]
NMAX = max(CHUNK_BATCHES) * SEQ
FAN_IN = 768
KT_TOK = FAN_IN // P
N_STATE = 16
DT_RANK = 64
CONV = 4
EXPERTS = 8
HIDDEN = 1024
HT = HIDDEN // P
PRIMS = 64
RANK = 64
TOP_PRIMS = 32
PRIM_TILES = PRIMS * RANK // P
KV_HEADS = 4
GROUP = 4
HEAD = 16
HPAD = 32
SLOTS = 2
BLOCKS = SLOTS * TOKENS // P + EXPERTS
EPS_LN = 1e-5
EPS_RMS = 1e-6
NEG = -1e30

L0A, L0F, L1A, L1F, L2A, L2F, L3A, L3F = range(8)


class Banks:

    def __init__(self, tensor, banks):
        self.tensor, self.banks = tensor, banks
        self.index, self.freed = {}, []

    def plan(self, key, freed_by):
        self.index[key] = len(self.freed)
        self.freed.append(freed_by)

    def at(self, key):
        return self.tensor[:, self.banks[self.index[key] % len(self.banks)], :]

    def wait_free(self, engine, key):
        i = self.index[key] - len(self.banks)
        if i >= 0:
            engine.wait_ge(*self.freed[i])
        return self.at(key)


def build(nc, t, out):
    x_slots = nc.dram_tensor("x_slots", (BLOCKS * P, D), F32, kind="Internal").ap()
    y_slots = nc.dram_tensor("y_slots", (BLOCKS * P, D), F32, kind="Internal").ap()
    with ExitStack() as ctx:
        def sb(name, shape, dt=F32):
            return ctx.enter_context(nc.sbuf_tensor(name, shape, dt))

        sems = {}

        def sem(name):
            if name not in sems:
                sems[name] = ctx.enter_context(nc.semaphore(name))
            return sems[name]

        h = sb("h", [P, HALVES, TOKENS])
        xn = sb("xn", [P, HALVES, TOKENS])
        ident = sb("ident", [P, P])
        eps_ln = sb("eps_ln", [P, 1])
        eps_rms = sb("eps_rms", [P, 1])
        mean_w = sb("mean_w", [P, P])
        ones = sb("ones", [P, P])
        causal = sb("causal", [SEQ, SEQ])
        sq = sb("sq", [P, 2, HALVES, NMAX])
        std = sb("std", [P, 2, NMAX])
        rstd = sb("rstd", [P, 2, NMAX])
        wz = sb("wz", [P, HALVES, D])
        wpar = sb("wpar", [P, HALVES, DT_RANK + N_STATE])
        wdt = sb("wdt", [DT_RANK, D])
        wout0 = sb("wout0", [P, HALVES, D])
        conv0 = sb("conv0", [P, HALVES, CONV])
        dtb = sb("dtb", [P, HALVES])
        alog = sb("alog", [P, HALVES, N_STATE])
        a_neg = sb("a_neg", [P, HALVES, N_STATE])
        a_keep = sb("a_keep", [P, HALVES, N_STATE])
        a_guard = sb("a_guard", [P, HALVES, N_STATE])
        w_f = sb("w_f", [P, HALVES, N_STATE])
        guarded = sb("guarded", [P, 1])
        any_guard = sb("any_guard", [1, 1], I32)
        a_t = sb("a_t", [P, 4, D])
        skip0 = sb("skip0", [P, HALVES])
        tokb = sb("tokb", [P, HALVES])
        w_attn = sb("w_attn", [P, 6 * HALVES * D])
        part = lambda a, n, **k: w_attn[:, a:a + n].rearrange("p (k n) -> p k n", **k)
        win1 = part(0, 4 * D, k=HALVES)
        wp1 = part(4 * D, 6 * D, k=HALVES)
        wout1 = part(10 * D, 2 * D, k=HALVES)
        vec1 = sb("vec1", [P, 2 + 4 + 8 + 2 + 6 + 2 + 2])
        wq2 = sb("wq2", [P, HALVES, D])
        wk2 = sb("wk2", [P, HALVES, D])
        wv2 = sb("wv2", [P, HALVES, D])
        wo2 = sb("wo2", [P, HALVES, D])
        wg0 = sb("wg0", [P, HALVES, EXPERTS])
        wg2 = sb("wg2", [P, HALVES, EXPERTS])
        sig3 = sb("sig3", [P, HALVES, EXPERTS])
        sgn3 = sb("sgn3", [P, 2, HALVES, EXPERTS])
        bg0 = sb("bg0", [P, EXPERTS])
        bg2 = sb("bg2", [P, EXPERTS])
        first = sb("first", [P, EXPERTS])
        be2 = sb("be2", [EXPERTS, D])
        be3 = sb("be3", [EXPERTS, D])
        wq3 = part(0, 4 * D, k=HALVES * GROUP).rearrange("p (k j) n -> p k j n", k=HALVES)
        wk3 = part(4 * D, D, k=HALVES)
        wv3 = part(5 * D, D, k=HALVES)
        wo3 = part(6 * D, 4 * D, k=GROUP)
        pos = sb("pos", [P, SLOTS, TILES], I32)
        blk = sb("blk", [1, 2, BLOCKS], I32)
        ecol = sb("ecol", [P, 6, EXPERTS])
        ecol_i = sb("ecol_i", [P, EXPERTS], I32)
        gate = sb("gate", [P, 6, TILES, EXPERTS])
        gcol = sb("gcol", [P, 8, TILES])
        prow = sb("prow", [PRIMS, 2, PRIMS])
        pcol = sb("pcol", [PRIMS, 2, 8])
        ptmp = sb("ptmp", [PRIMS, 2, PRIMS])
        ptmp2 = sb("ptmp2", [PRIMS, 2, PRIMS])
        lower = sb("lower", [PRIMS, PRIMS])
        pair = sb("pair", [PRIMS, PRIM_TILES])
        sel2 = sb("sel2", [PRIMS, P])
        before = sb("before", [P, P])
        jrow = sb("jrow", [1, BLOCKS])
        bcmp = sb("bcmp", [1, BLOCKS, EXPERTS])
        bexp = sb("bexp", [1, 2, BLOCKS])
        wexp = sb("wexp", [P, 2, PRIM_TILES])
        w_late = sb("w_late", [P, EXPERTS * HALVES * D])
        w1c = w_late[:, 0:HALVES * HIDDEN].rearrange("p (k n) -> p k n", k=HALVES)
        w2c = w_late[:, HALVES * HIDDEN:].rearrange("p (k n) -> p k n", k=HT)
        w_last = w_late[:].rearrange("p (e k n) -> p e k n", e=EXPERTS, k=HALVES)
        WORK = 25100
        work = sb("work", [P, WORK])
        psum = ctx.enter_context(nc.psum_tensor("psum", [P, 8, 512], F32))

        gT = work[0:EXPERTS, WORK - TOKENS:WORK]
        cursor = [0]
        limit = [WORK]

        def carve(n):
            cursor[0] += n
            assert cursor[0] <= limit[0], cursor
            return work[:, cursor[0] - n:cursor[0]]

        def full(parts=HALVES):
            return carve(parts * TOKENS).rearrange("p (m t) -> p m t", m=parts)

        cursor[0] = 0
        xp = carve(KT_TOK * BATCH * N_IMG).rearrange("p (k n) -> p k n", k=KT_TOK)
        wtok = carve(KT_TOK * D).rearrange("p (k n) -> p k n", k=KT_TOK)
        txt = carve(HALVES * BATCH * N_TXT).rearrange("p (m b t) -> p m b t", m=HALVES, t=N_TXT)
        cursor[0] = 0
        zs = full()
        u0 = full()
        dtx = full()
        d1 = carve(HALVES * BATCH * (SEQ + 1)).rearrange("p (m b t) -> p m b t", m=HALVES, t=SEQ + 1)
        pc = carve(TOKENS)
        NS = max(CHUNK_BATCHES) * (SEQ + 1)
        d_sel = sq[:].rearrange("p r m n -> p (r m n)")[:, 0:2 * NS].rearrange("p (r n) -> p r n", r=2)
        a_buf = carve(2 * NS).rearrange("p (r n) -> p r n", r=2)
        f_buf = carve(2 * NS).rearrange("p (r n) -> p r n", r=2)
        ym = carve(2 * NMAX).rearrange("p (r n) -> p r n", r=2)
        sp_a = sq[:, 0]
        sp_r = sq[:, 1]
        xcv0 = carve(HALVES * NMAX).rearrange("p (m n) -> p m n", m=HALVES)
        ytmp = xcv0
        at0 = [0]

        def take(n):
            at0[0] += n
            assert at0[0] <= WORK
            return work[:, at0[0] - n:at0[0]]

        w13 = take(2 * 2 * HALVES * HIDDEN).rearrange("p (r w k n) -> p r w k n", r=2, w=2, k=HALVES)
        w2 = take(2 * HT * D).rearrange("p (r k n) -> p r k n", r=2, k=HT)
        xtok = take(SLOTS * TILES * D).rearrange("p (s i n) -> p s i n", s=SLOTS, i=TILES)
        xblk = take(2 * D).rearrange("p (r n) -> p r n", r=2)
        xT = take(2 * D).rearrange("p (r k n) -> p r k n", r=2, k=HALVES)
        sq_flat = sq[:].rearrange("p r m n -> p (r m n)")
        sa = sq_flat[:, 0:2 * 4 * P].rearrange("p (r n) -> p r n", r=2)
        hm = take(2 * HIDDEN).rearrange("p (r k n) -> p r k n", r=2, k=HT)
        yblk = sq_flat[:, 8 * P:8 * P + 2 * D].rearrange("p (r n) -> p r n", r=2)
        zeros = work[:, 24000:24000 + D]
        limit[0] = WORK - TOKENS
        cursor[0] = 0
        u1 = full()
        gs = full()
        xr = full()
        up = carve(2 * HALVES * NMAX).rearrange("p (r m n) -> p r m n", r=2, m=HALVES)
        xcv1 = carve(2 * HALVES * NMAX).rearrange("p (r m n) -> p r m n", r=2, m=HALVES)
        abc = carve(2 * 6 * NMAX).rearrange("p (r m n) -> p r m n", r=2, m=6)
        cursor[0] = 0
        PSLOTS = 4
        tile_long = carve(PSLOTS * HIDDEN).rearrange("p (r n) -> p r n", r=PSLOTS)
        tile_short = carve(PSLOTS * D).rearrange("p (r n) -> p r n", r=PSLOTS)
        hm1 = carve(2 * HT * NMAX).rearrange("p (r m n) -> p r m n", r=2, m=HT)
        cursor[0] = 0
        qk = full(4)
        vb = carve(BATCH * D).rearrange("p (b n) -> p b n", n=D)
        pr = carve(CHUNKS * NMAX).rearrange("p (c n) -> p c n", c=CHUNKS)
        pT = carve(2 * NMAX).rearrange("p (r n) -> p r n", r=2)
        oT = carve(2 * HALVES * NMAX).rearrange("p (r m n) -> p r m n", r=2, m=HALVES)
        st = carve(CHUNKS * 3 * 8).rearrange("p (c a n) -> p c a n", c=CHUNKS, a=3)
        cursor[0] = 0
        xs2 = carve(2 * HALVES * NMAX).rearrange("p (r m n) -> p r m n", r=2, m=HALVES)
        cursor[0] = 2 * HALVES * NMAX
        kblk = carve(BATCH * KV_HEADS * SEQ).rearrange("p (b g s) -> p b g s", g=KV_HEADS, s=SEQ)
        vb3 = carve(BATCH * P).rearrange("p (b n) -> p b n", n=P)
        q3 = carve(GROUP * 2 * NMAX).rearrange("p (r j n) -> p r j n", r=2, j=GROUP)
        p3 = carve(2 * GROUP * KV_HEADS * SEQ).rearrange("p (r j g s) -> p r j g s", r=2, j=GROUP, g=KV_HEADS)
        pT3 = carve(4 * GROUP * SEQ).rearrange("p (r n) -> p r n", r=4)
        oT3 = xs2_oT3 = work[:, 0:GROUP * NMAX].rearrange("p (j n) -> p j n", j=GROUP)
        st3 = carve(2 * 3 * GROUP * KV_HEADS).rearrange("p (r a n) -> p r a n", r=2, a=3)

        nw1, inb1, cw1, cb1, pb1, sk1, ob1 = (vec1[:, a:b] for a, b in
                                              ((0, 2), (2, 6), (6, 14), (14, 16), (16, 22), (22, 24), (24, 26)))

        def chunk(c):
            return slice(CHUNK_B0[c] * SEQ, (CHUNK_B0[c] + CHUNK_BATCHES[c]) * SEQ)

        def ntok(c):
            return CHUNK_BATCHES[c] * SEQ

        def seqs(ap):
            return ap.rearrange("p (b t) -> p b t", t=SEQ)

        def both(ap, n):
            return ap.unsqueeze(1).to_broadcast([P, HALVES, n])

        def H(block, c, m):
            return 2 * (block * CHUNKS + c) + m + 1

        h_ready = sem("h_ready")
        wait_h = lambda e, block, c: e.wait_ge(h_ready, H(block, c, 1))

        A = Banks(psum, [0, 1, 2, 3, 4, 5])
        B = Banks(psum, [6, 7])
        pe_order = []

        def step(*what):
            pe_order.append(what)

        def plan_ln(b):
            for c in range(CHUNKS):
                A.plan(("mean", b, c), (sem("centred"), b * CHUNKS + c + 1))
                step("mean", b, c)
            for c in range(CHUNKS):
                if b == L1A:
                    A.plan(("var", b, c), (sem("rms_arg"), c + 1))
                else:
                    A.plan(("var", b, c), (sem("std_done"), b * CHUNKS + c + 1))
                step("var", b, c)

        def plan_h(key, block, c):
            for m in range(HALVES):
                A.plan((key, c, m), (h_ready, H(block + 1, c, m)))
            step(key, c)

        def plan_router(r):
            A.plan(("logits", r), (sem("logits_used"), r + 1))
            step("logits", r)
            if r == 0:
                return
            for j in range(CHUNKS):
                A.plan(("gateT", r, j), (sem("gateT_kept"), (r - 1) * CHUNKS + j + 1))
            step("gateT", r)

        def plan_gb(r, q):
            A.plan(("gb", r, q), (sem("x_gated"), 40 * (r - 1) + q + 1))
            step("gb", r, q)

        for c in range(CHUNKS):
            for m in range(HALVES):
                A.plan(("tok", c, m), (h_ready, H(0, c, m)))
            step("tok", c)
        plan_ln(L0A)
        A.plan(("guards",), (sem("guards_kept"), 1))
        step("guards")
        A.plan(("prim_sum",), (sem("prim_sum_used"), 1))
        A.plan(("prim_w",), (sem("prim_w_kept"), 1))
        step("prims")
        for c in range(CHUNKS):
            for m in range(HALVES):
                A.plan(("z", c, m), (sem("z_silu"), 2 * c + m + 1))
            A.plan(("par", c), (sem("par_kept"), c + 1))
            step("z", c)
        for c in range(CHUNKS):
            for m in range(HALVES):
                A.plan(("dt", c, m), (sem("dt_relu"), 2 * c + m + 1))
            step("dt", c)
        A.plan(("cb", 0), (sem("y_part"), 2))
        step("cb", 0)
        for k in range(CHUNKS * N_STATE):
            c, n = divmod(k, N_STATE)
            if n == 0:
                for m in range(HALVES):
                    B.plan(("yacc", c, m), (sem("y_gated"), 2 * c + m + 1))
            if k + 1 < CHUNKS * N_STATE:
                A.plan(("cb", k + 1), (sem("y_part"), 2 * (k + 1) + 2))
                step("cb", k + 1)
            step("yacc", k)
            if n == N_STATE - 1:
                for m in range(HALVES):
                    A.plan(("w2c", c, m), (sem("y_gated"), 2 * c + m + 1))
                step("w2c", c)
                plan_h("out0", L0A, c)
        plan_ln(L0F)
        plan_router(0)
        NQ = EXPERTS * CHUNKS
        XT_PAIRS = (TILES + 1) // 2
        for i in range(XT_PAIRS):
            A.plan(("xtok", i), (sem("xtok_kept"), SLOTS * min(2 * i + 2, TILES)))
            step("xtok", i)
        A.plan(("rank",), (sem("rank_used"), 1))
        A.plan(("count",), (sem("count_used"), 1))
        step("rank")
        A.plan(("xT", 0), (sem("xT_kept"), 1))
        step("xT", 0)
        for j in range(BLOCKS + 1):
            if j + 1 < BLOCKS:
                A.plan(("xT", j + 1), (sem("xT_kept"), j + 2))
                step("xT", j + 1)
            if j < BLOCKS:
                for q in range(2):
                    A.plan(("e1", j, q), (sem("e1_silu"), 2 * j + q + 1))
                    A.plan(("e3", j, q), (sem("hidden"), 2 * j + q + 1))
                step("e13", j)
            if j:
                B.plan(("ey", j - 1), (sem("y_kept"), j))
                step("ey", j - 1)
        for i in range(TILES):
            A.plan(("yT", i), (sem("h_tile"), i + 1))
            step("yT", i)
        plan_ln(L1A)
        for c in range(CHUNKS):
            for j in range(4):
                A.plan(("in1", c, j), (sem("in1_u"), 2 * c + j + 1) if j < 2 else (sem("in1_gate"), 2 * c + j - 1))
            step("in1", c)
        for c in range(CHUNKS):
            for j in range(6):
                A.plan(("par1", c, j), (sem("abc_done"), 6 * c + j + 1))
            step("par1", c)
            if c:
                plan_h("out1", L1A, c - 1)
        plan_h("out1", L1A, CHUNKS - 1)
        for f in range(2):
            for j in range(4):
                A.plan(("comp", f, j), (sem("composed"), 4 * f + j + 1))
            step("comp", f)
        plan_ln(L1F)
        for c in range(CHUNKS + 1):
            if c < CHUNKS:
                for j in range(HT):
                    A.plan(("f1", c, j), (sem("f1_gelu"), HT * c + j + 1))
                step("f1", c)
            if c:
                for m in range(HALVES):
                    B.plan(("f2", c - 1, m), (h_ready, H(L2A, c - 1, m)))
                step("f2", c - 1)
        plan_ln(L2A)
        VP = [(CHUNK_BATCHES[c] + 1) // 2 for c in range(CHUNKS)]
        V0 = [sum(VP[:c]) for c in range(CHUNKS + 1)]
        for c in range(CHUNKS):
            for j in range(4):
                A.plan(("qk", c, j), (sem("qk_kept"), 4 * c + j + 1))
            for j in range(VP[c]):
                A.plan(("v2", c, j), (sem("v2_kept"), V0[c] + j + 1))
            step("qkv2", c)
            A.plan(("s2", c), (sem("s2_scaled"), c + 1))
            step("s2", c)
        for c in range(CHUNKS):
            A.plan(("pT2", c), (sem("pT2_kept"), c + 1))
            step("pT2", c)
            for m in range(HALVES):
                A.plan(("o2", c, m), (sem("o2_kept"), 2 * c + m + 1))
            step("o2", c)
            plan_h("out2", L2A, c)
        plan_ln(L2F)
        plan_router(1)

        def plan_dense(r, block):
            plan_gb(r, 0)
            for q in range(NQ):
                c, e = divmod(q, EXPERTS)
                if q + 1 < NQ:
                    plan_gb(r, q + 1)
                if e == 0:
                    for m in range(HALVES):
                        B.plan(("dy", r, c, m), (h_ready, H(block + 1, c, m)))
                step("dense", r, q)

        plan_dense(1, L2F)
        plan_ln(L3A)
        V3 = [(CHUNK_BATCHES[c] + 3) // 4 for c in range(CHUNKS)]
        V30 = [sum(V3[:c]) for c in range(CHUNKS + 1)]
        for c in range(CHUNKS):
            A.plan(("k3", c), (sem("k3_kept"), c + 1))
            for j in range(V3[c]):
                A.plan(("v3", c, j), (sem("v3_kept"), V30[c] + j + 1))
            step("kv3", c)

        def plan_s3(b):
            for j in range(GROUP):
                A.plan(("s3", b, j), (sem("s3_shifted"), GROUP * b + j + 1))
            step("s3", b)

        def plan_q3(c):
            for j in range(GROUP):
                A.plan(("q3", c, j), (sem("q3_kept"), GROUP * c + j + 1))
            step("q3", c)

        plan_q3(0)
        plan_s3(0)
        for b in range(BATCH):
            if b in CHUNK_B0 and CHUNK_B0.index(b) + 1 < CHUNKS:
                plan_q3(CHUNK_B0.index(b) + 1)
            if b + 1 < BATCH:
                plan_s3(b + 1)
            for g in range(KV_HEADS):
                A.plan(("pT3", b, g), (sem("pT3_kept"), KV_HEADS * b + g + 1))
            B.plan(("o3", b), (sem("o3_kept"), b + 1))
            step("pv3", b)
            if b + 1 == BATCH or b + 1 in CHUNK_B0:
                plan_h("out3", L3A, CHUNKS - 1 if b + 1 == BATCH else CHUNK_B0.index(b + 1) - 1)
        plan_ln(L3F)
        plan_router(2)
        plan_dense(2, L3F)

        chunk_of = [c for c in range(CHUNKS) for _ in range(CHUNK_BATCHES[c])]
        router_block = [L0F, L2F, L3F]

        block = ctx.enter_context(nc.Block())

        @block.sync
        def _(sp):
            def load(dst, name, signal):
                sp.dma_start(dst, t[name]).then_inc(sem(signal), 16)

            load(wtok, "wtok", "tok_loaded")
            load(xp, "xp", "tok_loaded")
            load(tokb[:], "tokb", "tok_loaded")
            load(txt, "txt", "txt_loaded")
            sp.wait_ge(sem("zeros_set"), 1)
            sp.dma_start(x_slots.rearrange("(j p) d -> p j d", p=P),
                         zeros.unsqueeze(1).to_broadcast([P, BLOCKS, D])).then_inc(sem("slots_cleared"), 16)
            for dst, name in ((wz, "wz"), (wpar, "wpar"), (wdt, "wdt"), (wout0, "wout0"), (conv0, "conv0"),
                              (dtb, "dtb"), (alog, "alog"), (skip0, "skip0")):
                load(dst[:], name, "l0_loaded")
            load(a_t[DT_RANK:DT_RANK + N_STATE, 0, :], "alogT", "l0_loaded")
            for dst, name in ((lower, "lower"), (pair, "pair"), (sel2, "sel2"), (before, "before"), (jrow, "jrow")):
                load(dst[:], name, "prim_loaded")
            for f, name in enumerate(("fc1_logits", "fc2_logits")):
                sp.dma_start(prow[:, f, :], t[name + "_row"].to_broadcast([PRIMS, PRIMS])).then_inc(
                    sem("prim_loaded"), 16)
                sp.dma_start(pcol[:, f, 0:1], t[name + "_col"]).then_inc(sem("prim_loaded"), 16)
            for dst, name in ((wg0, "wg0"), (wg2, "wg2"), (sig3, "sig3"), (be2, "be2"), (be3, "be3")):
                load(dst[:], name, "gate_loaded")
            for dst, name in ((bg0, "bg0"), (bg2, "bg2"), (first, "first")):
                sp.dma_start(dst[:], t[name].to_broadcast([P, EXPERTS])).then_inc(sem("gate_loaded"), 16)
            for dst, name in ((win1, "win1"), (wp1, "wp1"), (wout1, "wout1"), (vec1[:], "vec1"), (wq2[:], "wq2"),
                              (wk2[:], "wk2"), (wv2[:], "wv2"), (wo2[:], "wo2")):
                load(dst, name, "rest_loaded")
            wait_h(sp, L0F, CHUNKS - 1)
            sp.wait_ge(sem("blocks_known"), 1)

            def load_block(j):
                if j >= 2:
                    sp.wait_ge(sem("xT_done"), j - 1)
                sp.dma_start(xblk[:, j % 2], x_slots[j * P:(j + 1) * P, :]).then_inc(sem(f"rows_loaded{j % 2}"), 16)
                if j >= 2:
                    sp.wait_ge(sem("ey_done"), j - 1)
                e = sp.value_load(blk[0:1, 0, j:j + 1], min_val=0, max_val=EXPERTS - 1)
                new = sp.value_load(blk[0:1, 1, j:j + 1], min_val=0, max_val=1) > 0 if j >= 2 else None
                for dst, name in ((w13[:, j % 2, 0], "W1"), (w13[:, j % 2, 1], "W3"), (w2[:, j % 2], "W2")):
                    src = t[name][bass.DynSlice(e, 1)].rearrange("e p k n -> (e p) k n")
                    sp.dma_start(dst, src, cond=new).then_inc(sem(f"expert_loaded{j % 2}"), 16)

            def store_block(j):
                sp.wait_ge(sem("y_kept"), j + 1)
                sp.dma_start(y_slots[j * P:(j + 1) * P, :], yblk[:, j % 2]).then_inc(sem(f"y_stored{j % 2}"), 16)

            sp.wait_ge(sem("scattered"), 16 * SLOTS * TILES)
            load_block(0)
            load_block(1)
            for j in range(BLOCKS):
                if j + 2 < BLOCKS:
                    load_block(j + 2)
                store_block(j)
            wait_h(sp, L1F, CHUNKS - 1)
            for i in range(2 * PRIM_TILES):
                f, kt = divmod(i, PRIM_TILES)
                if i >= PSLOTS:
                    sp.wait_ge(sem("tile_used"), i - PSLOTS + 1)
                sp.dma_start(tile_long[:, i % PSLOTS], t[("B1", "A2")[f]][kt]).then_inc(sem(f"tile{i % PSLOTS}"), 16)
                sp.dma_start(tile_short[:, i % PSLOTS], t[("A1", "B2")[f]][kt]).then_inc(sem(f"tile{i % PSLOTS}"), 16)
            for dst, name in ((wq3, "wq3"), (wk3, "wk3"), (wv3, "wv3"), (wo3, "wo3")):
                load(dst, name, "attn3_loaded")
            wait_h(sp, L2A, CHUNKS - 1)
            load(w_last, "we2", "we2_loaded")
            wait_h(sp, L3A, CHUNKS - 1)
            load(w_last, "we3", "we3_loaded")
            for c in range(CHUNKS):
                wait_h(sp, L3F + 1, c)
                sp.dma_start(out[:, :, chunk(c)], h[:, :, chunk(c)]).then_inc(sem("stored"), 16)
            sp.wait_ge(sem("stored"), 16 * CHUNKS)

        @block.tensor
        def _(pe):
            def product(dst, lhs, rhs, parts):
                for k in range(parts):
                    mm = pe.matmul(dst, lhs(k), rhs(k), start=(k == 0), stop=(k == parts - 1))
                return mm

            def mean(b, c):
                if b == 0 and c == 0:
                    pe.wait_ge(sem("txt_placed"), 1)
                    pe.wait_ge(sem("consts"), 1)
                wait_h(pe, b, c)
                dst = A.wait_free(pe, ("mean", b, c))
                product(dst[:, 0:ntok(c)], lambda k: mean_w[:], lambda k: h[:, k, chunk(c)],
                        HALVES).then_inc(sem("mean_done"), 1)

            def var(b, c):
                i = b * CHUNKS + c
                pe.wait_ge(sem("squared"), i + 1)
                dst = A.wait_free(pe, ("var", b, c))
                product(dst[:, 0:ntok(c)], lambda k: mean_w[:], lambda k: sq[:, i % 2, k, 0:ntok(c)],
                        HALVES).then_inc(sem("var_done"), 1)

            def into_h(key, w, rhs, c, parts=HALVES, ring=A, signal="to_h"):
                for m in range(HALVES):
                    dst = ring.wait_free(pe, (key, c, m))
                    product(dst[:, 0:ntok(c)], lambda k: w[:, k, m * P:(m + 1) * P], rhs, parts).then_inc(sem(signal), 1)

            def tok(c):
                if c == 0:
                    pe.wait_ge(sem("tok_loaded"), 48)
                nb, b0 = CHUNK_BATCHES[c], CHUNK_B0[c]
                for m in range(HALVES):
                    dst = A.wait_free(pe, ("tok", c, m))
                    product(dst[:, 0:nb * N_IMG], lambda k: wtok[:, k, m * P:(m + 1) * P],
                            lambda k: xp[:, k, b0 * N_IMG:(b0 + nb) * N_IMG], KT_TOK).then_inc(sem("tok_done"), 1)

            def prims():
                pe.wait_ge(sem("prim_exp"), 1)
                dst = A.wait_free(pe, ("prim_sum",))
                pe.matmul(dst[0:PRIMS, 0:2], ones[0:PRIMS, 0:PRIMS], pcol[:, :, 3], start=True,
                          stop=True).then_inc(sem("prim_sum"), 1)
                pe.wait_ge(sem("prim_spread"), 1)
                dst = A.wait_free(pe, ("prim_w",))
                pe.matmul(dst[:, 0:2 * PRIM_TILES], sel2[:], ptmp[:, 0, :], start=True, stop=True).then_inc(sem("prim_w"), 1)

            def guards():
                pe.wait_ge(sem("guards_listed"), 1)
                dst = A.wait_free(pe, ("guards",))
                pe.matmul(dst[0:1, 0:1], ones[:, 0:1], guarded[:], start=True, stop=True).then_inc(
                    sem("guards_counted"), 1)

            def z(c):
                if c == 0:
                    pe.wait_ge(sem("l0_loaded"), 9 * 16)
                pe.wait_ge(sem("normed"), c + 1)
                for m in range(HALVES):
                    dst = A.wait_free(pe, ("z", c, m))
                    product(dst[:, 0:ntok(c)], lambda k: wz[:, k, m * P:(m + 1) * P], lambda k: xn[:, k, chunk(c)],
                            HALVES).then_inc(sem("z_done"), 1)
                dst = A.wait_free(pe, ("par", c))
                product(dst[0:DT_RANK + N_STATE, 0:ntok(c)], lambda k: wpar[:, k, :], lambda k: xn[:, k, chunk(c)],
                        HALVES).then_inc(sem("par_done"), 1)

            def dt(c):
                pe.wait_ge(sem("par_kept"), c + 1)
                for m in range(HALVES):
                    dst = A.wait_free(pe, ("dt", c, m))
                    pe.matmul(dst[:, 0:ntok(c)], wdt[:, m * P:(m + 1) * P], pc[0:DT_RANK, chunk(c)], start=True,
                              stop=True).then_inc(sem("dt_done"), 1)

            def cb(k):
                c, n = divmod(k, N_STATE)
                lo, hi = DT_RANK, DT_RANK + N_STATE
                dst = A.wait_free(pe, ("cb", k))
                pe.matmul(dst[:, 0:ntok(c)], ident[lo:hi, lo + n:lo + n + 1].to_broadcast([N_STATE, P]),
                          pc[lo:hi, chunk(c)], start=True, stop=True).then_inc(sem("c_spread"), 1)

            def yacc(k):
                c, n = divmod(k, N_STATE)
                for m in range(HALVES):
                    g = 2 * k + m
                    dst = B.wait_free(pe, ("yacc", c, m)) if n == 0 else B.at(("yacc", c, m))
                    pe.wait_ge(sem("y_part"), g + 1)
                    pe.matmul(dst[:, 0:ntok(c)], ident[:], ym[:, g % 2, 0:ntok(c)], start=(n == 0),
                              stop=(n == N_STATE - 1)).then_inc(sem("y_added"), 1)

            def w2c_(c):
                if c == 0:
                    pe.wait_ge(sem("a_ready"), 1)
                lo, hi = DT_RANK, DT_RANK + N_STATE
                for m in range(HALVES):
                    dst = A.wait_free(pe, ("w2c", c, m))
                    pe.matmul(dst[:, 0:ntok(c)], a_t[lo:hi, 3, m * P:(m + 1) * P], pc[lo:hi, chunk(c)], start=True,
                              stop=True).then_inc(sem("cw_done"), 1)

            def out0(c):
                pe.wait_ge(sem("y_gated"), 2 * c + 2)
                into_h("out0", wout0, lambda k: zs[:, k, chunk(c)], c)

            def logits(r):
                blk = router_block[r]
                if r == 0:
                    pe.wait_ge(sem("gate_loaded"), 8 * 16)
                    pe.wait_ge(sem("signs"), 1)
                pe.wait_ge(sem("normed"), (blk + 1) * CHUNKS)
                w = (wg0[:], wg2[:], sgn3[:, 0])[r]
                dst = A.wait_free(pe, ("logits", r))
                for i in range(TILES):
                    mm = product(dst[:, i * EXPERTS:(i + 1) * EXPERTS], lambda k: xn[:, k, i * P:(i + 1) * P],
                                 lambda k: w[:, k, :], HALVES)
                mm.then_inc(sem("logits_done"), 1)

            def gateT(r):
                pe.wait_ge(sem("gates"), r)
                for j in range(CHUNKS):
                    dst = A.wait_free(pe, ("gateT", r, j))
                    for i in range(4 * j, min(4 * j + 4, TILES)):
                        tr = pe.transpose(dst[0:EXPERTS, (i - 4 * j) * P:(i - 4 * j + 1) * P], gate[:, 5, i, :], ident[:])
                    tr.then_inc(sem("gateT_done"), 1)

            def gb(r, q):
                c, e = divmod(q, EXPERTS)
                if q == 0:
                    pe.wait_ge(sem("gateT_kept"), r * CHUNKS)
                dst = A.wait_free(pe, ("gb", r, q))
                pe.matmul(dst[:, 0:ntok(c)], ident[0:EXPERTS, e:e + 1].to_broadcast([EXPERTS, P]), gT[:, chunk(c)],
                          start=True, stop=True).then_inc(sem("gate_spread"), 1)

            def xtok_(i):
                dst = A.wait_free(pe, ("xtok", i))
                for k in range(2 * i, min(2 * i + 2, TILES)):
                    for m in range(HALVES):
                        tr = pe.transpose(dst[:, (k % 2) * D + m * P:(k % 2) * D + (m + 1) * P],
                                          xn[:, m, k * P:(k + 1) * P], ident[:])
                tr.then_inc(sem("xtok_done"), 1)

            def rank():
                pe.wait_ge(sem("chosen"), 1)
                pe.wait_ge(sem("prim_loaded"), 9 * 16)
                dst = A.wait_free(pe, ("rank",))
                pe.matmul(dst[:, 0:TILES * EXPERTS], before[:], gate[:, 4], start=True, stop=False)
                for i in range(TILES - 1):
                    n = TILES - 1 - i
                    pe.matmul(dst[:, (i + 1) * EXPERTS:TILES * EXPERTS].rearrange("p (i e) -> p i e", e=EXPERTS),
                              ones[:], gate[:, 4, i, :].unsqueeze(1).to_broadcast([P, n, EXPERTS]), start=False,
                              stop=(i == TILES - 2))
                dst = A.wait_free(pe, ("count",))
                for i in range(TILES):
                    mm = pe.matmul(dst[:, 0:EXPERTS], ones[:], gate[:, 4, i, :], start=(i == 0), stop=(i == TILES - 1))
                mm.then_inc(sem("ranked"), 1)

            def xT_(j):
                pe.wait_ge(sem(f"rows_loaded{j % 2}"), 16 * (j // 2 + 1))
                dst = A.wait_free(pe, ("xT", j))
                for m in range(HALVES):
                    tr = pe.transpose(dst[:, m * P:(m + 1) * P], xblk[:, j % 2, m * P:(m + 1) * P], ident[:])
                tr.then_inc(sem("xT_done"), 1)

            def e13(j):
                pe.wait_ge(sem(f"expert_loaded{j % 2}"), 48 * (j // 2 + 1))
                pe.wait_ge(sem("xT_kept"), j + 1)
                for q in range(2):
                    for w, (key, done) in enumerate((("e1", "e1_done"), ("e3", "e3_done"))):
                        dst = A.wait_free(pe, (key, j, q))
                        for i in range(4):
                            col = (4 * q + i) * P
                            mm = product(dst[:, i * P:(i + 1) * P], lambda k: w13[:, j % 2, w, k, col:col + P],
                                         lambda k: xT[:, j % 2, k, :], HALVES)
                        mm.then_inc(sem(done), 1)

            def ey(j):
                pe.wait_ge(sem("hidden"), 2 * (j + 1))
                dst = B.wait_free(pe, ("ey", j))
                product(dst[:, 0:D], lambda k: hm[:, j % 2, k, :], lambda k: w2[:, j % 2, k, :], HT).then_inc(
                    sem("ey_done"), 1)

            def yT(i):
                pe.wait_ge(sem("y_summed"), i + 1)
                dst = A.wait_free(pe, ("yT", i))
                for m in range(HALVES):
                    tr = pe.transpose(dst[:, m * P:(m + 1) * P], xtok[:, 0, i, m * P:(m + 1) * P], ident[:])
                tr.then_inc(sem("yT_done"), 1)

            def in1(c):
                if c == 0:
                    pe.wait_ge(sem("rest_loaded"), 8 * 16)
                pe.wait_ge(sem("rms_normed"), 2 * c + 2)
                for j in range(4):
                    dst = A.wait_free(pe, ("in1", c, j))
                    product(dst[:, 0:ntok(c)], lambda k: win1[:, k, j * P:(j + 1) * P],
                            lambda k: xr[:, k, chunk(c)], HALVES).then_inc(sem("in1_done"), 1)

            def par1(c):
                pe.wait_ge(sem("u1_done"), 2 * c + 2)
                for j in range(6):
                    dst = A.wait_free(pe, ("par1", c, j))
                    product(dst[:, 0:ntok(c)], lambda k: wp1[:, k, j * P:(j + 1) * P], lambda k: u1[:, k, chunk(c)],
                            HALVES).then_inc(sem("par1_done"), 1)

            def out1(c):
                pe.wait_ge(sem("y1_gated"), 2 * c + 2)
                into_h("out1", wout1, lambda k: gs[:, k, chunk(c)], c)

            def comp(f):
                banks = [A.wait_free(pe, ("comp", f, j)) for j in range(4)]
                for kt in range(PRIM_TILES):
                    i = f * PRIM_TILES + kt
                    s = i % PSLOTS
                    pe.wait_ge(sem("tile_scaled"), i + 1)
                    first_mm, last_mm = kt == 0, kt == PRIM_TILES - 1
                    if f == 0:
                        for m in range(HALVES):
                            for n in range(2):
                                mm = pe.matmul(banks[2 * m + n], tile_short[:, s, m * P:(m + 1) * P],
                                               tile_long[:, s, n * 512:(n + 1) * 512], start=first_mm, stop=last_mm)
                    else:
                        for j in range(HT):
                            mm = pe.matmul(banks[j // 2][:, (j % 2) * D:(j % 2 + 1) * D],
                                           tile_long[:, s, j * P:(j + 1) * P], tile_short[:, s, :],
                                           start=first_mm and j % 2 == 0, stop=last_mm, skip_group_check=True)
                    mm.then_inc(sem("tile_used"), 1)

            def f1(c):
                if c == 0:
                    pe.wait_ge(sem("composed"), 8)
                pe.wait_ge(sem("normed"), L1F * CHUNKS + c + 1)
                for j in range(HT):
                    dst = A.wait_free(pe, ("f1", c, j))
                    product(dst[:, 0:ntok(c)], lambda k: w1c[:, k, j * P:(j + 1) * P], lambda k: xn[:, k, chunk(c)],
                            HALVES).then_inc(sem("f1_done"), 1)

            def f2(c):
                pe.wait_ge(sem("f1_gelu"), HT * (c + 1))
                into_h("f2", w2c, lambda k: hm1[:, c % 2, k, 0:ntok(c)], c, HT, B)

            def qkv2(c):
                pe.wait_ge(sem("normed"), L2A * CHUNKS + c + 1)
                for j in range(4):
                    w = (wq2, wk2)[j // 2]
                    dst = A.wait_free(pe, ("qk", c, j))
                    product(dst[:, 0:ntok(c)], lambda k: w[:, k, (j % 2) * P:(j % 2 + 1) * P],
                            lambda k: xn[:, k, chunk(c)], HALVES).then_inc(sem("qk_done"), 1)
                for j in range(VP[c]):
                    dst = A.wait_free(pe, ("v2", c, j))
                    for i in range(2 * j, min(2 * j + 2, CHUNK_BATCHES[c])):
                        b = CHUNK_B0[c] + i
                        mm = product(dst[0:SEQ, (i % 2) * D:(i % 2 + 1) * D], lambda k: xn[:, k, b * SEQ:(b + 1) * SEQ],
                                     lambda k: wv2[:, k, :], HALVES)
                    mm.then_inc(sem("v2_done"), 1)

            def s2(c):
                pe.wait_ge(sem("qk_kept"), 4 * c + 4)
                dst = A.wait_free(pe, ("s2", c))
                for i in range(CHUNK_BATCHES[c]):
                    b = CHUNK_B0[c] + i
                    mm = product(dst[0:SEQ, i * SEQ:(i + 1) * SEQ], lambda k: qk[:, k, b * SEQ:(b + 1) * SEQ],
                                 lambda k: qk[:, 2 + k, b * SEQ:(b + 1) * SEQ], HALVES)
                mm.then_inc(sem("s2_done"), 1)

            def pT2(c):
                pe.wait_ge(sem("p2_ready"), c + 1)
                dst = A.wait_free(pe, ("pT2", c))
                for i in range(CHUNK_BATCHES[c]):
                    tr = pe.transpose(dst[0:SEQ, i * SEQ:(i + 1) * SEQ], pr[0:SEQ, c, i * SEQ:(i + 1) * SEQ],
                                      ident[0:SEQ, 0:SEQ])
                tr.then_inc(sem("pT2_done"), 1)

            def o2(c):
                pe.wait_ge(sem("pT2_kept"), c + 1)
                pe.wait_ge(sem("v2_kept"), V0[c + 1])
                for m in range(HALVES):
                    dst = A.wait_free(pe, ("o2", c, m))
                    for i in range(CHUNK_BATCHES[c]):
                        mm = pe.matmul(dst[:, i * SEQ:(i + 1) * SEQ], vb[0:SEQ, CHUNK_B0[c] + i, m * P:(m + 1) * P],
                                       pT[0:SEQ, c % 2, i * SEQ:(i + 1) * SEQ], start=True, stop=True)
                    mm.then_inc(sem("o2_done"), 1)

            def out2(c):
                pe.wait_ge(sem("o2_kept"), 2 * c + 2)
                into_h("out2", wo2, lambda k: oT[:, c % 2, k, 0:ntok(c)], c)

            def dense(r, q):
                c, e = divmod(q, EXPERTS)
                if q == 0:
                    pe.wait_ge(sem(("we2_loaded", "we3_loaded")[r - 1]), 16)
                pe.wait_ge(sem("x_gated"), 40 * (r - 1) + q + 1)
                bias = (be2, be3)[r - 1]
                for m in range(HALVES):
                    dst = B.wait_free(pe, ("dy", r, c, m)) if e == 0 else B.at(("dy", r, c, m))
                    if e == 0:
                        pe.matmul(dst[:, 0:ntok(c)], bias[:, m * P:(m + 1) * P], gT[:, chunk(c)], start=True, stop=False)
                    for k in range(HALVES):
                        mm = pe.matmul(dst[:, 0:ntok(c)], w_last[:, e, k, m * P:(m + 1) * P],
                                       xs2[:, q % 2, k, 0:ntok(c)], start=False,
                                       stop=(e == EXPERTS - 1 and k == HALVES - 1))
                    if e == EXPERTS - 1:
                        mm.then_inc(sem("dense_out"), 1)
                    elif m == HALVES - 1:
                        mm.then_inc(sem("dense_used"), 1)

            def kv3(c):
                if c == 0:
                    pe.wait_ge(sem("attn3_loaded"), 4 * 16)
                pe.wait_ge(sem("normed"), L3A * CHUNKS + c + 1)
                dst = A.wait_free(pe, ("k3", c))
                product(dst[:, 0:ntok(c)], lambda k: wk3[:, k, :], lambda k: xn[:, k, chunk(c)],
                        HALVES).then_inc(sem("k3_done"), 1)
                for j in range(V3[c]):
                    dst = A.wait_free(pe, ("v3", c, j))
                    for i in range(4 * j, min(4 * j + 4, CHUNK_BATCHES[c])):
                        b = CHUNK_B0[c] + i
                        mm = product(dst[0:SEQ, (i % 4) * P:(i % 4 + 1) * P], lambda k: xn[:, k, b * SEQ:(b + 1) * SEQ],
                                     lambda k: wv3[:, k, :], HALVES)
                    mm.then_inc(sem("v3_done"), 1)

            def q3_(c):
                for j in range(GROUP):
                    dst = A.wait_free(pe, ("q3", c, j))
                    product(dst[:, 0:ntok(c)], lambda k: wq3[:, k, j, :], lambda k: xn[:, k, chunk(c)],
                            HALVES).then_inc(sem("q3_done"), 1)

            def s3(b):
                c = chunk_of[b]
                i = b - CHUNK_B0[c]
                pe.wait_ge(sem("q3_kept"), GROUP * (c + 1))
                pe.wait_ge(sem("k3_kept"), c + 1)
                for j in range(GROUP):
                    dst = A.wait_free(pe, ("s3", b, j))
                    pe.matmul(dst[0:SEQ, 0:KV_HEADS * SEQ], q3[:, c % 2, j, i * SEQ:(i + 1) * SEQ], kblk[:, b],
                              start=True, stop=True).then_inc(sem("s3_done"), 1)

            def pv3(b):
                c = chunk_of[b]
                pe.wait_ge(sem("p3_ready"), b + 1)
                for g in range(KV_HEADS):
                    dst = A.wait_free(pe, ("pT3", b, g))
                    for j in range(GROUP):
                        tr = pe.transpose(dst[0:SEQ, j * SEQ:(j + 1) * SEQ], p3[0:SEQ, b % 2, j, g, :],
                                          ident[0:SEQ, 0:SEQ])
                    tr.then_inc(sem("pT3_done"), 1)
                pe.wait_ge(sem("v3_kept"), V30[c + 1])
                dst = B.wait_free(pe, ("o3", b))
                for g in range(KV_HEADS):
                    pe.wait_ge(sem("pT3_kept"), KV_HEADS * b + g + 1)
                    mm = pe.matmul(dst[g * HPAD:(g + 1) * HPAD, 0:GROUP * SEQ], vb3[0:SEQ, b, g * HPAD:(g + 1) * HPAD],
                                   pT3[0:SEQ, g, :], start=True, stop=True, tile_position=(0, g * HPAD))
                mm.then_inc(sem("o3_done"), 1)

            def out3(c):
                pe.wait_ge(sem("o3_kept"), CHUNK_B0[c] + CHUNK_BATCHES[c])
                into_h("out3", wo3, lambda k: oT3[:, k, 0:ntok(c)], c, GROUP)

            steps = {"mean": mean, "var": var, "tok": tok, "prims": prims, "guards": guards, "z": z, "dt": dt, "cb": cb, "yacc": yacc,
                     "w2c": w2c_, "out0": out0, "logits": logits, "gateT": gateT, "gb": gb, "xtok": xtok_, "rank": rank, "xT": xT_, "yT": yT, "e13": e13, "ey": ey,
                     "in1": in1, "par1": par1, "out1": out1, "comp": comp, "f1": f1, "f2": f2, "qkv2": qkv2,
                     "s2": s2, "pT2": pT2, "o2": o2, "out2": out2, "dense": dense, "kv3": kv3, "q3": q3_,
                     "s3": s3, "pv3": pv3, "out3": out3}
            for name, *args in pe_order:
                steps[name](*args)

        @block.scalar
        def _(act):
            count = [0]

            def link(ins):
                count[0] += 1
                ins.then_inc(sem("act_chain"), 1)
                act.wait_ge(sem("act_chain"), count[0])

            def ln(b):
                for c in range(CHUNKS):
                    i = b * CHUNKS + c
                    act.wait_ge(sem("centred"), i + 1)
                    if i >= 2:
                        act.wait_ge(sem("var_done"), i - 1)
                    act.activation(sq[:, i % 2, :, 0:ntok(c)], xn[:, :, chunk(c)], ACT.Square).then_inc(sem("squared"), 1)
                for c in range(CHUNKS):
                    i = b * CHUNKS + c
                    act.wait_ge(sem("var_done"), i + 1)
                    if i >= 2:
                        act.wait_ge(sem("inverted"), i - 1)
                    act.activation(std[:, i % 2, 0:ntok(c)], A.at(("var", b, c))[:, 0:ntok(c)], ACT.Sqrt,
                                   bias=eps_ln[:, 0:1]).then_inc(sem("std_done"), 1)
                    if b == L1A:
                        act.wait_ge(sem("rms_arg"), c + 1)
                        act.activation(std[:, i % 2, 0:ntok(c)], rstd[:, i % 2, 0:ntok(c)], ACT.Sqrt,
                                       bias=eps_rms[:, 0:1]).then_inc(sem("rms_done"), 1)

            def copy(dst, src, signal):
                act.activation(dst, src, ACT.Copy).then_inc(sem(signal), 1)

            def router_act(r):
                if r == 0:
                    act.wait_ge(sem("top_shift"), 1)
                    act.activation(gcol[:, 3], gcol[:, 2], ACT.Exp).then_inc(sem("top_exp"), 1)
                    return
                if r == 1:
                    act.wait_ge(sem("router_shift"), 1)
                    act.activation(gate[:, 0], gate[:, 0], ACT.Exp).then_inc(sem("router_exp"), 1)
                for j in range(CHUNKS):
                    n = min(4 * P, TOKENS - 4 * P * j)
                    act.wait_ge(sem("gateT_done"), (r - 1) * CHUNKS + j + 1)
                    copy(gT[:, 4 * P * j:4 * P * j + n], A.at(("gateT", r, j))[0:EXPERTS, 0:n], "gateT_kept")

            act.wait_ge(sem("l0_loaded"), 9 * 16)
            act.activation(a_neg[:], alog[:], ACT.Exp)
            act.activation(a_t[DT_RANK:DT_RANK + N_STATE, 1, :], a_t[DT_RANK:DT_RANK + N_STATE, 0, :],
                           ACT.Exp).then_inc(sem("a_exp"), 1)
            act.wait_ge(sem("prim_shift"), 1)
            act.activation(pcol[:, :, 2], pcol[:, :, 1], ACT.Exp).then_inc(sem("prim_e"), 1)
            act.wait_ge(sem("gate_loaded"), 8 * 16)
            act.wait_ge(sem("consts"), 1)
            act.activation(sgn3[:, 0], sig3[:], ACT.Sign).then_inc(sem("signs"), 1)
            ln(L0A)
            act.wait_ge(sem("prim_w"), 1)
            copy(wexp[:], A.at(("prim_w",))[:, 0:2 * PRIM_TILES].rearrange("p (f n) -> p f n", f=2), "prim_w_kept")
            for c in range(CHUNKS):
                for m in range(HALVES):
                    act.wait_ge(sem("z_done"), 2 * c + m + 1)
                    act.activation(zs[:, m, chunk(c)], A.at(("z", c, m))[:, 0:ntok(c)], ACT.Silu).then_inc(sem("z_silu"), 1)
                act.wait_ge(sem("par_done"), c + 1)
                copy(pc[0:DT_RANK + N_STATE, chunk(c)], A.at(("par", c))[0:DT_RANK + N_STATE, 0:ntok(c)], "par_kept")
                for m in range(HALVES):
                    act.wait_ge(sem("conv0"), 2 * c + m + 1)
                    act.activation(u0[:, m, chunk(c)], xcv0[:, m, 0:ntok(c)], ACT.Silu).then_inc(sem("u0_done"), 1)
            for c in range(CHUNKS):
                for m in range(HALVES):
                    g, n = 2 * c + m, ntok(c)
                    v = A.at(("dt", c, m))[:, 0:n]
                    act.wait_ge(sem("dt_done"), g + 1)
                    if g >= 2:
                        act.wait_ge(sem("dt_ready"), g - 1)
                    link(act.activation(sp_a[:, g % 2, 0:n], v, ACT.Abs, bias=dtb[:, m:m + 1]))
                    act.activation(sp_r[:, g % 2, 0:n], v, ACT.Relu, bias=dtb[:, m:m + 1]).then_inc(sem("dt_relu"), 1)
                    link(act.activation(sp_a[:, g % 2, 0:n], sp_a[:, g % 2, 0:n], ACT.Exp, scale=-1.0))
                    act.activation(sp_a[:, g % 2, 0:n], sp_a[:, g % 2, 0:n], ACT.Ln, bias=1.0).then_inc(sem("dt_ln"), 1)
            act.wait_ge(sem("a_ready"), 1)
            act.wait_ge(sem("edges"), 1)
            for k in range(CHUNKS * N_STATE):
                c, n = divmod(k, N_STATE)
                nb, b0 = CHUNK_BATCHES[c], CHUNK_B0[c]
                for m in range(HALVES):
                    g = 2 * k + m
                    if n == 0:
                        act.wait_ge(sem("dt_ready"), 2 * c + m + 1)
                    if g >= 2:
                        act.wait_ge(sem("scanned"), g - 1)
                    dst = a_buf[:, g % 2, 0:nb * (SEQ + 1)].rearrange("p (b t) -> p b t", t=SEQ + 1)[:, :, 1:SEQ + 1]
                    act.activation(dst, seqs(dtx[:, m, chunk(c)]), ACT.Exp, scale=a_neg[:, m, n:n + 1]).then_inc(
                        sem("decay"), 1)
            ln(L0F)
            router_act(0)
            act.wait_ge(sem("chosen_weights"), 1)
            for i in range(TILES):
                act.wait_ge(sem("xtok_done"), i // 2 + 1)
                for k in range(SLOTS):
                    act.activation(xtok[:, k, i], A.at(("xtok", i // 2))[:, (i % 2) * D:(i % 2 + 1) * D], ACT.Copy,
                                   scale=gcol[:, 5 + k, i:i + 1]).then_inc(sem("xtok_kept"), 1)

            def keep_xT(j):
                act.wait_ge(sem("xT_done"), j + 1)
                if j >= 2:
                    act.wait_ge(sem("e3_done"), 2 * (j - 1))
                copy(xT[:, j % 2], A.at(("xT", j))[:, 0:D].rearrange("p (k n) -> p k n", k=HALVES), "xT_kept")

            def keep_y(j):
                act.wait_ge(sem("ey_done"), j + 1)
                if j >= 2:
                    act.wait_ge(sem(f"y_stored{j % 2}"), 16 * (j // 2))
                copy(yblk[:, j % 2], B.at(("ey", j))[:, 0:D], "y_kept")

            keep_xT(0)
            for j in range(BLOCKS):
                if j + 1 < BLOCKS:
                    keep_xT(j + 1)
                for q in range(2):
                    i = 2 * j + q
                    act.wait_ge(sem("e1_done"), i + 1)
                    if i >= 2:
                        act.wait_ge(sem("hidden"), i - 1)
                    act.activation(sa[:, i % 2], A.at(("e1", j, q)), ACT.Silu).then_inc(sem("e1_silu"), 1)
                if j:
                    keep_y(j - 1)
            keep_y(BLOCKS - 1)
            ln(L1A)
            for c in range(CHUNKS):
                for j in range(4):
                    src = A.at(("in1", c, j))[:, 0:ntok(c)]
                    act.wait_ge(sem("in1_done"), 4 * c + j + 1)
                    if j < 2:
                        if c >= 2:
                            act.wait_ge(sem("conv1"), 2 * (c - 2) + j + 1)
                        act.activation(up[:, c % 2, j, 0:ntok(c)], src, ACT.Identity, bias=inb1[:, j:j + 1]).then_inc(
                            sem("in1_u"), 1)
                    else:
                        act.activation(gs[:, j - 2, chunk(c)], src, ACT.Silu, bias=inb1[:, j:j + 1]).then_inc(
                            sem("in1_gate"), 1)
                for m in range(HALVES):
                    act.wait_ge(sem("conv1"), 2 * c + m + 1)
                    act.activation(u1[:, m, chunk(c)], xcv1[:, c % 2, m, 0:ntok(c)], ACT.Silu).then_inc(sem("u1_done"), 1)
            for c in range(CHUNKS):
                for j in range(6):
                    act.wait_ge(sem("par1_done"), 6 * c + j + 1)
                    if c >= 2 and j == 0:
                        act.wait_ge(sem("y1_gated"), 2 * (c - 1))
                    act.activation(abc[:, c % 2, j, 0:ntok(c)], A.at(("par1", c, j))[:, 0:ntok(c)],
                                   ACT.Tanh if j // 2 == 1 else ACT.Sigmoid, bias=pb1[:, j:j + 1]).then_inc(
                        sem("abc_done"), 1)
            for f in range(2):
                act.wait_ge(sem("tile_used"), (f + 1) * PRIM_TILES)
                for j in range(4):
                    src = A.at(("comp", f, j))
                    if f == 0:
                        copy(w1c[:, j // 2, (j % 2) * 512:(j % 2 + 1) * 512], src, "composed")
                    else:
                        copy(w2c[:, 2 * j:2 * j + 2, :], src.rearrange("p (k n) -> p k n", k=2), "composed")
            ln(L1F)
            for c in range(CHUNKS):
                for j in range(HT):
                    act.wait_ge(sem("f1_done"), HT * c + j + 1)
                    if c >= 2 and j == 0:
                        wait_h(act, L2A, c - 2)
                    act.activation(hm1[:, c % 2, j, 0:ntok(c)], A.at(("f1", c, j))[:, 0:ntok(c)],
                                   ACT.Gelu_apprx_tanh).then_inc(sem("f1_gelu"), 1)
            ln(L2A)
            for c in range(CHUNKS):
                for j in range(4):
                    act.wait_ge(sem("qk_done"), 4 * c + j + 1)
                    copy(qk[:, j, chunk(c)], A.at(("qk", c, j))[:, 0:ntok(c)], "qk_kept")
                for j in range(VP[c]):
                    n = min(2, CHUNK_BATCHES[c] - 2 * j)
                    b = CHUNK_B0[c] + 2 * j
                    act.wait_ge(sem("v2_done"), V0[c] + j + 1)
                    copy(vb[0:SEQ, b:b + n, :], A.at(("v2", c, j))[0:SEQ, 0:n * D].rearrange("p (b n) -> p b n", n=D),
                         "v2_kept")
            for c in range(CHUNKS):
                act.wait_ge(sem("s2_shifted"), c + 1)
                act.activation(pr[0:SEQ, c, 0:ntok(c)], pr[0:SEQ, c, 0:ntok(c)], ACT.Exp).then_inc(sem("s2_exp"), 1)
            for c in range(CHUNKS):
                act.wait_ge(sem("pT2_done"), c + 1)
                if c >= 2:
                    act.wait_ge(sem("o2_done"), 2 * (c - 1))
                copy(pT[0:SEQ, c % 2, 0:ntok(c)], A.at(("pT2", c))[0:SEQ, 0:ntok(c)], "pT2_kept")
                for m in range(HALVES):
                    act.wait_ge(sem("o2_done"), 2 * c + m + 1)
                    if c >= 2:
                        wait_h(act, L2F, c - 2)
                    copy(oT[:, c % 2, m, 0:ntok(c)], A.at(("o2", c, m))[:, 0:ntok(c)], "o2_kept")
            ln(L2F)
            router_act(1)
            ln(L3A)
            act.wait_ge(sem("kblk_clear"), 1)
            for c in range(CHUNKS):
                act.wait_ge(sem("k3_done"), c + 1)
                src = A.at(("k3", c))
                for g in range(KV_HEADS):
                    rows = slice(g * HPAD, (g + 1) * HPAD)
                    ins = act.activation(kblk[rows, CHUNK_B0[c]:CHUNK_B0[c] + CHUNK_BATCHES[c], g, :],
                                         seqs(src[rows, 0:ntok(c)]), ACT.Copy)
                ins.then_inc(sem("k3_kept"), 1)
                for j in range(V3[c]):
                    n = min(4, CHUNK_BATCHES[c] - 4 * j)
                    b = CHUNK_B0[c] + 4 * j
                    act.wait_ge(sem("v3_done"), V30[c] + j + 1)
                    copy(vb3[0:SEQ, b:b + n, :], A.at(("v3", c, j))[0:SEQ, 0:n * P].rearrange("p (b n) -> p b n", n=P),
                         "v3_kept")

            def keep_q3(c):
                for j in range(GROUP):
                    act.wait_ge(sem("q3_done"), GROUP * c + j + 1)
                    if c >= 2 and j == 0:
                        act.wait_ge(sem("s3_done"), GROUP * CHUNK_B0[c - 1])
                    copy(q3[:, c % 2, j, 0:ntok(c)], A.at(("q3", c, j))[:, 0:ntok(c)], "q3_kept")

            def exp3(b):
                act.wait_ge(sem("s3_shifted"), GROUP * (b + 1))
                v = p3[0:SEQ, b % 2]
                act.activation(v, v, ACT.Exp, scale=float(HEAD) ** -0.5).then_inc(sem("s3_exp"), 1)

            keep_q3(0)
            exp3(0)
            for b in range(BATCH):
                c = chunk_of[b]
                if b == CHUNK_B0[c] and c + 1 < CHUNKS:
                    keep_q3(c + 1)
                for g in range(KV_HEADS):
                    act.wait_ge(sem("pT3_done"), KV_HEADS * b + g + 1)
                    if b:
                        act.wait_ge(sem("o3_done"), b)
                    copy(pT3[0:SEQ, g, :], A.at(("pT3", b, g))[0:SEQ, 0:GROUP * SEQ], "pT3_kept")
                if b + 1 < BATCH:
                    exp3(b + 1)
                act.wait_ge(sem("o3_done"), b + 1)
                i = b - CHUNK_B0[c]
                if i == 0 and c >= 1:
                    wait_h(act, L3F, c - 1)
                copy(oT3[:, :, i * SEQ:(i + 1) * SEQ],
                     B.at(("o3", b))[:, 0:GROUP * SEQ].rearrange("p (j t) -> p j t", j=GROUP), "o3_kept")
            ln(L3F)
            router_act(2)

        @block.vector
        def _(dve):
            count = [0]

            def link(ins):
                count[0] += 1
                ins.then_inc(sem("dve_chain"), 1)
                dve.wait_ge(sem("dve_chain"), count[0])

            def ln(b):
                for c in range(CHUNKS):
                    i = b * CHUNKS + c
                    dve.wait_ge(sem("mean_done"), i + 1)
                    dve.tensor_tensor(xn[:, :, chunk(c)], h[:, :, chunk(c)],
                                      both(A.at(("mean", b, c))[:, 0:ntok(c)], ntok(c)), ALU.subtract).then_inc(
                        sem("centred"), 1)
                for c in range(CHUNKS):
                    i, n = b * CHUNKS + c, ntok(c)
                    r = rstd[:, i % 2, 0:n]
                    dve.wait_ge(sem("std_done"), i + 1)
                    dve.reciprocal(r, std[:, i % 2, 0:n]).then_inc(sem("inverted"), 1)
                    dve.wait_ge(sem("inverted"), i + 1)
                    dve.wait_ge(sem("squared"), i + 1)
                    dve.tensor_tensor(xn[:, :, chunk(c)], xn[:, :, chunk(c)], both(r, n), ALU.mult).then_inc(
                        sem("normed"), 1)
                    if b == L1A:
                        dve.wait_ge(sem("normed"), i + 1)
                        link(dve.tensor_tensor(r, r, r, ALU.mult))
                        dve.tensor_tensor(r, r, A.at(("var", b, c))[:, 0:n], ALU.mult).then_inc(sem("rms_arg"), 1)
                        dve.wait_ge(sem("rms_done"), c + 1)
                        link(dve.reciprocal(r, std[:, i % 2, 0:n]))
                        for m in range(HALVES):
                            dve.scalar_tensor_tensor(xr[:, m, chunk(c)], xn[:, m, chunk(c)], nw1[:, m:m + 1], r,
                                                     ALU.mult, ALU.mult).then_inc(sem("rms_normed"), 1)

            to_h = [0]

            def add_h(block, key, c, ring=A, signal="to_h", bias=None):
                for m in range(HALVES):
                    to_h[0] += 1
                    dve.wait_ge(sem(signal), to_h[0])
                    dst, src = h[:, m, chunk(c)], ring.at((key, c, m))[:, 0:ntok(c)]
                    if bias is None:
                        ins = dve.tensor_tensor(dst, dst, src, ALU.add)
                    else:
                        ins = dve.scalar_tensor_tensor(dst, src, bias[:, m:m + 1], dst, ALU.add, ALU.add)
                    ins.then_inc(h_ready, 1)

            def conv(dst, src, taps, bias, signal):
                if bias is None:
                    link(dve.tensor_scalar(dst, src, taps[:, CONV - 1:CONV], None, ALU.mult))
                else:
                    link(dve.tensor_scalar(dst, src, taps[:, CONV - 1:CONV], bias, ALU.mult, ALU.add))
                d, s = seqs(dst), seqs(src)
                for k in range(1, CONV):
                    ins = dve.scalar_tensor_tensor(d[:, :, k:SEQ], s[:, :, 0:SEQ - k], taps[:, CONV - 1 - k:CONV - k],
                                                   d[:, :, k:SEQ], ALU.mult, ALU.add)
                    if k < CONV - 1:
                        link(ins)
                ins.then_inc(sem(signal), 1)

            def top1(src, dst, tmp, col):
                bc = lambda a: a.unsqueeze(2).to_broadcast([P, TILES, EXPERTS])
                link(dve.tensor_reduce(gcol[:, col], src, AX_X, ALU.max))
                link(dve.tensor_tensor(tmp, src, bc(gcol[:, col]), ALU.is_equal))
                link(dve.tensor_tensor(tmp, tmp, first[:].unsqueeze(1).to_broadcast([P, TILES, EXPERTS]), ALU.mult))
                link(dve.tensor_reduce(gcol[:, 7], tmp, AX_X, ALU.max))
                link(dve.tensor_tensor(dst, tmp, bc(gcol[:, 7]), ALU.is_equal))

            def places(oh1, oh2, tmp):
                count, blocks, last, start, base = (ecol[:, i] for i in range(5))
                dve.wait_ge(sem("ranked"), 1)
                link(dve.tensor_copy(count, A.at(("count",))[:, 0:EXPERTS]))
                link(dve.tensor_scalar(blocks, count, 1.0 / P, float(P - 1) / P - 0.5 + 1.0 / (2 * P), ALU.mult, ALU.add))
                link(dve.tensor_copy(ecol_i[:], blocks))
                link(dve.tensor_copy(blocks, ecol_i[:]))
                link(dve.tensor_scalar(blocks, blocks, 1.0, None, ALU.max))
                link(dve.tensor_tensor_scan(last, ones[:, 0:EXPERTS], blocks, 0.0, ALU.mult, ALU.add))
                link(dve.tensor_tensor(start, last, blocks, ALU.subtract))
                dve.tensor_scalar(base, start, float(P), None, ALU.mult).then_inc(sem("count_used"), 1)
                dve.wait_ge(sem("count_used"), 1)
                link(dve.tensor_tensor(gate[:, 0], A.at(("rank",))[:, 0:TILES * EXPERTS].rearrange(
                    "p (i e) -> p i e", e=EXPERTS), base.unsqueeze(1).to_broadcast([P, TILES, EXPERTS]), ALU.add))
                for k, oh in enumerate((oh1, oh2)):
                    link(dve.tensor_tensor(tmp, gate[:, 0], oh, ALU.mult))
                    link(dve.tensor_reduce(gcol[:, k], tmp, AX_X, ALU.add))
                dve.tensor_copy(pos[:], gcol[:, 0:SLOTS]).then_inc(sem("rank_used"), 1)
                link(dve.tensor_tensor(bcmp[:], last[0:1].unsqueeze(1).to_broadcast([1, BLOCKS, EXPERTS]),
                                       jrow[:].unsqueeze(2).to_broadcast([1, BLOCKS, EXPERTS]), ALU.is_le))
                link(dve.tensor_reduce(bexp[:, 0], bcmp[:], AX_X, ALU.add))
                link(dve.tensor_scalar(bexp[:, 0], bexp[:, 0], float(EXPERTS - 1), None, ALU.min))
                link(dve.tensor_tensor(bexp[:, 1, 2:BLOCKS], bexp[:, 0, 2:BLOCKS], bexp[:, 0, 0:BLOCKS - 2], ALU.not_equal))
                link(dve.memset(bexp[:, 1, 0:2], 1.0))
                dve.tensor_copy(blk[:], bexp[:]).then_inc(sem("blocks_known"), 1)

            def router(r):
                bc = lambda a: a.unsqueeze(2).to_broadcast([P, TILES, EXPERTS])
                x, tmp, oh1, oh2, rest, res = (gate[:, i] for i in range(6))
                dve.wait_ge(sem("logits_done"), r + 1)
                if r == 0:
                    dve.wait_ge(sem("gate_loaded"), 8 * 16)
                src = A.at(("logits", r))[:, 0:TILES * EXPERTS].rearrange("p (i e) -> p i e", e=EXPERTS)
                if r < 2:
                    bias = (bg0, bg2)[r][:].unsqueeze(1).to_broadcast([P, TILES, EXPERTS])
                    ins = dve.tensor_tensor(x, src, bias, ALU.add)
                else:
                    ins = dve.tensor_copy(x, src)
                ins.then_inc(sem("logits_used"), 1)
                dve.wait_ge(sem("logits_used"), r + 1)
                if r == 1:
                    link(dve.tensor_reduce(gcol[:, 2], x, AX_X, ALU.max))
                    dve.tensor_tensor(x, x, bc(gcol[:, 2]), ALU.subtract).then_inc(sem("router_shift"), 1)
                    dve.wait_ge(sem("router_exp"), 1)
                    link(dve.tensor_reduce(gcol[:, 2], x, AX_X, ALU.add))
                    link(dve.reciprocal(gcol[:, 3], gcol[:, 2]))
                    link(dve.tensor_tensor(x, x, bc(gcol[:, 3]), ALU.mult))
                if r == 2:
                    top1(x, oh1, tmp, 0)
                    dve.tensor_copy(res, oh1).then_inc(sem("gates"), 1)
                    return
                top1(x, oh1, tmp, 0)
                link(dve.tensor_scalar(rest, oh1, -3.0e38, None, ALU.mult))
                link(dve.tensor_tensor(rest, rest, x, ALU.add))
                top1(rest, oh2, tmp, 1)
                if r == 0:
                    dve.tensor_tensor(rest, oh1, oh2, ALU.add).then_inc(sem("chosen"), 1)
                    dve.tensor_tensor(gcol[:, 2], gcol[:, 1], gcol[:, 0], ALU.subtract).then_inc(sem("top_shift"), 1)
                    dve.wait_ge(sem("top_exp"), 1)
                    link(dve.tensor_scalar(gcol[:, 4], gcol[:, 3], 1.0, None, ALU.add))
                    link(dve.reciprocal(gcol[:, 5], gcol[:, 4]))
                    dve.tensor_tensor(gcol[:, 6], gcol[:, 3], gcol[:, 5], ALU.mult).then_inc(
                        sem("chosen_weights"), 1)
                    places(oh1, oh2, tmp)
                    return
                else:
                    link(dve.tensor_tensor(gcol[:, 2], gcol[:, 0], gcol[:, 1], ALU.add))
                    link(dve.reciprocal(gcol[:, 3], gcol[:, 2]))
                    link(dve.tensor_tensor(gcol[:, 5], gcol[:, 0], gcol[:, 3], ALU.mult))
                    link(dve.tensor_tensor(gcol[:, 6], gcol[:, 1], gcol[:, 3], ALU.mult))
                link(dve.tensor_tensor(oh1, oh1, bc(gcol[:, 5]), ALU.mult))
                link(dve.tensor_tensor(oh2, oh2, bc(gcol[:, 6]), ALU.mult))
                dve.tensor_tensor(res, oh1, oh2, ALU.add).then_inc(sem("gates"), 1)

            def gate_x(r, q, buf):
                c = q // EXPERTS
                dve.wait_ge(sem("gate_spread"), 40 * (r - 1) + q + 1)
                if q >= 2:
                    c2, e2 = divmod(q - 2, EXPERTS)
                    if e2 == EXPERTS - 1:
                        dve.wait_ge(sem("dense_out"), HALVES * ((r - 1) * CHUNKS + c2 + 1))
                    else:
                        dve.wait_ge(sem("dense_used"), (EXPERTS - 1) * ((r - 1) * CHUNKS + c2) + e2 + 1)
                dve.tensor_tensor(buf[:, q % 2, :, 0:ntok(c)], xn[:, :, chunk(c)],
                                  both(A.at(("gb", r, q))[:, 0:ntok(c)], ntok(c)), ALU.mult).then_inc(sem("x_gated"), 1)

            def dense(r, blk):
                gate_x(r, 0, xs2)
                for q in range(NQ):
                    if q + 1 < NQ:
                        gate_x(r, q + 1, xs2)
                    c, e = divmod(q, EXPERTS)
                    if e == EXPERTS - 1:
                        for m in range(HALVES):
                            dve.wait_ge(sem("dense_out"), HALVES * ((r - 1) * CHUNKS + c) + m + 1)
                            dve.tensor_tensor(h[:, m, chunk(c)], h[:, m, chunk(c)], B.at(("dy", r, c, m))[:, 0:ntok(c)],
                                              ALU.add).then_inc(h_ready, 1)

            dve.memset(mean_w[:], 1.0 / D)
            dve.memset(ones[:], 1.0)
            dve.memset(eps_ln[:], EPS_LN)
            dve.memset(eps_rms[:], EPS_RMS).then_inc(sem("dve_consts"), 1)
            dve.wait_ge(sem("a_exp"), 1)
            rows = slice(DT_RANK, DT_RANK + N_STATE)
            link(dve.tensor_scalar(a_guard[:], a_neg[:], 1e-5, None, ALU.is_lt))
            dve.tensor_reduce(guarded[:], a_guard[:].rearrange("p m n -> p (m n)"), AX_X, ALU.max).then_inc(
                sem("guards_listed"), 1)
            link(dve.tensor_scalar(a_keep[:], a_guard[:], -1.0, 1.0, ALU.mult, ALU.add))
            link(dve.tensor_scalar(a_neg[:], a_neg[:], -1.0, None, ALU.mult))
            link(dve.tensor_scalar(w_f[:], a_neg[:], 1e-10, None, ALU.add))
            link(dve.tensor_tensor(w_f[:], w_f[:], a_keep[:], ALU.mult))
            link(dve.tensor_tensor(w_f[:], w_f[:], a_guard[:], ALU.add))
            link(dve.reciprocal(w_f[:], w_f[:]))
            at, gt, kt = a_t[rows, 1, :], a_t[rows, 2, :], a_t[rows, 3, :]
            link(dve.tensor_scalar(gt, at, 1e-5, None, ALU.is_lt))
            link(dve.tensor_scalar(at, at, -1.0, 1e-10, ALU.mult, ALU.add))
            link(dve.tensor_scalar(kt, gt, -1.0, 1.0, ALU.mult, ALU.add))
            link(dve.tensor_tensor(at, at, kt, ALU.mult))
            link(dve.tensor_tensor(at, at, gt, ALU.add))
            link(dve.reciprocal(at, at))
            dve.tensor_tensor(kt, at, kt, ALU.mult).then_inc(sem("a_ready"), 1)
            dve.wait_ge(sem("prim_loaded"), 9 * 16)
            for f in range(2):
                lcol = pcol[:, f, 0:1]
                link(dve.tensor_scalar(ptmp[:, f], prow[:, f], lcol, None, ALU.is_equal))
                link(dve.tensor_tensor(ptmp[:, f], ptmp[:, f], lower[:], ALU.mult))
                link(dve.tensor_scalar(ptmp2[:, f], prow[:, f], lcol, None, ALU.is_gt))
                link(dve.tensor_tensor(ptmp[:, f], ptmp[:, f], ptmp2[:, f], ALU.add))
                link(dve.tensor_reduce(pcol[:, f, 4:5], ptmp[:, f], AX_X, ALU.add))
                link(dve.tensor_scalar(pcol[:, f, 5:6], pcol[:, f, 4:5], float(TOP_PRIMS), None, ALU.is_lt))
                link(dve.tensor_reduce(pcol[:, f, 6:7], prow[:, f], AX_X, ALU.max))
                link(dve.tensor_tensor(pcol[:, f, 1:2], pcol[:, f, 0:1], pcol[:, f, 6:7], ALU.subtract))
            dve.tensor_copy(pcol[:, :, 7], pcol[:, :, 1]).then_inc(sem("prim_shift"), 1)
            dve.wait_ge(sem("prim_e"), 1)
            dve.tensor_tensor(pcol[:, :, 3], pcol[:, :, 2], pcol[:, :, 5], ALU.mult).then_inc(sem("prim_exp"), 1)
            for c in range(CHUNKS):
                nb, b0 = CHUNK_BATCHES[c], CHUNK_B0[c]
                for m in range(HALVES):
                    dve.wait_ge(sem("tok_done"), 2 * c + m + 1)
                    dve.tensor_scalar(seqs(h[:, m, chunk(c)])[:, :, 0:N_IMG],
                                      A.at(("tok", c, m))[:, 0:nb * N_IMG].rearrange("p (b t) -> p b t", t=N_IMG),
                                      tokb[:, m:m + 1], None, ALU.add).then_inc(h_ready, 1)
            ln(L0A)
            dve.wait_ge(sem("guards_counted"), 1)
            dve.tensor_copy(any_guard[:], A.at(("guards",))[0:1, 0:1]).then_inc(sem("guards_kept"), 1)
            dve.wait_ge(sem("prim_sum"), 1)
            dve.reciprocal(pcol[:, :, 4], A.at(("prim_sum",))[0:PRIMS, 0:2]).then_inc(sem("prim_sum_used"), 1)
            dve.wait_ge(sem("prim_sum_used"), 1)
            link(dve.tensor_tensor(pcol[:, :, 7], pcol[:, :, 3], pcol[:, :, 4], ALU.mult))
            ptv = ptmp[:, 0, :].rearrange("p (f n) -> p f n", f=2)
            for f in range(2):
                ins = dve.tensor_scalar(ptv[:, f], pair[:], pcol[:, f, 7:8], None, ALU.mult)
            ins.then_inc(sem("prim_spread"), 1)
            for c in range(CHUNKS):
                for m in range(HALVES):
                    if c >= 1:
                        dve.wait_ge(sem("u0_done"), 2 * (c - 1) + m + 1)
                    conv(xcv0[:, m, 0:ntok(c)], xn[:, m, chunk(c)], conv0[:, m], None, "conv0")
            for c in range(CHUNKS):
                for m in range(HALVES):
                    g, n = 2 * c + m, ntok(c)
                    dve.wait_ge(sem("dt_ln"), g + 1)
                    r, l = seqs(sp_r[:, g % 2, 0:n]), seqs(sp_a[:, g % 2, 0:n])
                    d = seqs(dtx[:, m, chunk(c)])
                    dve.tensor_tensor(d[:, :, 1:SEQ], r[:, :, 0:SEQ - 1], l[:, :, 0:SEQ - 1], ALU.add)
                    dve.tensor_tensor(d[:, :, 0:1], r[:, :, 0:1], l[:, :, 0:1], ALU.add).then_inc(sem("dt_ready"), 1)

            def scan(g, general):
                k, m = divmod(g, 2)
                c, n = divmod(k, N_STATE)
                seq = slice(CHUNK_B0[c], CHUNK_B0[c] + CHUNK_BATCHES[c])
                N = CHUNK_BATCHES[c] * (SEQ + 1)
                added = d1[:, m, seq, :].rearrange("p b t -> p (b t)")
                dve.wait_ge(sem("steps_ready"), 2 * c + m + 1)
                if general:
                    sel = d_sel[:, g % 2, 0:N]
                    s3 = sel.rearrange("p (b t) -> p b t", t=SEQ + 1)
                    d, u = seqs(dtx[:, m, chunk(c)]), seqs(u0[:, m, chunk(c)])
                    guard, keep = a_guard[:, m, n:n + 1], a_keep[:, m, n:n + 1]
                    if g == 0:
                        dve.wait_ge(sem("dt_ready"), 2 * CHUNKS)
                    if g >= 2:
                        dve.wait_ge(sem("scanned"), g - 1)
                    general_link(dve.memset(sel, 0.0))
                    general_link(dve.scalar_tensor_tensor(s3[:, :, 1:2], d[:, :, 0:1], guard, u[:, :, 0:1],
                                                          ALU.mult, ALU.mult))
                    general_link(dve.scalar_tensor_tensor(s3[:, :, 2:SEQ + 1], d[:, :, 1:SEQ], guard,
                                                          u[:, :, 0:SEQ - 1], ALU.mult, ALU.mult))
                    general_link(dve.scalar_tensor_tensor(sel, added, keep, sel, ALU.mult, ALU.add))
                    added = sel
                dve.wait_ge(sem("decay"), g + 1)
                if g >= 2:
                    dve.wait_ge(sem("y_part"), g - 1)
                dve.tensor_tensor_scan(f_buf[:, g % 2, 0:N], a_buf[:, g % 2, 0:N], added, 0.0,
                                       ALU.mult, ALU.add).then_inc(sem("scanned"), 1)

            NG = 2 * CHUNKS * N_STATE

            def scans(general):
                scan(0, general)
                for g in range(NG):
                    k, m = divmod(g, 2)
                    c, n = divmod(k, N_STATE)
                    if g + 1 < NG:
                        scan(g + 1, general)
                    dve.wait_ge(sem("scanned"), g + 1)
                    dve.wait_ge(sem("c_spread"), k + 1)
                    if g >= 2:
                        dve.wait_ge(sem("y_added"), g - 1)
                    f = f_buf[:, g % 2, 0:CHUNK_BATCHES[c] * (SEQ + 1)].rearrange("p (b t) -> p b t", t=SEQ + 1)
                    dve.scalar_tensor_tensor(seqs(ym[:, g % 2, 0:ntok(c)]), f[:, :, 1:SEQ + 1], w_f[:, m, n:n + 1],
                                             seqs(A.at(("cb", k))[:, 0:ntok(c)]), ALU.mult, ALU.mult).then_inc(
                        sem("y_part"), 1)
                    if n < N_STATE - 1 or m == 0:
                        continue
                    for mm in range(HALVES):
                        N = ntok(c)
                        dve.wait_ge(sem("cw_done"), 2 * c + mm + 1)
                        dve.wait_ge(sem("y_added"), 2 * (c * N_STATE + N_STATE - 1) + mm + 1)
                        y = ytmp[:, mm, 0:N]
                        scan_link(dve.scalar_tensor_tensor(y, A.at(("w2c", c, mm))[:, 0:N], skip0[:, mm:mm + 1],
                                                           u0[:, mm, chunk(c)], ALU.subtract, ALU.mult))
                        scan_link(dve.tensor_tensor(y, B.at(("yacc", c, mm))[:, 0:N], y, ALU.subtract))
                        dve.tensor_tensor(zs[:, mm, chunk(c)], y, zs[:, mm, chunk(c)], ALU.mult).then_inc(
                            sem("y_gated"), 1)
                    add_h(L0A, "out0", c)

            steps_seen = [0, 0]

            def general_link(ins):
                steps_seen[0] += 1
                ins.then_inc(sem("general_chain"), 1)
                dve.wait_ge(sem("general_chain"), steps_seen[0])

            def scan_link(ins):
                steps_seen[1] += 1
                ins.then_inc(sem("scan_chain"), 1)
                dve.wait_ge(sem("scan_chain"), steps_seen[1])

            dve.wait_ge(sem("guards_kept"), 1)
            flag = dve.value_load(any_guard[0:1, 0:1], min_val=0, max_val=P)
            before = to_h[0]
            with dve.If(flag > 0):
                scans(True)
            to_h[0], steps_seen[1] = before, 0
            with dve.Else():
                scans(False)
            ln(L0F)
            router(0)
            for j in range(BLOCKS):
                if j >= 2:
                    dve.wait_ge(sem("ey_done"), j - 1)
                for q in range(2):
                    i = 2 * j + q
                    dve.wait_ge(sem("e1_silu"), i + 1)
                    dve.wait_ge(sem("e3_done"), i + 1)
                    dve.tensor_tensor(hm[:, j % 2, 4 * q:4 * q + 4, :].rearrange("p k n -> p (k n)"), sa[:, i % 2],
                                      A.at(("e3", j, q)), ALU.mult).then_inc(sem("hidden"), 1)

            def sum_y(i):
                dve.wait_ge(sem(f"gathered{i % 4}"), 16 * SLOTS * (i // 4 + 1))
                dve.tensor_tensor(xtok[:, 0, i], xtok[:, 0, i], xtok[:, 1, i], ALU.add).then_inc(sem("y_summed"), 1)

            dve.wait_ge(sem("h_plus_x"), CHUNKS)
            sum_y(0)
            done = 0
            for i in range(TILES):
                if i + 1 < TILES:
                    sum_y(i + 1)
                dve.wait_ge(sem("yT_done"), i + 1)
                v = h[:, :, i * P:(i + 1) * P]
                dve.tensor_tensor(v, v, A.at(("yT", i))[:, 0:D].rearrange("p (k n) -> p k n", k=HALVES),
                                  ALU.add).then_inc(sem("h_tile"), 1)
                while done < CHUNKS and (i + 1) * P >= chunk(done).stop:
                    dve.wait_ge(sem("h_tile"), i + 1)
                    for m in range(HALVES):
                        dve.memset(ecol[0:1, 5, m:m + 1], 0.0).then_inc(h_ready, 1)
                    done += 1
            ln(L1A)
            for c in range(CHUNKS):
                for m in range(HALVES):
                    dve.wait_ge(sem("in1_u"), 2 * c + m + 1)
                    if c >= 2:
                        dve.wait_ge(sem("u1_done"), 2 * (c - 2) + m + 1)
                    conv(xcv1[:, c % 2, m, 0:ntok(c)], up[:, c % 2, m, 0:ntok(c)], cw1[:, m * CONV:(m + 1) * CONV],
                         cb1[:, m:m + 1], "conv1")
            for c in range(CHUNKS):
                N = ntok(c)
                for m in range(HALVES):
                    a, b, cc = (abc[:, c % 2, 2 * i + m, 0:N] for i in range(3))
                    u, g = u1[:, m, chunk(c)], gs[:, m, chunk(c)]
                    dve.wait_ge(sem("abc_done"), 6 * c + 4 + m + 1)
                    dve.wait_ge(sem("u1_done"), 2 * c + m + 1)
                    dve.wait_ge(sem("in1_gate"), 2 * c + m + 1)
                    dve.memset(seqs(a)[:, :, 0:1], 0.0)
                    link(dve.tensor_tensor(b, b, u, ALU.mult))
                    link(dve.tensor_tensor_scan(a, a, b, 0.0, ALU.mult, ALU.add))
                    link(dve.tensor_tensor(cc, cc, a, ALU.mult))
                    link(dve.scalar_tensor_tensor(cc, u, sk1[:, m:m + 1], cc, ALU.mult, ALU.add))
                    dve.tensor_tensor(g, cc, g, ALU.mult).then_inc(sem("y1_gated"), 1)
                if c >= 1:
                    dve.wait_ge(sem("h_plus_x"), CHUNKS + c)
                    add_h(L1A, "out1", c - 1, bias=ob1)
            dve.wait_ge(sem("h_plus_x"), 2 * CHUNKS)
            add_h(L1A, "out1", CHUNKS - 1, bias=ob1)
            ln(L1F)
            for c in range(CHUNKS):
                add_h(L1F, "f2", c, B)
            ln(L2A)
            for c in range(CHUNKS):
                nb, N = CHUNK_BATCHES[c], ntok(c)
                s = seqs(pr[0:SEQ, c, 0:N])
                bc = lambda a: a.unsqueeze(2).to_broadcast([SEQ, nb, SEQ])
                mx = st[0:SEQ, c, 0, 0:nb]
                dve.wait_ge(sem("s2_done"), c + 1)
                dve.scalar_tensor_tensor(s, seqs(A.at(("s2", c))[0:SEQ, 0:N]), float(D) ** -0.5,
                                         causal[:].unsqueeze(1).to_broadcast([SEQ, nb, SEQ]), ALU.mult,
                                         ALU.add).then_inc(sem("s2_scaled"), 1)
                dve.wait_ge(sem("s2_scaled"), c + 1)
                link(dve.tensor_reduce(mx, s, AX_X, ALU.max))
                dve.tensor_tensor(s, s, bc(mx), ALU.subtract).then_inc(sem("s2_shifted"), 1)
            for c in range(CHUNKS):
                nb, N = CHUNK_BATCHES[c], ntok(c)
                s = seqs(pr[0:SEQ, c, 0:N])
                bc = lambda a: a.unsqueeze(2).to_broadcast([SEQ, nb, SEQ])
                total, inv = st[0:SEQ, c, 1, 0:nb], st[0:SEQ, c, 2, 0:nb]
                dve.wait_ge(sem("s2_exp"), c + 1)
                link(dve.tensor_reduce(total, s, AX_X, ALU.add))
                link(dve.reciprocal(inv, total))
                dve.tensor_tensor(s, s, bc(inv), ALU.mult).then_inc(sem("p2_ready"), 1)
            for c in range(CHUNKS):
                add_h(L2A, "out2", c)
            ln(L2F)
            router(1)
            dense(1, L2F)
            ln(L3A)

            def shift3(b):
                if b >= 2:
                    dve.wait_ge(sem("pT3_done"), KV_HEADS * (b - 1))
                for j in range(GROUP):
                    dve.wait_ge(sem("s3_done"), GROUP * b + j + 1)
                    s = A.at(("s3", b, j))[0:SEQ, 0:KV_HEADS * SEQ].rearrange("p (g s) -> p g s", g=KV_HEADS)
                    mx = st3[0:SEQ, b % 2, 0, j * KV_HEADS:(j + 1) * KV_HEADS]
                    link(dve.tensor_reduce(mx, s, AX_X, ALU.max))
                    dve.tensor_tensor(p3[0:SEQ, b % 2, j], s, mx.unsqueeze(2).to_broadcast([SEQ, KV_HEADS, SEQ]),
                                      ALU.subtract).then_inc(sem("s3_shifted"), 1)

            shift3(0)
            for b in range(BATCH):
                if b in CHUNK_B0 and b:
                    add_h(L3A, "out3", CHUNK_B0.index(b) - 1)
                if b + 1 < BATCH:
                    shift3(b + 1)
                dve.wait_ge(sem("s3_exp"), b + 1)
                v = p3[0:SEQ, b % 2].rearrange("p j g s -> p (j g) s")
                total, inv = st3[0:SEQ, b % 2, 1, :], st3[0:SEQ, b % 2, 2, :]
                link(dve.tensor_reduce(total, v, AX_X, ALU.add))
                if b >= 2:
                    dve.wait_ge(sem("p3_ready"), b - 1)
                dve.reciprocal(inv, total).then_inc(sem("s3_sum"), 1)
            add_h(L3A, "out3", CHUNKS - 1)
            ln(L3F)
            router(2)
            dense(2, L3F)

        @block.gpsimd
        def _(pool):
            pool.memset(zeros, 0.0).then_inc(sem("zeros_set"), 1)
            pool.memset(ident[:], 0.0).then_inc(sem("pool_zeros"), 1)
            pool.memset(causal[:], 0.0).then_inc(sem("pool_zeros"), 1)
            pool.wait_ge(sem("pool_zeros"), 2)
            pool.affine_select(out=ident[:], in_=ident[:], compare_op=ALU.not_equal, fill=1.0, base=0,
                               pattern=[[-1, P]], channel_multiplier=1)
            pool.affine_select(out=causal[:], in_=causal[:], compare_op=ALU.is_ge, fill=NEG, base=0,
                               pattern=[[-1, SEQ]], channel_multiplier=1).then_inc(sem("pool_consts"), 1)
            pool.wait_ge(sem("pool_consts"), 1)
            pool.wait_ge(sem("dve_consts"), 1)
            pool.memset(gT[:, 0:1], 0.0).then_inc(sem("consts"), 1)
            pool.wait_ge(sem("txt_loaded"), 16)
            hv = h[:].rearrange("p m (b t) -> p m b t", t=SEQ)
            for m in range(HALVES):
                ins = pool.tensor_copy(hv[:, m, :, N_IMG:SEQ], txt[:, m])
            ins.then_inc(sem("txt_placed"), 1)
            wait_h(pool, 0, CHUNKS - 1)
            pool.wait_ge(sem("txt_placed"), 1)
            for r in range(2):
                pool.memset(a_buf[:, r].rearrange("p (b t) -> p b t", t=SEQ + 1)[:, :, 0:1], 0.0)
            pool.memset(d1[:, :, :, 1:2], 0.0).then_inc(sem("edges"), 1)
            for c in range(CHUNKS):
                for m in range(HALVES):
                    d = d1[:, m, CHUNK_B0[c]:CHUNK_B0[c] + CHUNK_BATCHES[c], :]
                    u = seqs(u0[:, m, chunk(c)])
                    pool.wait_ge(sem("u0_done"), 2 * c + m + 1)
                    pool.tensor_copy(d[:, :, 0:1], u[:, :, 0:1])
                    pool.tensor_tensor(d[:, :, 2:SEQ + 1], u[:, :, 1:SEQ], u[:, :, 0:SEQ - 1], ALU.subtract).then_inc(
                        sem("steps_ready"), 1)

            def add_x(blk):
                for c in range(CHUNKS):
                    pool.wait_ge(sem("normed"), blk * CHUNKS + c + 1)
                    pool.tensor_tensor(h[:, :, chunk(c)], h[:, :, chunk(c)], xn[:, :, chunk(c)], ALU.add).then_inc(
                        sem("h_plus_x"), 1)

            add_x(L0F)
            pool.wait_ge(sem("slots_cleared"), 16)
            pool.wait_ge(sem("rank_used"), 1)
            for i in range(TILES):
                pool.wait_ge(sem("xtok_kept"), SLOTS * (i + 1))
                for k in range(SLOTS):
                    pool.indirect_dma_start(x_slots, bass.IndirectOffsetOnAxis(pos[:, k, i:i + 1], 0), xtok[:, k, i],
                                            None).then_inc(sem("scattered"), 16)
            pool.wait_ge(sem("scattered"), 16 * SLOTS * TILES)
            for r in range(2):
                pool.wait_ge(sem(f"y_stored{r}"), 16 * ((BLOCKS + 1 - r) // 2))
            for i in range(TILES):
                if i >= 4:
                    pool.wait_ge(sem(f"gathered{i % 4}"), 16 * SLOTS * (i // 4))
                for k in range(SLOTS):
                    pool.indirect_dma_start(xtok[:, k, i], None, y_slots, bass.IndirectOffsetOnAxis(
                        pos[:, k, i:i + 1], 0)).then_inc(sem(f"gathered{i % 4}"), 16)
            add_x(L1A)
            for i in range(2 * PRIM_TILES):
                f, kt = divmod(i, PRIM_TILES)
                pool.wait_ge(sem(f"tile{i % PSLOTS}"), 32 * (i // PSLOTS + 1))
                pool.wait_ge(sem("prim_w_kept"), 1)
                v = tile_short[:, i % PSLOTS]
                pool.tensor_scalar(v, v, wexp[:, f, kt:kt + 1], None, ALU.mult).then_inc(sem("tile_scaled"), 1)
            wait_h(pool, L3A, CHUNKS - 1)
            pool.memset(kblk, 0.0).then_inc(sem("kblk_clear"), 1)
            for b in range(BATCH):
                pool.wait_ge(sem("s3_sum"), b + 1)
                v = p3[0:SEQ, b % 2].rearrange("p j g s -> p (j g) s")
                pool.tensor_tensor(v, v, st3[0:SEQ, b % 2, 2, :].unsqueeze(2).to_broadcast([SEQ, GROUP * KV_HEADS, SEQ]),
                                   ALU.mult).then_inc(sem("p3_ready"), 1)


def rows(w):
    k, n = w.shape
    return w.reshape(k // P, P, n).transpose(1, 0, 2)


def halves(v):
    return v.reshape(HALVES, P, *v.shape[1:]).swapaxes(0, 1)


def pad_heads(w, heads):
    out = np.zeros((w.shape[0], heads, HPAD), w.dtype)
    out[:, :, :HEAD] = w.reshape(w.shape[0], heads, HEAD)
    return out


def layouts(i):
    patch = i["x"].reshape(BATCH, 3, 6, 16, 6, 16).transpose(1, 3, 5, 0, 2, 4).reshape(FAN_IN, BATCH * N_IMG)
    wpar = i["L0_attn_W_params"]
    wpar = np.concatenate([wpar[:DT_RANK], wpar[DT_RANK + N_STATE:]], 0).T
    q = pad_heads(i["L3_attn_Wq"].T, KV_HEADS * GROUP).reshape(D, KV_HEADS, GROUP, HPAD).transpose(0, 2, 1, 3)
    o = pad_heads(i["L3_attn_Wo"], KV_HEADS * GROUP).reshape(D, KV_HEADS, GROUP, HPAD).transpose(1, 3, 2, 0)
    vec = [halves(i["L1_attn_norm_w"]), i["L1_attn_in_b"].reshape(4, P).T,
           i["L1_attn_conv_w"].T.reshape(HALVES, P, CONV).transpose(1, 0, 2).reshape(P, -1),
           halves(i["L1_attn_conv_b"]), i["L1_attn_param_b"].reshape(6, P).T, halves(i["L1_attn_skip"]),
           halves(i["L1_attn_out_b"])]
    f32 = np.float32
    idx = np.arange(PRIMS)

    def factors(a, b):
        a = a.transpose(0, 2, 1).reshape(PRIM_TILES, P, -1)
        return a, b.reshape(PRIM_TILES, P, -1)

    a1, b1 = factors(i["L1_ffn_fc1_A"], i["L1_ffn_fc1_B"])
    a2, b2 = factors(i["L1_ffn_fc2_A"], i["L1_ffn_fc2_B"])
    return {
        "xp": rows(patch), "wtok": rows(i["L0_tok_W"].T), "tokb": halves(i["L0_tok_b"]),
        "txt": halves(i["txt"].transpose(2, 0, 1)),
        "wz": rows(i["L0_attn_W_z"].T), "wpar": rows(wpar), "wdt": i["L0_attn_W_dt"].T,
        "wout0": rows(i["L0_attn_W_out"].T), "conv0": halves(i["L0_attn_conv_w"][:, 0]),
        "dtb": halves(i["L0_attn_b_dt"]), "alog": halves(i["L0_attn_A_log"]), "alogT": i["L0_attn_A_log"].T,
        "skip0": halves(i["L0_attn_D"]),
        "lower": (idx[None, :] < idx[:, None]).astype(f32),
        "before": (np.arange(P)[:, None] < np.arange(P)[None, :]).astype(f32),
        "jrow": np.arange(BLOCKS, dtype=f32)[None],
        "pair": (idx[:, None] // 2 == np.arange(PRIM_TILES)[None, :]).astype(f32),
        "sel2": (idx[:, None] % 2 == np.arange(P)[None, :] // RANK).astype(f32),
        "fc1_logits_row": i["L1_ffn_fc1_logits"][None], "fc1_logits_col": i["L1_ffn_fc1_logits"][:, None],
        "fc2_logits_row": i["L1_ffn_fc2_logits"][None], "fc2_logits_col": i["L1_ffn_fc2_logits"][:, None],
        "wg0": rows(i["L0_ffn_Wg"]), "wg2": rows(i["L2_ffn_Wg"]), "sig3": rows(i["L3_ffn_tile_sigs"].T),
        "be2": i["L2_ffn_be"], "be3": i["L3_ffn_b"], "bg0": i["L0_ffn_bg"][None], "bg2": i["L2_ffn_bg"][None],
        "first": (EXPERTS - np.arange(EXPERTS)).astype(f32)[None],
        "win1": rows(i["L1_attn_in_w"]), "wp1": rows(i["L1_attn_param_w"]), "wout1": rows(i["L1_attn_out_w"]),
        "vec1": np.concatenate([v.reshape(P, -1) for v in vec], 1),
        "wq2": rows(i["L2_attn_Wq"]), "wk2": rows(i["L2_attn_Wk"]), "wv2": rows(i["L2_attn_Wv"]),
        "wo2": rows(i["L2_attn_Wo"]),
        "wq3": rows(q.reshape(D, -1)).reshape(P, HALVES, GROUP, P),
        "wk3": rows(pad_heads(i["L3_attn_Wk"].T, KV_HEADS).reshape(D, -1)),
        "wv3": rows(pad_heads(i["L3_attn_Wv"].T, KV_HEADS).reshape(D, -1)),
        "wo3": o.reshape(P, GROUP, D),
        "we2": i["L2_ffn_We"].transpose(2, 0, 1).reshape(HALVES, P, EXPERTS, D).transpose(1, 2, 0, 3),
        "we3": i["L3_ffn_W"].transpose(1, 0, 2).reshape(HALVES, P, EXPERTS, D).transpose(1, 2, 0, 3),
        "W1": i["L0_ffn_W1"].reshape(EXPERTS, HALVES, P, HIDDEN).transpose(0, 2, 1, 3),
        "W3": i["L0_ffn_W3"].reshape(EXPERTS, HALVES, P, HIDDEN).transpose(0, 2, 1, 3),
        "W2": i["L0_ffn_W2"].reshape(EXPERTS, HT, P, D).transpose(0, 2, 1, 3),
        "A1": a1, "B1": b1, "A2": a2, "B2": b2,
    }


def kernel(**inputs):
    import concourse.bacc as bacc
    from concourse.bass_utils import run_bass_kernel_spmd

    nc = bacc.Bacc("TRN2", target_bir_lowering=False, num_devices=1)
    arrays, t = {}, {}
    for name, a in layouts({k: np.asarray(v) for k, v in inputs.items()}).items():
        a = np.ascontiguousarray(a)
        arrays[f"in_{name}"] = a
        t[name] = nc.dram_tensor(f"in_{name}", a.shape, F32, kind="ExternalInput").ap()
    out = nc.dram_tensor("out", (P, HALVES, TOKENS), F32, kind="ExternalOutput").ap()
    build(nc, t, out)
    got = run_bass_kernel_spmd(nc, [arrays], core_ids=[0]).results[0]["out"]
    return np.ascontiguousarray(got.swapaxes(0, 1).reshape(D, BATCH, SEQ).transpose(1, 2, 0))
```
